# Optimizing a Trainium2 kernel written in Bass

```python
import numpy as np
import jax
import jax.numpy as jnp

def _softmax(x, axis=-1):
    return jax.nn.softmax(x, axis=axis)

def _gelu(x):
    return jax.nn.gelu(x, approximate=True)

def _silu(x):
    return jax.nn.silu(x)

def _sigmoid(x):
    return jax.nn.sigmoid(x)

def _layernorm(x, axis=-1, eps=1e-05):
    m = jnp.mean(x, axis=axis, keepdims=True)
    v = jnp.var(x, axis=axis, keepdims=True)
    return (x - m) / jnp.sqrt(v + eps)

def _scatter_add(tgt, idx, src, axis=0):
    return tgt.at[idx].add(src)

def _segment_sum(src, seg, n):
    return jax.ops.segment_sum(src, seg, n)
kernel_name = 'mk_sandwich_d1_jaxref_r4_f92bd9'

def setup_inputs(seed: int=0):
    np.random.seed(seed)
    _w = jnp.asarray

    def _L0_attn_setup():
        import jax, jax.numpy as jnp
        import numpy as np
        EPS = float(np.finfo(np.float32).eps)
        B, S, F_, E, H = (8, 1024, 256, 256, 16)
        HD = E // H
        LAYER = 1
        LAMBDA_INIT = 0.8 - 0.6 * float(np.exp(-0.3 * (LAYER - 1)))
        SCALE = 1.0 / float(np.sqrt(E // 2))

        def _rms(x, g):
            return x * jax.lax.rsqrt(jnp.mean(x * x, axis=-1, keepdims=True) + EPS) * g
        key = jax.random.key(seed)
        ks = jax.random.split(key, 7)
        x = jax.random.normal(ks[0], (B, S, F_), jnp.float32)
        s = 0.02
        Wq = jax.random.normal(ks[1], (E, F_), jnp.float32) * s
        Wk = jax.random.normal(ks[2], (E, F_), jnp.float32) * s
        Wv = jax.random.normal(ks[3], (E, F_), jnp.float32) * s
        W1 = jax.random.normal(ks[4], (E, E), jnp.float32) * s
        W2 = jax.random.normal(ks[5], (E, E), jnp.float32) * s
        lambda_params = jnp.full((4,), 0.8, jnp.float32)
        g1 = jnp.ones((F_,), jnp.float32)
        g2 = jnp.ones((HD,), jnp.float32)
        g3 = jnp.ones((E,), jnp.float32)
        return dict(x=x, Wq=Wq, Wk=Wk, Wv=Wv, lambda_params=lambda_params, g1=g1, g2=g2, g3=g3, W1=W1, W2=W2)
    _L0_attn_in = _L0_attn_setup()

    def _L0_ffn_setup():
        import jax, jax.numpy as jnp
        import numpy as np
        B, S, D = (2, 512, 256)
        H, HKV = (16, 4)
        HD = D // H
        F, E, K = (512, 8, 2)
        THETA = 10000.0
        EPS = 1e-05

        def _rmsnorm(x, w):
            return x * jax.lax.rsqrt(jnp.mean(x * x, axis=-1, keepdims=True) + EPS) * w

        def _rope_cos_sin(seq_len, head_dim, theta):
            inv_freq = 1.0 / theta ** (jnp.arange(0, head_dim, 2, dtype=jnp.float32) / head_dim)
            freqs = jnp.arange(seq_len, dtype=jnp.float32)[:, None] * inv_freq
            return (jnp.cos(freqs), jnp.sin(freqs))

        def _apply_rope(x, cos, sin):
            x1, x2 = jnp.split(x, 2, axis=-1)
            c = cos[None, :, None, :]
            s = sin[None, :, None, :]
            return jnp.concatenate([x1 * c - x2 * s, x2 * c + x1 * s], axis=-1)
        key = jax.random.key(seed)
        ks = jax.random.split(key, 12)
        s = 0.02
        return {'hidden_states': jax.random.normal(ks[0], (B, S, D), jnp.float32), 'ln1_w': 1.0 + 0.1 * jax.random.normal(ks[1], (D,), jnp.float32), 'ln2_w': 1.0 + 0.1 * jax.random.normal(ks[2], (D,), jnp.float32), 'Wq': s * jax.random.normal(ks[3], (D, H * HD), jnp.float32), 'Wk': s * jax.random.normal(ks[4], (D, HKV * HD), jnp.float32), 'Wv': s * jax.random.normal(ks[5], (D, HKV * HD), jnp.float32), 'Wo': s * jax.random.normal(ks[6], (H * HD, D), jnp.float32), 'Wr': s * jax.random.normal(ks[7], (D, E), jnp.float32), 'Wg': s * jax.random.normal(ks[8], (E, D, F), jnp.float32), 'Wu': s * jax.random.normal(ks[9], (E, D, F), jnp.float32), 'Wd': s * jax.random.normal(ks[10], (E, F, D), jnp.float32)}
    _L0_ffn_in = _L0_ffn_setup()
    _d = {'L0_attn_x': _L0_attn_in['x'], 'L0_attn_Wq': _L0_attn_in['Wq'], 'L0_attn_Wk': _L0_attn_in['Wk'], 'L0_attn_Wv': _L0_attn_in['Wv'], 'L0_attn_lambda_params': _L0_attn_in['lambda_params'], 'L0_attn_g1': _L0_attn_in['g1'], 'L0_attn_g2': _L0_attn_in['g2'], 'L0_attn_g3': _L0_attn_in['g3'], 'L0_attn_W1': _L0_attn_in['W1'], 'L0_attn_W2': _L0_attn_in['W2'], 'L0_ffn_ln1_w': _L0_ffn_in['ln1_w'], 'L0_ffn_ln2_w': _L0_ffn_in['ln2_w'], 'L0_ffn_Wq': _L0_ffn_in['Wq'], 'L0_ffn_Wk': _L0_ffn_in['Wk'], 'L0_ffn_Wv': _L0_ffn_in['Wv'], 'L0_ffn_Wo': _L0_ffn_in['Wo'], 'L0_ffn_Wr': _L0_ffn_in['Wr'], 'L0_ffn_Wg': _L0_ffn_in['Wg'], 'L0_ffn_Wu': _L0_ffn_in['Wu'], 'L0_ffn_Wd': _L0_ffn_in['Wd']}
    _x0 = _d['L0_attn_x']
    _d['L0_attn_x'] = jax.random.normal(jax.random.fold_in(jax.random.key(seed), 1), (8, 1024, 256), dtype=_x0.dtype)
    del _x0
    return _d

def reference(L0_attn_x, L0_attn_Wq, L0_attn_Wk, L0_attn_Wv, L0_attn_lambda_params, L0_attn_g1, L0_attn_g2, L0_attn_g3, L0_attn_W1, L0_attn_W2, L0_ffn_ln1_w, L0_ffn_ln2_w, L0_ffn_Wq, L0_ffn_Wk, L0_ffn_Wv, L0_ffn_Wo, L0_ffn_Wr, L0_ffn_Wg, L0_ffn_Wu, L0_ffn_Wd):

    def _L0_attn_ref(x, Wq, Wk, Wv, lambda_params, g1, g2, g3, W1, W2):
        import jax, jax.numpy as jnp
        import numpy as np
        EPS = float(np.finfo(np.float32).eps)
        B, S, F_, E, H = (8, 1024, 256, 256, 16)
        HD = E // H
        LAYER = 1
        LAMBDA_INIT = 0.8 - 0.6 * float(np.exp(-0.3 * (LAYER - 1)))
        SCALE = 1.0 / float(np.sqrt(E // 2))

        def _rms(x, g):
            return x * jax.lax.rsqrt(jnp.mean(x * x, axis=-1, keepdims=True) + EPS) * g
        b, s_len, _ = x.shape
        xn = _rms(x, g1)
        Q = jnp.einsum('bsf,ef->bse', xn, Wq).reshape(b, s_len, H, HD)
        K = jnp.einsum('bsf,ef->bse', xn, Wk).reshape(b, s_len, H, HD)
        V = jnp.einsum('bsf,ef->bse', xn, Wv).reshape(b, s_len, H, HD)
        pQ = jax.nn.elu(Q)
        pK = jax.nn.elu(K)
        Q1, Q2 = jnp.split(pQ, 2, axis=-1)
        K1, K2 = jnp.split(pK, 2, axis=-1)
        kv1 = jnp.einsum('bshe,bshd->bsed', K1, V) * SCALE
        kv2 = jnp.einsum('bshe,bshd->bsed', K2, V) * SCALE
        w1 = jnp.einsum('bshe,bsed->bshd', Q1, kv1)
        w2 = jnp.einsum('bshe,bsed->bshd', Q2, kv2)
        lmb = jnp.exp(lambda_params[0] * lambda_params[1]) - jnp.exp(lambda_params[2] * lambda_params[3]) + LAMBDA_INIT
        attn = w1 - lmb * w2
        attn = (1.0 - LAMBDA_INIT) * _rms(attn, g2)
        attn = attn.reshape(b, s_len, E)
        attn = _rms(attn, g3) + attn
        h = jax.nn.gelu(jnp.einsum('bse,fe->bsf', attn, W1), approximate=False)
        out = jnp.einsum('bsf,ef->bse', h, W2) + attn
        return out

    def _L0_ffn_ref(hidden_states, ln1_w, ln2_w, Wq, Wk, Wv, Wo, Wr, Wg, Wu, Wd):
        import jax, jax.numpy as jnp
        import numpy as np
        B, S, D = (2, 512, 256)
        H, HKV = (16, 4)
        HD = D // H
        F, E, K = (512, 8, 2)
        THETA = 10000.0
        EPS = 1e-05

        def _rmsnorm(x, w):
            return x * jax.lax.rsqrt(jnp.mean(x * x, axis=-1, keepdims=True) + EPS) * w

        def _rope_cos_sin(seq_len, head_dim, theta):
            inv_freq = 1.0 / theta ** (jnp.arange(0, head_dim, 2, dtype=jnp.float32) / head_dim)
            freqs = jnp.arange(seq_len, dtype=jnp.float32)[:, None] * inv_freq
            return (jnp.cos(freqs), jnp.sin(freqs))

        def _apply_rope(x, cos, sin):
            x1, x2 = jnp.split(x, 2, axis=-1)
            c = cos[None, :, None, :]
            s = sin[None, :, None, :]
            return jnp.concatenate([x1 * c - x2 * s, x2 * c + x1 * s], axis=-1)
        b, s, d = hidden_states.shape
        residual = hidden_states
        h = _rmsnorm(hidden_states, ln1_w)
        q = (h @ Wq).reshape(b, s, H, HD)
        k = (h @ Wk).reshape(b, s, HKV, HD)
        v = (h @ Wv).reshape(b, s, HKV, HD)
        cos, sin = _rope_cos_sin(s, HD, THETA)
        q = _apply_rope(q, cos, sin)
        k = _apply_rope(k, cos, sin)
        rep = H // HKV
        k = jnp.repeat(k, rep, axis=2)
        v = jnp.repeat(v, rep, axis=2)
        scores = jnp.einsum('bqhd,bkhd->bhqk', q, k) / np.sqrt(HD).astype(np.float32)
        causal = jnp.tril(jnp.ones((s, s), dtype=bool))
        scores = jnp.where(causal[None, None], scores, jnp.finfo(scores.dtype).min)
        attn = jax.nn.softmax(scores, axis=-1)
        ctx = jnp.einsum('bhqk,bkhd->bqhd', attn, v).reshape(b, s, H * HD)
        attn_out = ctx @ Wo
        h = jnp.clip(residual + attn_out, -100.0, 100.0)
        residual = h
        hn = _rmsnorm(h, ln2_w)
        flat = hn.reshape(b * s, d)
        logits = flat @ Wr
        probs = jax.nn.softmax(logits, axis=-1)
        topv, topi = jax.lax.top_k(probs, K)
        topv = topv / jnp.sum(topv, axis=-1, keepdims=True)
        w = jnp.sum(jax.nn.one_hot(topi, E, dtype=flat.dtype) * topv[..., None], axis=1)
        g = jnp.einsum('td,edf->etf', flat, Wg)
        u = jnp.einsum('td,edf->etf', flat, Wu)
        a = jax.nn.silu(g) * u
        o = jnp.einsum('etf,efd->etd', a, Wd)
        moe_out = jnp.einsum('te,etd->td', w, o).reshape(b, s, d)
        out = jnp.clip(residual + moe_out, -100.0, 100.0)
        return out
    x = L0_attn_x
    x = x + _layernorm(_L0_attn_ref(_layernorm(x, axis=-1), L0_attn_Wq, L0_attn_Wk, L0_attn_Wv, L0_attn_lambda_params, L0_attn_g1, L0_attn_g2, L0_attn_g3, L0_attn_W1, L0_attn_W2), axis=-1)
    x = x + _layernorm(_L0_ffn_ref(_layernorm(x, axis=-1), L0_ffn_ln1_w, L0_ffn_ln2_w, L0_ffn_Wq, L0_ffn_Wk, L0_ffn_Wv, L0_ffn_Wo, L0_ffn_Wr, L0_ffn_Wg, L0_ffn_Wu, L0_ffn_Wd), axis=-1)
    return x

_drawn_inputs = setup_inputs


def setup_inputs(seed=0):
    import zlib

    import numpy as np

    out = dict(_drawn_inputs(seed))
    spreads = {'L0_attn_lambda_params': (0.800000011920929, 0.2),
     'L0_attn_g1': (1.0, 0.2),
     'L0_attn_g2': (1.0, 0.2),
     'L0_attn_g3': (1.0, 0.2)}
    factors = {'L0_ffn_ln1_w': 8.0,
     'L0_ffn_ln2_w': 8.0,
     'L0_ffn_Wq': 8.0,
     'L0_ffn_Wk': 8.0,
     'L0_ffn_Wv': 8.0,
     'L0_ffn_Wo': 8.0,
     'L0_ffn_Wr': 8.0,
     'L0_ffn_Wg': 8.0,
     'L0_ffn_Wu': 8.0,
     'L0_ffn_Wd': 7.996}
    for name, (base, spread) in spreads.items():
        noise = np.random.default_rng([zlib.crc32(name.encode()), seed]).standard_normal(out[name].shape)
        drawn = base * np.exp(spread * noise) if base else spread * noise
        out[name] = jnp.asarray(drawn.astype(out[name].dtype))
    for name, factor in factors.items():
        out[name] = (out[name] * factor).astype(out[name].dtype)
    return out
```

```python
from contextlib import ExitStack

import numpy as np

import concourse.bass as bass
from concourse import mybir

F32 = mybir.dt.float32
BF16 = mybir.dt.bfloat16
U32 = mybir.dt.uint32
ALU = mybir.AluOpType
ACT = mybir.ActivationFunctionType
AX = mybir.AxisListType

P = 128
B, S, D = 8, 1024, 256
NT = S // P
FC = D // P
H, HD = 16, 16
HKV = 4
G = H // HKV
KV = HKV * HD
NQKV = D + 2 * KV
E, F = 8, 512
FK = F // P
CH = 4
LN_EPS = 1e-5
EPS1 = float(np.finfo(np.float32).eps)
LAMBDA_INIT = 0.8 - 0.6 * float(np.exp(-0.3 * 0))
SCALE1 = 1.0 / float(np.sqrt(D // 2))
SCALE2 = 0.25
THETA = 10000.0
MASKED = -1e30
Q_PART = [0, 0, 0, 1, 1, 2]
K_PART = [0, 1, 2, 0, 1, 0]
NSLOT = len(Q_PART)
MROW = NSLOT * HD
KROWS = MROW + 3


class Signal:

    def __init__(self, sem):
        self.sem = sem
        self.n = 0

    def by(self, instruction, k=1):
        instruction.then_inc(self.sem, k)
        self.n += k

    def settle(self, eng):
        eng.wait_ge(self.sem, self.n)


class Signals:
    def __init__(self, nc, ctx, names, prefix):
        self.all = []
        self.table = {}
        for name in names.split():
            s = Signal(ctx.enter_context(nc.semaphore(prefix + name)))
            self.table[name] = s
            self.all.append(s)

    def __getitem__(self, name):
        return self.table[name]


def attention_kernel(nc, a, dram):
    ctx = ExitStack()
    with ctx:
        def sb(name, shape, dt=F32):
            return ctx.enter_context(nc.sbuf_tensor(name, shape, dt))

        def ps(name, shape, dt=F32):
            return ctx.enter_context(nc.psum_tensor(name, shape, dt))

        w_raw = sb("w_raw", [P, 5, FC, D])
        wqkvT = sb("wqkvT", [P, FC, 3 * D])
        w1T = sb("w1T", [P, FC, D])
        w2T = sb("w2T", [P, FC, D])
        wqkv2 = sb("wqkv2", [P, FC, NQKV])
        wo = sb("wo", [P, FC, D])
        wr = sb("wr", [P, FC, E])
        g1c = sb("g1c", [P, FC])
        ln1c = sb("ln1c", [P, FC])
        g2row = sb("g2row", [P, D])
        g3row = sb("g3row", [P, D])
        ln2row = sb("ln2row", [P, D])
        lam = sb("lam", [P, 8])
        crow = sb("crow", [P, D])
        rope = sb("rope", [P, NT, 2 * HD])
        ident = sb("ident", [P, P])
        identb = sb("identb", [P, P], BF16)
        mask_qk = sb("mask_qk", [P, P], BF16)
        mask_kq = sb("mask_kq", [P, P], BF16)
        nhalf = sb("nhalf", [P, P])
        iota_e = sb("iota_e", [P, NT, E])
        X = sb("X", [P, NT, D])
        AT = sb("AT", [P, NT, D])
        A2 = sb("A2", [P, NT, D])
        O1 = sb("O1", [P, NT, D])
        HS = sb("HS", [P, NT, D])
        XN = sb("XN", [P, 2, D])
        XT = sb("XT", [P, 2, FC, P])
        EX = sb("EX", [P, 2, 2 * D])
        QK = sb("QK", [P, 2, 2 * D])
        VS = sb("VS", [P, 2, D])
        KP = sb("KP", [P, 2, D])
        KVS = sb("KVS", [P, D])
        SQ = sb("SQ", [P, 2, D])
        work = sb("work", [P, 3 * H * D])
        P1 = [work[:, i * H * D:(i + 1) * H * D] for i in range(2)]
        P2 = work[:, 2 * H * D:3 * H * D]
        workb = work[:, :].bitcast(BF16)
        QST = workb[:, 0:H * S].rearrange("p (h s) -> p h s", h=H)
        QTS = workb[:, H * S:H * S + 3 * FC * S].rearrange("p (j c s) -> p j c s", j=3, c=FC)
        KST = sb("KST", [P, HKV, S], BF16)
        KTS = sb("KTS", [KV, 3, S], BF16)
        A2T = sb("A2T", [P, FC, CH * P])
        HT = sb("HT", [P, 2, FC, CH * P])
        Q2 = sb("Q2", [P, 2, D + KV])
        RA = sb("RA", [P, D + KV])
        RB = sb("RB", [P, D + KV])
        PT = sb("PT", [P, 2, 3, D + KV], BF16)
        V1 = sb("V1", [P, NT, HKV, 32])
        PR = sb("PR", [P, 8, 512])
        OT = sb("OT", [P, 512])
        RC = sb("RC", [P, 4, G])
        NM = sb("NM", [P, NT, G])
        NMR = sb("NMR", [P, NT, G])
        MT = sb("MT", [P, NT, 3, G], BF16)
        MR = sb("MR", [3 * G, S], BF16)
        CTX = O1
        H2 = A2
        FL = AT
        bst = sb("bst", [P, NT, 6])
        mv = sb("mv", [P, NT, 2])
        st = sb("st", [P, 12, NT])
        MS = sb("MS", [P, NT, H])
        R16 = sb("R16", [P, NT, H])
        LG = sb("LG", [P, NT, E])
        top = sb("top", [P, NT, 8])
        topi = sb("topi", [P, NT, 8], U32)
        topf = sb("topf", [P, NT, 2])
        tw = sb("tw", [P, 4, NT])
        W8 = sb("W8", [P, 2, NT, E])

        MX = ps("MX", [P, 2, 2, 512])
        SP_ = ps("SP_", [P, 2, 512])
        OA = ps("OA", [P, 512])
        OB = ps("OB", [P, 512])

        names = ("x_loaded stats coef xn tp xT qkv expo vcopy e1 qk kprime prod1 kv prod2 attn sq ms r16 an ssq a2 "
                 "tpb a2T hid hidT out1 o1 y1 x1 stats2 coef2 hs tph hT qkv2 q2 v2 rope ropes part0 part1 part2 partd tpq qts kts "
                 "bounced bouncek qst kst mx nm mt mrow s exp pv o ot otp rc ctx "
                 "tpc cT wo h2 ss2 coef3 fl tpf fT lg lgs topk stored pool_step dve_step act_step phase")
        sg = Signals(nc, ctx, names, "s_")
        setup = Signals(nc, ctx, "wload tpw wT pool dve act lam done", "i_")
        arrive = ctx.enter_context(nc.semaphore("batch_arrive"))
        go = {n: ctx.enter_context(nc.semaphore("batch_go_" + n)) for n in ("act", "dve", "pe", "pool")}

        xb = a["L0_attn_x"].rearrange("b (t p) f -> b p t f", p=P)
        qd, kd = dram["qd"], dram["kd"]
        x1d, h2d, fld, w8d = (dram[n].rearrange("(b t p) f -> b p t f", b=B, p=P) for n in ("x1", "h2", "flat", "w8"))
        NWLOAD = 5 + 3 + 1 + 1 + 2 + 3 + 1 + 1
        phases = 5

        STEPS = 3 * CH
        PPS = -(-G * NT // STEPS)

        def OAB(t):
            return (OA, OB)[t % 2][:, :]

        def steps():
            for g in range(HKV):
                for c in range(S // 512):
                    for kt in range(CH * (c + 1)):
                        yield g, c, kt

        def pv_steps(g, c):
            return STEPS * g + (CH if c == 0 else STEPS)

        def dve_plan():
            pieces = [(h, qt) for h in range(G) for qt in range(NT)]
            for p in pieces:
                yield 0, "max", p
            yield 0, "parts", None
            yield 0, "rows", None
            for g in range(HKV):
                for s in range(STEPS):
                    if g + 1 < HKV:
                        for p in pieces[PPS * s:PPS * (s + 1)]:
                            yield g + 1, "max", p
                        if s == STEPS - 1:
                            yield g + 1, "parts", None
                            yield g + 1, "rows", None
                    if s == 0 and g >= 1:
                        yield g - 1, "out", 1
                    if s == 1 and g >= 1:
                        yield g - 1, "ctx", 1
                    if s == CH:
                        yield g, "out", 0
                    if s == CH + 1:
                        yield g, "ctx", 0
            yield HKV - 1, "out", 1
            yield HKV - 1, "ctx", 1

        block = ctx.enter_context(nc.Block())

        def end_phase(eng, k):
            eng.sem_inc(sg["phase"].sem, 1)
            eng.wait_ge(sg["phase"].sem, 4 * k)

        def end_batch(eng, own):
            eng.sem_inc(arrive, 1)
            eng.wait_ge(go[own], 1)
            eng.sem_clear(go[own])

        @block.sync
        def _(sp):
            w = setup["wload"]
            for i, n in enumerate(("Wq", "Wk", "Wv", "W1", "W2")):
                w.by(sp.dma_start(w_raw[:, i], a["L0_attn_" + n].rearrange("(c p) n -> p c n", p=P)), 16)
            for i, (n, c0, c1) in enumerate((("Wq", 0, D), ("Wk", D, D + KV), ("Wv", D + KV, NQKV))):
                w.by(sp.dma_start(wqkv2[:, :, c0:c1], a["L0_ffn_" + n].rearrange("(c p) n -> p c n", p=P)), 16)
            w.by(sp.dma_start(wo[:, :, :], a["L0_ffn_Wo"].rearrange("(c p) n -> p c n", p=P)), 16)
            w.by(sp.dma_start(wr[:, :, :], a["L0_ffn_Wr"].rearrange("(c p) n -> p c n", p=P)), 16)
            w.by(sp.dma_start(g1c[:, :], a["L0_attn_g1"].rearrange("(c p) -> p c", p=P), allow_slow_non_contiguous=True), 16)
            w.by(sp.dma_start(ln1c[:, :], a["L0_ffn_ln1_w"].rearrange("(c p) -> p c", p=P), allow_slow_non_contiguous=True), 16)
            w.by(sp.dma_start(g2row[:, 0:HD], a["L0_attn_g2"].partition_broadcast(P)), 16)
            w.by(sp.dma_start(g3row[:, :], a["L0_attn_g3"].partition_broadcast(P)), 16)
            w.by(sp.dma_start(ln2row[:, :], a["L0_ffn_ln2_w"].partition_broadcast(P)), 16)
            w.by(sp.dma_start(lam[:, 0:4], a["L0_attn_lambda_params"].partition_broadcast(P)), 16)
            w.by(sp.dma_start(rope[:, :, :], a["rope"].rearrange("(t p) n -> p t n", p=P)), 16)
            assert w.n == 16 * NWLOAD

            with sp.Fori(0, B) as b:
                sg["x_loaded"].by(sp.dma_start(X[:, :, :], xb[bass.ds(b, 1)].squeeze(0)), 16)
                sp.wait_ge(sg["kts"].sem, NT)
                sg["bouncek"].by(sp.dma_start(kd.rearrange("j r s -> r j s"), KTS[:, :, :]), 16)
                sp.wait_ge(sg["qts"].sem, NT)
                sg["bounced"].by(sp.dma_start(qd.rearrange("j (c r) s -> r j c s", c=FC), QTS), 16)
                sp.wait_ge(sg["bouncek"].sem, 16)
                for i in range(NSLOT):
                    sg["kst"].by(sp.dma_start(KST[HD * i:HD * (i + 1), :, :],
                                              kd[K_PART[i]].rearrange("(h e) s -> e h s", e=HD)), 16)
                sp.wait_ge(sg["bounced"].sem, 16)
                for i in range(NSLOT):
                    sg["qst"].by(sp.dma_start(QST[HD * i:HD * (i + 1), :, :],
                                              qd[Q_PART[i]].rearrange("(h e) s -> e h s", e=HD)), 16)
                for g in range(HKV):
                    sp.wait_ge(sg["mt"].sem, g + 1)
                    for j in range(3):
                        sg["mrow"].by(sp.dma_start(QST[MROW + j:MROW + j + 1, G * g:G * (g + 1), :],
                                                   MR[G * j:G * (j + 1), :]), 16)
                st_ = sg["stored"]
                sp.wait_ge(sg["x1"].sem, NT)
                st_.by(sp.dma_start(x1d[bass.ds(b, 1)].squeeze(0), X[:, :, :]), 16)
                sp.wait_ge(sg["h2"].sem, NT)
                st_.by(sp.dma_start(h2d[bass.ds(b, 1)].squeeze(0), H2[:, :, :]), 16)
                sp.wait_ge(sg["fl"].sem, NT)
                st_.by(sp.dma_start(fld[bass.ds(b, 1)].squeeze(0), FL[:, :, :]), 16)
                sp.wait_ge(sg["topk"].sem, 1)
                st_.by(sp.dma_start(w8d[bass.ds(b, 1)].squeeze(0), W8[:, 0]), 16)
                st_.settle(sp)
                sp.wait_ge(arrive, len(go))
                for s in (arrive, *(x.sem for x in sg.all)):
                    sp.sem_clear(s)
                for s in go.values():
                    sp.sem_inc(s, 1)

        @block.gpsimd
        def _(pool):
            ps_ = setup["pool"]
            ps_.by(pool.memset(ident[:, :], 0.0))
            ps_.by(pool.memset(identb[:, :], 0.0))
            ps_.by(pool.memset(mask_qk[:, :], 0.0))
            ps_.by(pool.memset(mask_kq[:, :], 0.0))
            ps_.by(pool.memset(nhalf[:, :], -0.5))
            ps_.by(pool.memset(V1[:, :, :, HD:32], 0.0))
            ps_.settle(pool)
            ps_.by(pool.memset(KST[MROW:P, :, :], 1.0))
            ps_.settle(pool)
            ps_.by(pool.iota(iota_e[:, :, :], [[0, NT], [1, E]], base=0, channel_multiplier=0,
                             allow_small_or_imprecise_dtypes=True))
            ps_.settle(pool)
            for m in (ident, identb):
                ps_.by(pool.affine_select(out=m[:, :], in_=m[:, :], compare_op=ALU.not_equal, fill=1.0, base=0,
                                          pattern=[[-1, P]], channel_multiplier=1))
            ps_.by(pool.affine_select(out=mask_qk[:, :], in_=mask_qk[:, :], compare_op=ALU.is_ge, fill=MASKED,
                                      base=0, pattern=[[-1, P]], channel_multiplier=1))
            ps_.by(pool.affine_select(out=mask_kq[:, :], in_=mask_kq[:, :], compare_op=ALU.is_ge, fill=MASKED,
                                      base=0, pattern=[[1, P]], channel_multiplier=-1))
            ps_.by(pool.memset(V1[:, :, :, HD:HD + 1], 1.0))
            ps_.settle(pool)
            pool.wait_ge(setup["done"].sem, 1)

            ps1 = sg["pool_step"]

            def rsqrt(dst, src, scale, eps):
                ps1.by(pool.tensor_scalar(dst, src, scale, eps, ALU.mult, ALU.add))
                ps1.settle(pool)
                ps1.by(pool.tensor_tensor(dst, dst, nhalf[:, 0:dst.shape[-1]], ALU.pow))
                ps1.settle(pool)

            def mul(dst, x, y):
                ps1.by(pool.tensor_tensor(dst, x, y, ALU.mult))
                ps1.settle(pool)

            def norm_coefficients(eps2, done, with_second):
                rsqrt(st[:, 0, :], mv[:, :, 1], 1.0, LN_EPS)
                mul(st[:, 1, :], mv[:, :, 1], st[:, 0, :])
                mul(st[:, 1, :], st[:, 1, :], st[:, 0, :])
                rsqrt(st[:, 2, :], st[:, 1, :], 1.0, eps2)
                if with_second:
                    mul(st[:, 3, :], st[:, 0, :], st[:, 2, :])
                else:
                    ps1.by(pool.tensor_copy(st[:, 3, :], st[:, 0, :]))
                    ps1.settle(pool)
                mul(st[:, 4, :], mv[:, :, 0], st[:, 3, :])
                done.by(pool.tensor_scalar(st[:, 4, :], st[:, 4, :], -1.0, 0.0, ALU.mult, ALU.add))

            with pool.Fori(0, B) as b:
                pool.wait_ge(sg["stats"].sem, 2 * NT)
                norm_coefficients(EPS1, sg["coef"], True)
                for t in range(NT):
                    pool.wait_ge(sg["qk"].sem, t + 1)
                    sg["kprime"].by(pool.tensor_tensor(KP[:, t % 2], QK[:, t % 2, D:2 * D], crow[:, :], ALU.mult))
                    sg["kprime"].settle(pool)
                    pool.wait_ge(sg["vcopy"].sem, t + 1)
                    if t >= 2:
                        pool.wait_ge(sg["kv"].sem, t - 1)
                    sg["prod1"].by(pool.tensor_tensor(
                        P1[t % 2].rearrange("p (e d h) -> p e d h", e=HD, d=HD),
                        KP[:, t % 2].rearrange("p (h e) -> p e h", e=HD).unsqueeze(2).broadcast_to([P, HD, HD, H]),
                        VS[:, t % 2].rearrange("p (h d) -> p d h", d=HD).unsqueeze(1).broadcast_to([P, HD, HD, H]),
                        ALU.mult))
                pool.wait_ge(sg["ms"].sem, NT)
                R = R16[:, :, :].rearrange("p t h -> p (t h)")
                rsqrt(R, MS[:, :, :].rearrange("p t h -> p (t h)"), 1.0 / HD, EPS1)
                pool.sem_inc(sg["r16"].sem, 1)
                pool.wait_ge(sg["ssq"].sem, NT)
                rsqrt(st[:, 6, :], st[:, 5, :], 1.0 / D, EPS1)
                pool.sem_inc(sg["r16"].sem, 1)
                sg["prod1"].settle(pool)
                end_phase(pool, 1)
                pool.wait_ge(sg["stats2"].sem, 2 * NT)
                norm_coefficients(1.0, sg["coef2"], False)
                for t in range(NT):
                    pool.wait_ge(sg["y1"].sem, t + 1)
                    sg["x1"].by(pool.tensor_tensor(X[:, t], X[:, t], O1[:, t], ALU.add))
                sg["x1"].settle(pool)
                end_phase(pool, 2)
                pool.wait_ge(sg["stats2"].sem, 4 * NT)
                norm_coefficients(LN_EPS, sg["coef2"], False)
                for t in range(NT):
                    pool.wait_ge(sg["q2"].sem, t + 1)
                    q = Q2[:, t % 2].rearrange("p (h a e) -> p h a e", a=2, e=HD // 2)
                    ra = RA[:, :].rearrange("p (h a e) -> p h a e", a=2, e=HD // 2)
                    rb = RB[:, :].rearrange("p (h a e) -> p h a e", a=2, e=HD // 2)
                    nh = (D + KV) // HD
                    sh = [P, nh, HD // 2]

                    def table(c0):
                        return rope[:, t, c0:c0 + HD // 2].unsqueeze(1).broadcast_to(sh)
                    if t >= 1:
                        pool.wait_ge(sg["part1"].sem, 2 * t)
                    for half in range(2):
                        ps1.by(pool.tensor_tensor(ra[:, :, half], q[:, :, half], table(0), ALU.mult))
                        ps1.by(pool.tensor_tensor(rb[:, :, half], q[:, :, 1 - half], table(HD + 8 * half), ALU.mult))
                    ps1.settle(pool)
                    sg["rope"].by(pool.tensor_tensor(RA[:, :], RA[:, :], RB[:, :], ALU.add))
                    sg["rope"].settle(pool)
                end_phase(pool, 3)
                end_phase(pool, 4)
                pool.wait_ge(sg["ss2"].sem, NT)
                rsqrt(st[:, 8, :], st[:, 7, :], 1.0 / D, LN_EPS)
                pool.sem_inc(sg["coef3"].sem, 1)
                end_batch(pool, "pool")

        @block.scalar
        def _(act):
            act.wait_ge(setup["wload"].sem, 16 * NWLOAD)
            act.wait_ge(setup["dve"].sem, 2)
            setup["act"].by(act.activation(lam[:, 6:8], lam[:, 4:6], ACT.Exp))

            with act.Fori(0, B) as b:
                act.wait_ge(sg["coef"].sem, 1)
                for t in range(NT + 1):
                    if t < NT:
                        if t >= 2:
                            act.wait_ge(sg["tp"].sem, t - 1)
                        sg["xn"].by(act.activation(XN[:, t % 2], X[:, t], ACT.Identity, bias=st[:, 4, t:t + 1],
                                                   scale=st[:, 3, t:t + 1]))
                    if t >= 1:
                        u = t - 1
                        act.wait_ge(sg["qkv"].sem, u + 1)
                        if u >= 2:
                            act.wait_ge(sg["qk"].sem, u - 1)
                            act.wait_ge(sg["prod1"].sem, u - 1)
                        sg["expo"].by(act.activation(EX[:, u % 2], MX[:, u % 2, 0, :], ACT.Exp))
                        sg["vcopy"].by(act.activation(VS[:, u % 2], MX[:, u % 2, 1, 0:D], ACT.Copy))
                    if t >= 2:
                        u = t - 2
                        act.wait_ge(sg["attn"].sem, u + 1)
                        if u >= 2:
                            act.wait_ge(sg["ms"].sem, u - 1)
                        sg["sq"].by(act.activation(SQ[:, u % 2], AT[:, u], ACT.Square))
                u = NT - 1
                act.wait_ge(sg["attn"].sem, u + 1)
                act.wait_ge(sg["ms"].sem, u - 1)
                sg["sq"].by(act.activation(SQ[:, u % 2], AT[:, u], ACT.Square))
                act.wait_ge(sg["ms"].sem, NT)
                act.wait_ge(sg["an"].sem, 2)
                for t in range(NT):
                    if t >= 2:
                        act.wait_ge(sg["ssq"].sem, t - 1)
                    sg["ssq"].by(act.activation(SQ[:, t % 2], AT[:, t], ACT.Square, accum_out=st[:, 5, t:t + 1]))
                sg["ssq"].settle(act)
                end_phase(act, 1)
                for c in range(NT // CH):
                    for t in range(CH * c, CH * (c + 1)):
                        act.wait_ge(sg["tpb"].sem, t + 1)
                        if t == CH * c and c >= 1:
                            act.wait_ge(sg["hid"].sem, c)
                        sg["a2T"].by(act.activation(A2T[:, :, (t % CH) * P:(t % CH + 1) * P],
                                                    SP_[:, t % 2, 0:D].rearrange("p (c s) -> p c s", c=FC), ACT.Copy))
                    act.wait_ge(sg["hid"].sem, c + 1)
                    for fo in range(FC):
                        sg["hidT"].by(act.activation(HT[:, c, fo, :], MX[:, 0, fo, :], ACT.Gelu))
                act.wait_ge(sg["coef2"].sem, 1)
                for t in range(NT):
                    sg["y1"].by(act.activation(O1[:, t], O1[:, t], ACT.Identity, bias=st[:, 4, t:t + 1],
                                               scale=st[:, 3, t:t + 1]))
                sg["y1"].settle(act)
                end_phase(act, 2)
                act.wait_ge(sg["coef2"].sem, 2)
                for t in range(NT):
                    sg["hs"].by(act.activation(HS[:, t], X[:, t], ACT.Identity, bias=st[:, 4, t:t + 1],
                                               scale=st[:, 3, t:t + 1]))
                for t in range(NT):
                    act.wait_ge(sg["tph"].sem, t + 1)
                    if t >= 2:
                        act.wait_ge(sg["qkv2"].sem, t - 1)
                    sg["hT"].by(act.activation(XT[:, t % 2].rearrange("p c s -> p (c s)"), SP_[:, t % 2, 0:D], ACT.Copy))
                    act.wait_ge(sg["qkv2"].sem, t + 1)
                    if t >= 2:
                        act.wait_ge(sg["part2"].sem, t - 1)
                    sg["q2"].by(act.activation(Q2[:, t % 2], MX[:, 0, t % 2, 0:D + KV], ACT.Copy,
                                               scale=st[:, 2, t:t + 1]))
                    sg["v2"].by(act.activation(V1[:, t, :, 0:HD],
                                               MX[:, 0, t % 2, D + KV:NQKV].rearrange("p (g e) -> p g e", g=HKV),
                                               ACT.Copy, scale=st[:, 2, t:t + 1]))
                    if t >= 1:
                        u = t - 1
                        act.wait_ge(sg["tpq"].sem, 2 * u + 2)
                        sg["qts"].by(act.activation(
                            QTS[:, :, :, u * P:(u + 1) * P],
                            MX[:, 1, u % 2, :].bitcast(BF16)[:, 0:3 * FC * P].rearrange("p (j c s) -> p j c s", j=3, c=FC),
                            ACT.Copy))
                u = NT - 1
                act.wait_ge(sg["tpq"].sem, 2 * u + 2)
                sg["qts"].by(act.activation(
                    QTS[:, :, :, u * P:(u + 1) * P],
                    MX[:, 1, u % 2, :].bitcast(BF16)[:, 0:3 * FC * P].rearrange("p (j c s) -> p j c s", j=3, c=FC),
                    ACT.Copy))
                sg["qts"].settle(act)
                sg["v2"].settle(act)
                end_phase(act, 3)
                n = 0
                for g, c, kt in steps():
                    q0 = max(0, kt - CH * c) * P
                    for h in range(G):
                        act.wait_ge(sg["s"].sem, n + 1)
                        if n >= 8:
                            act.wait_ge(sg["pv"].sem, (n - 8) // G + 1)
                        sg["exp"].by(act.activation(PR[:, n % 8, q0:512], SP_[:, n % 2, q0:512], ACT.Exp))
                        n += 1
                sg["exp"].settle(act)
                end_phase(act, 4)
                for t in range(NT):
                    act.wait_ge(sg["tpc"].sem, t + 1)
                    if t >= 2:
                        act.wait_ge(sg["wo"].sem, t - 1)
                    sg["cT"].by(act.activation(XT[:, t % 2].rearrange("p c s -> p (c s)"), SP_[:, t % 2, 0:D], ACT.Copy))
                    if t >= 1:
                        u = t - 1
                        act.wait_ge(sg["h2"].sem, u + 1)
                        if u >= 2:
                            act.wait_ge(sg["ss2"].sem, u - 1)
                        sg["ss2"].by(act.activation(SQ[:, u % 2], H2[:, u], ACT.Square, accum_out=st[:, 7, u:u + 1]))
                u = NT - 1
                act.wait_ge(sg["h2"].sem, u + 1)
                act.wait_ge(sg["ss2"].sem, u - 1)
                sg["ss2"].by(act.activation(SQ[:, u % 2], H2[:, u], ACT.Square, accum_out=st[:, 7, u:u + 1]))
                for t in range(NT):
                    act.wait_ge(sg["tpf"].sem, t + 1)
                    if t >= 2:
                        act.wait_ge(sg["lg"].sem, t - 1)
                    sg["fT"].by(act.activation(XN[:, t % 2], SP_[:, t % 2, 0:D], ACT.Copy))
                act.wait_ge(sg["lgs"].sem, 1)
                sg["act_step"].by(act.activation(tw[:, 1, :], tw[:, 0, :], ACT.Exp))
                sg["act_step"].settle(act)
                end_batch(act, "act")

        @block.vector
        def _(dve):
            dve.wait_ge(setup["wload"].sem, 16 * NWLOAD)
            sd = setup["dve"]
            sd.by(dve.tensor_tensor(lam[:, 4:5], lam[:, 0:1], lam[:, 1:2], ALU.mult))
            sd.by(dve.tensor_tensor(lam[:, 5:6], lam[:, 2:3], lam[:, 3:4], ALU.mult))
            for n in (HD, 2 * HD, 4 * HD, 8 * HD):
                sd.settle(dve)
                sd.by(dve.tensor_copy(g2row[:, n:2 * n], g2row[:, 0:n]))
            sd.settle(dve)
            sd.by(dve.tensor_scalar(g2row[:, :], g2row[:, :], 1.0 - LAMBDA_INIT, None, ALU.mult))
            dve.wait_ge(setup["act"].sem, 1)
            sd.by(dve.memset(crow[:, :], SCALE1))
            sd.settle(dve)
            c3 = crow[:, :].rearrange("p (h e) -> p h e", e=HD)[:, :, HD // 2:HD]
            sd.by(dve.tensor_tensor(lam[:, 0:1], lam[:, 6:7], lam[:, 7:8], ALU.subtract))
            sd.settle(dve)
            sd.by(dve.tensor_scalar(lam[:, 0:1], lam[:, 0:1], LAMBDA_INIT, -1.0, ALU.add, ALU.mult))
            sd.settle(dve)
            assert sd.n == 10 - 0, sd.n
            sd.by(dve.tensor_scalar(c3, c3, lam[:, 0:1], None, ALU.mult))
            for c in range(FC):
                sd.by(dve.tensor_scalar(wqkv2[:, c, 0:D], wqkv2[:, c, 0:D], ln1c[:, c:c + 1], SCALE2, ALU.mult, ALU.mult))
                sd.by(dve.tensor_scalar(wqkv2[:, c, D:NQKV], wqkv2[:, c, D:NQKV], ln1c[:, c:c + 1], None, ALU.mult))
            for i in range(5):
                dve.wait_ge(setup["tpw"].sem, i + 1)
                src = SP_[:, i % 2, :].rearrange("p (c n) -> p c n", c=FC)
                if i < 3:
                    for c in range(FC):
                        setup["wT"].by(dve.tensor_scalar(wqkvT[:, c, i * D:(i + 1) * D], src[:, c], g1c[:, c:c + 1],
                                                         None, ALU.mult))
                else:
                    dst = (w1T, w2T)[i - 3]
                    for c in range(FC):
                        setup["wT"].by(dve.tensor_copy(dst[:, c], src[:, c]))
            setup["wT"].settle(dve)
            sd.settle(dve)
            dve.sem_inc(setup["done"].sem, 1)
            dve.wait_ge(setup["pool"].sem, 13)

            ds = sg["dve_step"]

            def stats(t, src, done):
                done.by(dve.bn_stats(bst[:, t], src))

            def aggregate(done):
                done.settle(dve)
                for t in range(NT):
                    done.by(dve.bn_aggr(mv[:, t], bst[:, t]))

            with dve.Fori(0, B) as b:
                dve.wait_ge(sg["x_loaded"].sem, 16)
                for t in range(NT):
                    stats(t, X[:, t], sg["stats"])
                aggregate(sg["stats"])
                for t in range(NT + 1):
                    if t < NT:
                        dve.wait_ge(sg["tp"].sem, t + 1)
                        if t >= 2:
                            dve.wait_ge(sg["qkv"].sem, t - 1)
                        sg["xT"].by(dve.tensor_copy(XT[:, t % 2].rearrange("p c s -> p (c s)"), SP_[:, t % 2, 0:D]))
                    if t >= 1:
                        u = t - 1
                        dve.wait_ge(sg["expo"].sem, u + 1)
                        sg["e1"].by(dve.tensor_scalar(EX[:, u % 2], EX[:, u % 2], 1.0, -1.0, ALU.min, ALU.add))
                        sg["e1"].settle(dve)
                        if u >= 2:
                            dve.wait_ge(sg["kprime"].sem, u - 1)
                        sg["qk"].by(dve.scalar_tensor_tensor(out=QK[:, u % 2], in0=MX[:, u % 2, 0, :], scalar=0.0,
                                                             in1=EX[:, u % 2], op0=ALU.max, op1=ALU.add))
                        sg["qk"].settle(dve)
                        dve.wait_ge(sg["prod1"].sem, u + 1)
                        sg["kv"].by(dve.tensor_reduce(KVS[:, :], P1[u % 2].rearrange("p (x h) -> p x h", h=H), AX.X, ALU.add))
                        sg["kv"].settle(dve)
                        sg["prod2"].by(dve.tensor_tensor(
                            P2.rearrange("p (h d e) -> p h d e", d=HD, e=HD),
                            QK[:, u % 2, 0:D].rearrange("p (h e) -> p h e", e=HD).unsqueeze(2).broadcast_to([P, H, HD, HD]),
                            KVS[:, :].rearrange("p (e d) -> p d e", d=HD).unsqueeze(1).broadcast_to([P, H, HD, HD]),
                            ALU.mult))
                        sg["prod2"].settle(dve)
                        sg["attn"].by(dve.tensor_reduce(AT[:, u], P2.rearrange("p (x e) -> p x e", e=HD), AX.X, ALU.add))
                    if t >= 2:
                        u = t - 2
                        dve.wait_ge(sg["sq"].sem, u + 1)
                        sg["ms"].by(dve.tensor_reduce(MS[:, u], SQ[:, u % 2].rearrange("p (h d) -> p h d", d=HD), AX.X, ALU.add))
                u = NT - 1
                dve.wait_ge(sg["sq"].sem, u + 1)
                sg["ms"].by(dve.tensor_reduce(MS[:, u], SQ[:, u % 2].rearrange("p (h d) -> p h d", d=HD), AX.X, ALU.add))
                dve.wait_ge(sg["r16"].sem, 1)
                at4 = AT[:, :, :].rearrange("p t (h d) -> p (t h) d", d=HD)
                sg["attn"].settle(dve)
                sg["an"].by(dve.tensor_tensor(at4, at4, R16[:, :, :].rearrange("p t h -> p (t h)").unsqueeze(2)
                                              .broadcast_to([P, NT * H, HD]), ALU.mult))
                sg["an"].settle(dve)
                sg["an"].by(dve.tensor_tensor(AT[:, :, :], AT[:, :, :], g2row[:, :].unsqueeze(1).broadcast_to([P, NT, D]),
                                              ALU.mult))
                sg["an"].settle(dve)
                dve.wait_ge(sg["r16"].sem, 2)
                for t in range(NT):
                    ds.by(dve.tensor_scalar(A2[:, t], g3row[:, :], st[:, 6, t:t + 1], 1.0, ALU.mult, ALU.add))
                ds.settle(dve)
                for t in range(NT):
                    sg["a2"].by(dve.tensor_tensor(A2[:, t], A2[:, t], AT[:, t], ALU.mult))
                sg["a2"].settle(dve)
                end_phase(dve, 1)
                for t in range(NT):
                    dve.wait_ge(sg["out1"].sem, t + 1)
                    sg["o1"].by(dve.tensor_tensor(O1[:, t], OAB(t)[:, 0:D], A2[:, t], ALU.add))
                    sg["o1"].settle(dve)
                    stats(t, O1[:, t], sg["stats2"])
                aggregate(sg["stats2"])
                sg["stats2"].settle(dve)
                end_phase(dve, 2)
                for t in range(NT):
                    stats(t, X[:, t], sg["stats2"])
                aggregate(sg["stats2"])
                for t in range(NT):
                    dve.wait_ge(sg["rope"].sem, t + 1)
                    if t >= 2:
                        dve.wait_ge(sg["tpq"].sem, 2 * (t - 1))
                    pt = PT[:, t % 2]
                    ds.by(dve.tensor_copy(pt[:, 0], RA[:, :]))
                    ds.settle(dve)
                    sg["part1"].by(dve.tensor_tensor(Q2[:, t % 2], RA[:, :], pt[:, 0], ALU.subtract))
                    sg["part1"].settle(dve)
                    sg["part1"].by(dve.tensor_copy(pt[:, 1], Q2[:, t % 2]))
                    sg["part1"].settle(dve)
                    sg["part2"].by(dve.tensor_tensor(pt[:, 2], Q2[:, t % 2], pt[:, 1], ALU.subtract))
                    if t >= 1:
                        u = t - 1
                        dve.wait_ge(sg["tpq"].sem, 2 * u + 2)
                        sg["kts"].by(dve.tensor_copy(
                            KTS[:, :, u * P:(u + 1) * P],
                            OAB(u).bitcast(BF16)[0:KV, 0:3 * P].rearrange("p (j s) -> p j s", j=3)))
                u = NT - 1
                dve.wait_ge(sg["tpq"].sem, 2 * u + 2)
                sg["kts"].by(dve.tensor_copy(
                    KTS[:, :, u * P:(u + 1) * P],
                    OAB(u).bitcast(BF16)[0:KV, 0:3 * P].rearrange("p (j s) -> p j s", j=3)))
                sg["kts"].settle(dve)
                end_phase(dve, 3)
                piece = 0
                for g, kind, arg in dve_plan():
                    if kind == "max":
                        h, qt = arg
                        dve.wait_ge(sg["nm"].sem, piece + 1)
                        n = (qt + 1) * P
                        src = MX[:, piece % 2].rearrange("p a n -> p (a n)")[:, 0:n]
                        sg["mx"].by(dve.tensor_reduce(NM[:, qt, h:h + 1], src, AX.X, ALU.max, negate=True))
                        piece += 1
                    elif kind == "parts":
                        sg["mx"].settle(dve)
                        mt = MT[:, :, :, :]
                        ds.by(dve.tensor_copy(mt[:, :, 0], NM[:, :, :]))
                        ds.settle(dve)
                        ds.by(dve.tensor_tensor(NMR[:, :, :], NM[:, :, :], mt[:, :, 0], ALU.subtract))
                        ds.settle(dve)
                        ds.by(dve.tensor_copy(mt[:, :, 1], NMR[:, :, :]))
                        ds.settle(dve)
                        sg["part0"].by(dve.tensor_tensor(mt[:, :, 2], NMR[:, :, :], mt[:, :, 1], ALU.subtract))
                    elif kind == "rows":
                        dve.wait_ge(sg["nm"].sem, piece + 1)
                        if g >= 1:
                            dve.wait_ge(sg["mrow"].sem, 48 * g)
                        src = MX[0:3 * G, piece % 2, 0, :].bitcast(BF16)
                        dve_mt = dve.tensor_copy(MR[:, :], src)
                        sg["mt"].by(dve_mt)
                        sg["mt"].settle(dve)
                        dve.sem_inc(sg["mx"].sem, 1)
                        sg["mx"].n += 1
                        piece += 1
                    elif kind == "out":
                        c = arg
                        k = (g * 2 + c)
                        dve.wait_ge(sg["pv"].sem, pv_steps(g, c))
                        if k >= 1:
                            dve.wait_ge(sg["otp"].sem, k)
                        sg["ot"].by(dve.tensor_copy(OT[:, :], OA[:, :]))
                    else:
                        c = arg
                        k = (g * 2 + c)
                        dve.wait_ge(sg["otp"].sem, k + 1)
                        o = OB[:, :].rearrange("p (q h d) -> p q h d", q=CH, h=G)
                        ds.by(dve.reciprocal(RC[:, :, :], o[:, :, :, HD]))
                        ds.settle(dve)
                        sg["ctx"].by(dve.tensor_tensor(
                            CTX[:, CH * c:CH * (c + 1), g * G * HD:(g + 1) * G * HD].rearrange("p q (h d) -> p q h d", d=HD),
                            o[:, :, :, 0:HD], RC[:, :, :].unsqueeze(3).broadcast_to([P, CH, G, HD]), ALU.mult))
                        sg["ctx"].settle(dve)
                end_phase(dve, 4)
                for t in range(NT):
                    dve.wait_ge(sg["wo"].sem, t + 1)
                    ds.by(dve.tensor_tensor(H2[:, t], OAB(t)[:, 0:D], HS[:, t], ALU.add))
                    ds.settle(dve)
                    sg["h2"].by(dve.tensor_scalar(H2[:, t], H2[:, t], 100.0, -100.0, ALU.min, ALU.max))
                sg["h2"].settle(dve)
                dve.wait_ge(sg["coef3"].sem, 1)
                for t in range(NT):
                    sg["fl"].by(dve.scalar_tensor_tensor(out=FL[:, t], in0=H2[:, t], scalar=st[:, 8, t:t + 1],
                                                         in1=ln2row[:, :], op0=ALU.mult, op1=ALU.mult))
                dve.wait_ge(sg["lg"].sem, NT)
                ds.by(dve.tensor_copy(LG[:, :, :], MX[:, 0, 0, 0:NT * E].rearrange("p (t e) -> p t e", e=E)))
                ds.settle(dve)
                for t in range(NT):
                    ds.by(dve.max(top[:, t], LG[:, t]))
                ds.settle(dve)
                for t in range(NT):
                    ds.by(dve.max_index(topi[:, t], top[:, t], LG[:, t]))
                sg["lgs"].by(dve.tensor_tensor(tw[:, 0, :], top[:, :, 1], top[:, :, 0], ALU.subtract))
                ds.settle(dve)
                ds.by(dve.tensor_copy(topf[:, :, :], topi[:, :, 0:2]))
                dve.wait_ge(sg["act_step"].sem, 1)
                ds.by(dve.tensor_scalar(tw[:, 2, :], tw[:, 1, :], 1.0, None, ALU.add))
                ds.settle(dve)
                ds.by(dve.reciprocal(tw[:, 2, :], tw[:, 2, :]))
                ds.settle(dve)
                ds.by(dve.tensor_tensor(tw[:, 3, :], tw[:, 1, :], tw[:, 2, :], ALU.mult))
                ds.settle(dve)
                for j in range(2):
                    ds.by(dve.tensor_tensor(W8[:, j], iota_e[:, :, :], topf[:, :, j].unsqueeze(2).broadcast_to([P, NT, E]),
                                            ALU.is_equal))
                    ds.settle(dve)
                    ds.by(dve.tensor_tensor(W8[:, j], W8[:, j], tw[:, 2 + j].unsqueeze(2).broadcast_to([P, NT, E]), ALU.mult))
                    ds.settle(dve)
                sg["topk"].by(dve.tensor_tensor(W8[:, 0], W8[:, 0], W8[:, 1], ALU.add))
                sg["topk"].settle(dve)
                end_batch(dve, "dve")

        @block.tensor
        def _(pe):
            pe.wait_ge(setup["pool"].sem, 13)
            pe.wait_ge(setup["wload"].sem, 16 * NWLOAD)
            for i in range(5):
                if i >= 2:
                    pe.wait_ge(setup["wT"].sem, 2 * (i - 1))
                for fc in range(FC):
                    for ec in range(FC):
                        m = pe.transpose(SP_[:, i % 2, fc * D + ec * P:fc * D + (ec + 1) * P],
                                         w_raw[:, i, ec, fc * P:(fc + 1) * P], ident[:, :])
                setup["tpw"].by(m)
            pe.wait_ge(setup["done"].sem, 1)

            def transpose_tile(dst, src):
                for c in range(FC):
                    m = pe.transpose(dst[:, c * P:(c + 1) * P], src[:, c * P:(c + 1) * P], ident[:, :])
                return m

            with pe.Fori(0, B) as b:
                for t in range(NT + 1):
                    if t < NT:
                        pe.wait_ge(sg["xn"].sem, t + 1)
                        if t >= 2:
                            pe.wait_ge(sg["xT"].sem, t - 1)
                        sg["tp"].by(transpose_tile(SP_[:, t % 2], XN[:, t % 2]))
                    if t >= 1:
                        u = t - 1
                        pe.wait_ge(sg["xT"].sem, u + 1)
                        if u >= 2:
                            pe.wait_ge(sg["qk"].sem, u - 1)
                            pe.wait_ge(sg["vcopy"].sem, u - 1)
                        for c in range(FC):
                            pe.matmul(MX[:, u % 2, 0, :], XT[:, u % 2, c], wqkvT[:, c, 0:2 * D], start=c == 0, stop=c == FC - 1)
                        for c in range(FC):
                            m = pe.matmul(MX[:, u % 2, 1, 0:D], XT[:, u % 2, c], wqkvT[:, c, 2 * D:3 * D], start=c == 0,
                                          stop=c == FC - 1)
                        sg["qkv"].by(m)
                sg["qkv"].settle(pe)
                end_phase(pe, 1)
                for c in range(NT // CH):
                    for t in range(CH * c, CH * (c + 1)):
                        if t >= 2:
                            pe.wait_ge(sg["a2T"].sem, t - 1)
                        sg["tpb"].by(transpose_tile(SP_[:, t % 2], A2[:, t]))
                    pe.wait_ge(sg["a2T"].sem, CH * (c + 1))
                    if c >= 1:
                        pe.wait_ge(sg["hidT"].sem, FC * c)
                    for fo in range(FC):
                        for k in range(FC):
                            m = pe.matmul(MX[:, 0, fo, :], w1T[:, k, fo * P:(fo + 1) * P], A2T[:, k, :], start=k == 0,
                                          stop=k == FC - 1)
                    sg["hid"].by(m)
                    pe.wait_ge(sg["hidT"].sem, FC * (c + 1))
                    for t in range(CH * c, CH * (c + 1)):
                        if t >= 2:
                            pe.wait_ge(sg["o1"].sem, t - 1)
                        for k in range(FC):
                            m = pe.matmul(OAB(t)[:, 0:D], HT[:, c, k, (t % CH) * P:(t % CH + 1) * P], w2T[:, k, :],
                                          start=k == 0, stop=k == FC - 1)
                        sg["out1"].by(m)
                sg["out1"].settle(pe)
                end_phase(pe, 2)
                for t in range(NT + 1):
                    if t < NT:
                        pe.wait_ge(sg["hs"].sem, t + 1)
                        if t >= 2:
                            pe.wait_ge(sg["hT"].sem, t - 1)
                        sg["tph"].by(transpose_tile(SP_[:, t % 2], HS[:, t]))
                        pe.wait_ge(sg["hT"].sem, t + 1)
                        if t >= 2:
                            pe.wait_ge(sg["v2"].sem, t - 1)
                        for k in range(FC):
                            m = pe.matmul(MX[:, 0, t % 2, 0:NQKV], XT[:, t % 2, k], wqkv2[:, k, :], start=k == 0, stop=k == FC - 1)
                        sg["qkv2"].by(m)
                    if t >= 1:
                        u = t - 1
                        pe.wait_ge(sg["part2"].sem, u + 1)
                        if u >= 2:
                            pe.wait_ge(sg["qts"].sem, u - 1)
                            pe.wait_ge(sg["kts"].sem, u - 1)
                        for j in range(3):
                            for k in range(FC):
                                m = pe.transpose(MX[:, 1, u % 2, :].bitcast(BF16)[:, (FC * j + k) * P:(FC * j + k + 1) * P],
                                                 PT[:, u % 2, j, k * P:(k + 1) * P], identb[:, :])
                        sg["tpq"].by(m)
                        for j in range(3):
                            m = pe.transpose(OAB(u).bitcast(BF16)[0:KV, j * P:(j + 1) * P], PT[:, u % 2, j, D:D + KV], identb[:, :])
                        sg["tpq"].by(m)
                sg["tpq"].settle(pe)
                end_phase(pe, 3)
                state = {"piece": 0, "n": 0}

                def max_piece(g, h, qt):
                    i = state["piece"]
                    if i >= 2:
                        pe.wait_ge(sg["mx"].sem, i - 1)
                    n = (qt + 1) * P
                    lhsT = QST[0:MROW, g * G + h, qt * P:(qt + 1) * P]
                    for k0 in range(0, n, 512):
                        k1 = min(n, k0 + 512)
                        out = MX[:, i % 2, k0 // 512, 0:k1 - k0]
                        last = k1 == n
                        m = pe.matmul(out, lhsT, KST[0:MROW, g, k0:k1], start=True, stop=not last)
                        if last:
                            m = pe.matmul(out[:, k1 - k0 - P:k1 - k0], identb[:, :], mask_qk[:, :], start=False, stop=True)
                    sg["nm"].by(m)
                    state["piece"] += 1

                def max_rows(g):
                    i = state["piece"]
                    pe.wait_ge(sg["part0"].sem, g + 1)
                    pe.wait_ge(sg["mx"].sem, i - 1)
                    for qt in range(NT):
                        m = pe.transpose(MX[0:3 * G, i % 2, 0, :].bitcast(BF16)[:, qt * P:(qt + 1) * P],
                                         MT[:, qt].rearrange("p j h -> p (j h)"), identb[:, :])
                    sg["nm"].by(m)
                    state["piece"] += 1

                def scores(g, c, kt, h):
                    n = state["n"]
                    q0 = max(0, kt - CH * c) * P
                    diag = kt >= CH * c
                    if n >= 2:
                        pe.wait_ge(sg["exp"].sem, n - 1)
                    m = pe.matmul(SP_[:, n % 2, q0:512], KST[0:KROWS, g, kt * P:(kt + 1) * P],
                                  QST[0:KROWS, g * G + h, c * 512 + q0:(c + 1) * 512], start=True, stop=not diag)
                    if diag:
                        m = pe.matmul(SP_[:, n % 2, q0:q0 + P], identb[:, :], mask_kq[:, :], start=False, stop=True)
                    sg["s"].by(m)
                    state["n"] += 1

                def weighted_values(k, g, c, kt):
                    q0 = max(0, kt - CH * c) * P
                    pe.wait_ge(sg["exp"].sem, G * (k + 1))
                    if kt == 0 and k > 0:
                        pe.wait_ge(sg["ot"].sem, 2 * g + c)
                    last = kt == CH * (c + 1) - 1
                    for h in range(G):
                        m = pe.matmul(OA[32 * h:32 * (h + 1), q0:512], V1[:, kt, g, :], PR[:, (G * k + h) % 8, q0:512],
                                      start=kt == 0, stop=last, tile_position=(0, 32 * h))
                    sg["pv"].by(m)

                def turn_out(i):
                    pe.wait_ge(sg["ot"].sem, i + 1)
                    if i >= 1:
                        pe.wait_ge(sg["ctx"].sem, i)
                    for q in range(CH):
                        m = pe.transpose(OB[:, q * P:(q + 1) * P], OT[:, q * P:(q + 1) * P], ident[:, :])
                    sg["otp"].by(m)

                pe.wait_ge(sg["qst"].sem, 16 * NSLOT)
                pe.wait_ge(sg["kst"].sem, 16 * NSLOT)
                pieces = [(h, qt) for h in range(G) for qt in range(NT)]
                for h, qt in pieces:
                    max_piece(0, h, qt)
                max_rows(0)
                order = list(steps())
                for k, (g, c, kt) in enumerate(order):
                    s = k % STEPS
                    if s == 0:
                        pe.wait_ge(sg["mrow"].sem, 48 * (g + 1))
                    scores(g, c, kt, 0)
                    scores(g, c, kt, 1)
                    if k >= 1:
                        weighted_values(k - 1, *order[k - 1])
                    scores(g, c, kt, 2)
                    scores(g, c, kt, 3)
                    if g + 1 < HKV:
                        for h, qt in pieces[PPS * s:PPS * (s + 1)]:
                            max_piece(g + 1, h, qt)
                        if s == STEPS - 1:
                            max_rows(g + 1)
                    if s == 1 and g >= 1:
                        turn_out(2 * g - 1)
                    if s == CH + 1:
                        turn_out(2 * g)
                weighted_values(len(order) - 1, *order[-1])
                turn_out(2 * HKV - 1)
                sg["otp"].settle(pe)
                end_phase(pe, 4)
                for t in range(NT + 1):
                    if t < NT:
                        if t >= 2:
                            pe.wait_ge(sg["cT"].sem, t - 1)
                        sg["tpc"].by(transpose_tile(SP_[:, t % 2], CTX[:, t]))
                    if t >= 1:
                        u = t - 1
                        pe.wait_ge(sg["cT"].sem, u + 1)
                        if u >= 2:
                            pe.wait_ge(sg["h2"].sem, u - 1)
                        for k in range(FC):
                            m = pe.matmul(OAB(u)[:, 0:D], XT[:, u % 2, k], wo[:, k, :], start=k == 0, stop=k == FC - 1)
                        sg["wo"].by(m)
                for t in range(NT + 1):
                    if t < NT:
                        pe.wait_ge(sg["fl"].sem, t + 1)
                        if t >= 2:
                            pe.wait_ge(sg["fT"].sem, t - 1)
                        else:
                            pe.wait_ge(sg["cT"].sem, NT)
                        sg["tpf"].by(transpose_tile(SP_[:, t % 2], FL[:, t]))
                    if t >= 1:
                        u = t - 1
                        pe.wait_ge(sg["fT"].sem, u + 1)
                        for k in range(FC):
                            m = pe.matmul(MX[:, 0, 0, u * E:(u + 1) * E], XN[:, u % 2, k * P:(k + 1) * P], wr[:, k, :],
                                          start=k == 0, stop=k == FC - 1)
                        sg["lg"].by(m)
                sg["lg"].settle(pe)
                end_batch(pe, "pe")


def experts_kernel(nc, a, dram, out):
    ctx = ExitStack()
    with ctx:
        def sb(name, shape, dt=F32):
            return ctx.enter_context(nc.sbuf_tensor(name, shape, dt))

        def ps(name, shape, dt=F32):
            return ctx.enter_context(nc.psum_tensor(name, shape, dt))

        wg = sb("wg", [P, E, FC, F])
        wu = sb("wu", [P, E, FC, F])
        wd = sb("wd", [P, E, FK, D])
        identm = sb("identm", [P, P])
        nhalfm = sb("nhalfm", [P, 2])
        FLm = sb("FLm", [P, 2, D])
        X1m = sb("X1m", [P, 2, D])
        ACC = sb("ACC", [P, 2, D])
        W8m = sb("W8m", [P, 2, E])
        FT = sb("FT", [P, 2, FC, P])
        AG = sb("AG", [P, 2, F])
        AGT = sb("AGT", [P, 2, FK, P])
        bs = sb("bs", [P, 2, 6])
        mvm = sb("mvm", [P, 2, 2])
        cf = sb("cf", [P, 4, 2])
        GU = ps("GU", [P, 2, 2, F])
        TA = ps("TA", [P, 2, 512])
        DN = ps("DN", [P, 2, 512])

        sg = Signals(nc, ctx, "loaded tpf fT gu silu ag tpa agT down acc yclip ystat yvar coef step norm y stored", "m_")
        setup = Signals(nc, ctx, "wload ident", "ms_")
        arrive = ctx.enter_context(nc.semaphore("pair_arrive"))
        go = {n: ctx.enter_context(nc.semaphore("pair_go_" + n)) for n in ("act", "dve", "pe", "pool")}

        def end_pair(eng, own):
            eng.sem_inc(arrive, 1)
            eng.wait_ge(go[own], 1)
            eng.sem_clear(go[own])

        block = ctx.enter_context(nc.Block())
        fl, x1, h2, w8 = (dram[n].rearrange("(i j p) f -> i p j f", j=2, p=P) for n in ("flat", "x1", "h2", "w8"))
        od = out.rearrange("b (i j p) f -> (b i) p j f", j=2, p=P)
        NI = B * NT // 2
        NS = 2 * E

        @block.sync
        def _(sp):
            w = setup["wload"]
            w.by(sp.dma_start(wg[:, :], a["L0_ffn_Wg"].rearrange("e (c p) f -> p e c f", p=P)), 16)
            w.by(sp.dma_start(wu[:, :], a["L0_ffn_Wu"].rearrange("e (c p) f -> p e c f", p=P)), 16)
            w.by(sp.dma_start(wd[:, :], a["L0_ffn_Wd"].rearrange("e (c p) f -> p e c f", p=P)), 16)
            with sp.Fori(0, NI) as i:
                for dst, src in ((FLm, fl), (X1m, x1), (ACC, h2), (W8m, w8)):
                    sg["loaded"].by(sp.dma_start(dst[:, :, :], src[bass.ds(i, 1)].squeeze(0)), 16)
                sp.wait_ge(sg["y"].sem, 2)
                sg["stored"].by(sp.dma_start(od[bass.ds(i, 1)].squeeze(0), X1m[:, :, :]), 16)
                sp.wait_ge(sg["stored"].sem, 16)
                sp.wait_ge(arrive, len(go))
                for s in (arrive, *(x.sem for x in sg.all)):
                    sp.sem_clear(s)
                for s in go.values():
                    sp.sem_inc(s, 1)

        @block.gpsimd
        def _(pool):
            setup["ident"].by(pool.memset(identm[:, :], 0.0))
            setup["ident"].by(pool.memset(nhalfm[:, :], -0.5))
            setup["ident"].settle(pool)
            setup["ident"].by(pool.affine_select(out=identm[:, :], in_=identm[:, :], compare_op=ALU.not_equal, fill=1.0,
                                               base=0, pattern=[[-1, P]], channel_multiplier=1))
            with pool.Fori(0, NI) as i:
                pool.wait_ge(sg["yvar"].sem, 2)
                st = sg["step"].sem
                pool.tensor_scalar(cf[:, 0, :], mvm[:, :, 1], 1.0, LN_EPS, ALU.mult, ALU.add).then_inc(st, 1)
                pool.wait_ge(st, 1)
                pool.tensor_tensor(cf[:, 1, :], cf[:, 0, :], nhalfm[:, :], ALU.pow).then_inc(st, 1)
                pool.wait_ge(st, 2)
                pool.tensor_tensor(cf[:, 2, :], cf[:, 1, :], mvm[:, :, 0], ALU.mult).then_inc(st, 1)
                pool.wait_ge(st, 3)
                pool.tensor_scalar(cf[:, 3, :], cf[:, 2, :], -1.0, 0.0, ALU.mult, ALU.add).then_inc(st, 1)
                for j in range(2):
                    pool.wait_ge(sg["norm"].sem, j + 1)
                    pool.tensor_tensor(X1m[:, j], X1m[:, j], ACC[:, j], ALU.add).then_inc(sg["y"].sem, 1)
                pool.wait_ge(sg["y"].sem, 2)
                end_pair(pool, "pool")

        @block.scalar
        def _(act):
            with act.Fori(0, NI) as i:
                for j in range(2):
                    act.wait_ge(sg["tpf"].sem, j + 1)
                    act.activation(FT[:, j].rearrange("p c s -> p (c s)"), TA[:, j, 0:D], ACT.Copy).then_inc(sg["fT"].sem, 1)
                for s in range(NS):
                    act.wait_ge(sg["gu"].sem, s + 1)
                    if s >= 2:
                        act.wait_ge(sg["tpa"].sem, s - 1)
                    act.activation(AG[:, s % 2], GU[:, s % 2, 0], ACT.Silu).then_inc(sg["silu"].sem, 1)
                    if s >= 1:
                        act.wait_ge(sg["tpa"].sem, s)
                        if s >= 3:
                            act.wait_ge(sg["down"].sem, s - 2)
                        act.activation(AGT[:, (s - 1) % 2].rearrange("p c s -> p (c s)"), TA[:, (s - 1) % 2],
                                       ACT.Copy).then_inc(sg["agT"].sem, 1)
                s = NS
                act.wait_ge(sg["tpa"].sem, s)
                act.wait_ge(sg["down"].sem, s - 2)
                act.activation(AGT[:, (s - 1) % 2].rearrange("p c s -> p (c s)"), TA[:, (s - 1) % 2],
                               ACT.Copy).then_inc(sg["agT"].sem, 1)
                act.wait_ge(sg["step"].sem, 4)
                for j in range(2):
                    act.activation(ACC[:, j], ACC[:, j], ACT.Identity, bias=cf[:, 3, j:j + 1],
                                   scale=cf[:, 1, j:j + 1]).then_inc(sg["norm"].sem, 1)
                act.wait_ge(sg["norm"].sem, 2)
                end_pair(act, "act")

        @block.vector
        def _(dve):
            with dve.Fori(0, NI) as i:
                dve.wait_ge(sg["loaded"].sem, 64)
                for s in range(NS + 2):
                    if s < NS:
                        dve.wait_ge(sg["silu"].sem, s + 1)
                        dve.tensor_tensor(AG[:, s % 2], GU[:, s % 2, 1], AG[:, s % 2], ALU.mult).then_inc(sg["ag"].sem, 1)
                    if s >= 2:
                        u = s - 2
                        j, e = u // E, u % E
                        dve.wait_ge(sg["down"].sem, u + 1)
                        if e >= 1:
                            dve.wait_ge(sg["acc"].sem, u)
                        dve.scalar_tensor_tensor(out=ACC[:, j], in0=DN[:, u % 2, 0:D], scalar=W8m[:, j, e:e + 1], in1=ACC[:, j],
                                                 op0=ALU.mult, op1=ALU.add).then_inc(sg["acc"].sem, 1)
                dve.wait_ge(sg["acc"].sem, NS)
                for j in range(2):
                    dve.tensor_scalar(ACC[:, j], ACC[:, j], 100.0, -100.0, ALU.min, ALU.max).then_inc(sg["yclip"].sem, 1)
                dve.wait_ge(sg["yclip"].sem, 2)
                for j in range(2):
                    dve.bn_stats(bs[:, j], ACC[:, j]).then_inc(sg["ystat"].sem, 1)
                dve.wait_ge(sg["ystat"].sem, 2)
                for j in range(2):
                    dve.bn_aggr(mvm[:, j], bs[:, j]).then_inc(sg["yvar"].sem, 1)
                dve.wait_ge(sg["yvar"].sem, 2)
                end_pair(dve, "dve")

        @block.tensor
        def _(pe):
            pe.wait_ge(setup["wload"].sem, 48)
            pe.wait_ge(setup["ident"].sem, 3)
            with pe.Fori(0, NI) as i:
                pe.wait_ge(sg["loaded"].sem, 64)
                for j in range(2):
                    for c in range(FC):
                        m = pe.transpose(TA[:, j, c * P:(c + 1) * P], FLm[:, j, c * P:(c + 1) * P], identm[:, :])
                    m.then_inc(sg["tpf"].sem, 1)
                for s in range(NS + 2):
                    if s < NS:
                        j, e = s // E, s % E
                        if e == 0:
                            pe.wait_ge(sg["fT"].sem, j + 1)
                        if s >= 2:
                            pe.wait_ge(sg["ag"].sem, s - 1)
                        for x, w in enumerate((wg, wu)):
                            for c in range(FC):
                                m = pe.matmul(GU[:, s % 2, x], FT[:, j, c], w[:, e, c], start=c == 0, stop=c == FC - 1)
                        m.then_inc(sg["gu"].sem, 1)
                    if 1 <= s <= NS:
                        u = s - 1
                        pe.wait_ge(sg["ag"].sem, u + 1)
                        if u < 2:
                            pe.wait_ge(sg["fT"].sem, 2)
                        else:
                            pe.wait_ge(sg["agT"].sem, u - 1)
                        for c in range(FK):
                            m = pe.transpose(TA[:, u % 2, c * P:(c + 1) * P], AG[:, u % 2, c * P:(c + 1) * P], identm[:, :])
                        m.then_inc(sg["tpa"].sem, 1)
                    if s >= 2:
                        u = s - 2
                        e = u % E
                        pe.wait_ge(sg["agT"].sem, u + 1)
                        if u >= 2:
                            pe.wait_ge(sg["acc"].sem, u - 1)
                        for c in range(FK):
                            m = pe.matmul(DN[:, u % 2, 0:D], AGT[:, u % 2, c], wd[:, e, c], start=c == 0, stop=c == FK - 1)
                        m.then_inc(sg["down"].sem, 1)
                pe.wait_ge(sg["acc"].sem, NS)
                end_pair(pe, "pe")


_INS = ["L0_attn_x", "L0_attn_Wq", "L0_attn_Wk", "L0_attn_Wv", "L0_attn_lambda_params", "L0_attn_g1", "L0_attn_g2",
        "L0_attn_g3", "L0_attn_W1", "L0_attn_W2", "L0_ffn_ln1_w", "L0_ffn_ln2_w", "L0_ffn_Wq", "L0_ffn_Wk", "L0_ffn_Wv",
        "L0_ffn_Wo", "L0_ffn_Wr", "L0_ffn_Wg", "L0_ffn_Wu", "L0_ffn_Wd"]


def rope_table():
    inv = (1.0 / np.float32(THETA) ** (np.arange(0, HD, 2, dtype=np.float32) / np.float32(HD))).astype(np.float32)
    ang = (np.arange(S, dtype=np.float32)[:, None] * inv).astype(np.float32)
    c, s = np.cos(ang).astype(np.float32), np.sin(ang).astype(np.float32)
    return np.concatenate([c, c, -s, s], axis=1)


def build(nc, a, out):
    dram = {}
    for name, shape, dt in (("x1", [B * S, D], F32), ("h2", [B * S, D], F32), ("flat", [B * S, D], F32),
                            ("w8", [B * S, E], F32), ("qd", [3, D, S], BF16), ("kd", [3, KV, S], BF16)):
        dram[name] = nc.dram_tensor("scratch_" + name, shape, dt, kind="Internal").ap()
    attention_kernel(nc, a, dram)
    experts_kernel(nc, a, dram, out)


def kernel(**inputs):
    import concourse.bacc as bacc
    from concourse.bass_utils import run_bass_kernel_spmd

    nc = bacc.Bacc("TRN2", target_bir_lowering=False, num_devices=1)
    arrays = {"in_" + n: np.ascontiguousarray(inputs[n]) for n in _INS}
    arrays["in_rope"] = rope_table()
    a = {n[3:]: nc.dram_tensor(n, v.shape, mybir.dt.from_np(v.dtype), kind="ExternalInput").ap() for n, v in arrays.items()}
    out = nc.dram_tensor("out", (B, S, D), F32, kind="ExternalOutput").ap()
    build(nc, a, out)
    r = run_bass_kernel_spmd(nc, [arrays], core_ids=[0])
    return r.results[0]["out"]
```

```python
from contextlib import ExitStack

import numpy as np

import concourse.bass as bass
from concourse import mybir

F32 = mybir.dt.float32
BF16 = mybir.dt.bfloat16
U32 = mybir.dt.uint32
I32 = mybir.dt.int32
ALU = mybir.AluOpType
ACT = mybir.ActivationFunctionType
AX = mybir.AxisListType

P = 128
B, S, D = 8, 1024, 256
NT = S // P
FC = D // P
H, HD = 16, 16
HKV = 4
G = H // HKV
KV = HKV * HD
NQKV = D + 2 * KV
E, F = 8, 512
FK = F // P
TT = B * NT
UNROLL = 8
NSLOT_TILES = -(-(2 * TT + E - 1) // UNROLL) * UNROLL
CH = 4
LN_EPS = 1e-5
EPS1 = float(np.finfo(np.float32).eps)
LAMBDA_INIT = 0.8 - 0.6 * float(np.exp(-0.3 * 0))
SCALE1 = 1.0 / float(np.sqrt(D // 2))
SCALE2 = 0.25
THETA = 10000.0
MASKED = -1e30
Q_PART = [0, 0, 0, 1, 1, 2]
K_PART = [0, 1, 2, 0, 1, 0]
NSLOT = len(Q_PART)
MROW = NSLOT * HD
KROWS = MROW + 3


class Signal:

    def __init__(self, sem):
        self.sem = sem
        self.n = 0

    def by(self, instruction, k=1):
        instruction.then_inc(self.sem, k)
        self.n += k

    def settle(self, eng):
        eng.wait_ge(self.sem, self.n)


class Signals:
    def __init__(self, nc, ctx, names, prefix):
        self.all = []
        self.table = {}
        for name in names.split():
            s = Signal(ctx.enter_context(nc.semaphore(prefix + name)))
            self.table[name] = s
            self.all.append(s)

    def __getitem__(self, name):
        return self.table[name]


def attention_kernel(nc, a, dram):
    ctx = ExitStack()
    with ctx:
        def sb(name, shape, dt=F32):
            return ctx.enter_context(nc.sbuf_tensor(name, shape, dt))

        def ps(name, shape, dt=F32):
            return ctx.enter_context(nc.psum_tensor(name, shape, dt))

        w_raw = sb("w_raw", [P, 5, FC, D])
        wqkvT = sb("wqkvT", [P, FC, 3 * D])
        w1T = sb("w1T", [P, FC, D])
        w2T = sb("w2T", [P, FC, D])
        wqkv2 = sb("wqkv2", [P, FC, NQKV])
        wo = sb("wo", [P, FC, D])
        wr = sb("wr", [P, FC, E])
        g1c = sb("g1c", [P, FC])
        ln1c = sb("ln1c", [P, FC])
        g2row = sb("g2row", [P, D])
        g3row = sb("g3row", [P, D])
        ln2row = sb("ln2row", [P, D])
        lam = sb("lam", [P, 8])
        crow = sb("crow", [P, D])
        rope = sb("rope", [P, NT, 2 * HD])
        ident = sb("ident", [P, P])
        identb = sb("identb", [P, P], BF16)
        mask_qk = sb("mask_qk", [P, P], BF16)
        mask_kq = sb("mask_kq", [P, P], BF16)
        nhalf = sb("nhalf", [P, P])
        X = sb("X", [P, NT, D])
        AT = sb("AT", [P, NT, D])
        A2 = sb("A2", [P, NT, D])
        O1 = sb("O1", [P, NT, D])
        HS = sb("HS", [P, NT, D])
        XN = sb("XN", [P, 2, D])
        XT = sb("XT", [P, 2, FC, P])
        EX = sb("EX", [P, 2, 2 * D])
        QK = sb("QK", [P, 2, 2 * D])
        VS = sb("VS", [P, 2, D])
        KP = sb("KP", [P, 2, D])
        KVS = sb("KVS", [P, D])
        SQ = sb("SQ", [P, 2, D])
        work = sb("work", [P, 3 * H * D])
        P1 = [work[:, i * H * D:(i + 1) * H * D] for i in range(2)]
        P2 = work[:, 2 * H * D:3 * H * D]
        workb = work[:, :].bitcast(BF16)
        QST = workb[:, 0:H * S].rearrange("p (h s) -> p h s", h=H)
        QTS = workb[:, H * S:H * S + 3 * FC * S].rearrange("p (j c s) -> p j c s", j=3, c=FC)
        KST = sb("KST", [P, HKV, S], BF16)
        KTS = sb("KTS", [KV, 3, S], BF16)
        A2T = sb("A2T", [P, FC, CH * P])
        HT = sb("HT", [P, 2, FC, CH * P])
        Q2 = sb("Q2", [P, 2, D + KV])
        RA = sb("RA", [P, D + KV])
        RB = sb("RB", [P, D + KV])
        PT = sb("PT", [P, 2, 3, D + KV], BF16)
        V1 = sb("V1", [P, NT, HKV, 32])
        PR = sb("PR", [P, 8, 512])
        OT = sb("OT", [P, 512])
        RC = sb("RC", [P, 4, G])
        NM = sb("NM", [P, NT, G])
        NMR = sb("NMR", [P, NT, G])
        MT = sb("MT", [P, NT, 3, G], BF16)
        MR = sb("MR", [3 * G, S], BF16)
        CTX = O1
        H2 = A2
        FL = AT
        bst = sb("bst", [P, NT, 6])
        mv = sb("mv", [P, NT, 2])
        st = sb("st", [P, 12, NT])
        MS = sb("MS", [P, NT, H])
        R16 = sb("R16", [P, NT, H])
        LG = sb("LG", [P, NT, E])
        top = sb("top", [P, NT, 8])
        topi = sb("topi", [P, NT, 8], U32)
        ROUTE = sb("ROUTE", [P, NT, 4])
        tw = sb("tw", [P, 4, NT])

        MX = ps("MX", [P, 2, 2, 512])
        SP_ = ps("SP_", [P, 2, 512])
        OA = ps("OA", [P, 512])
        OB = ps("OB", [P, 512])

        names = ("x_loaded stats coef xn tp xT qkv expo vcopy e1 qk kprime prod1 kv prod2 attn sq ms r16 an ssq a2 "
                 "tpb a2T hid hidT out1 o1 y1 x1 stats2 coef2 hs tph hT qkv2 q2 v2 rope ropes part0 part1 part2 partd tpq qts kts "
                 "bounced bouncek qst kst mx nm mt mrow s exp pv o ot otp rc ctx "
                 "tpc cT wo h2 ss2 coef3 fl tpf fT lg lgs topk stored pool_step dve_step act_step phase")
        sg = Signals(nc, ctx, names, "s_")
        setup = Signals(nc, ctx, "wload tpw wT pool dve act lam done", "i_")
        arrive = ctx.enter_context(nc.semaphore("batch_arrive"))
        go = {n: ctx.enter_context(nc.semaphore("batch_go_" + n)) for n in ("act", "dve", "pe", "pool")}

        xb = a["L0_attn_x"].rearrange("b (t p) f -> b p t f", p=P)
        qd, kd = dram["qd"], dram["kd"]
        x1d, h2d, fld, routed = (dram[n].rearrange("(b t p) f -> b p t f", b=B, p=P) for n in ("x1", "h2", "flat", "route"))
        NWLOAD = 5 + 3 + 1 + 1 + 2 + 3 + 1 + 1
        phases = 5

        STEPS = 3 * CH
        PPS = -(-G * NT // STEPS)

        def OAB(t):
            return (OA, OB)[t % 2][:, :]

        def steps():
            for g in range(HKV):
                for c in range(S // 512):
                    for kt in range(CH * (c + 1)):
                        yield g, c, kt

        def pv_steps(g, c):
            return STEPS * g + (CH if c == 0 else STEPS)

        def dve_plan():
            pieces = [(h, qt) for h in range(G) for qt in range(NT)]
            for p in pieces:
                yield 0, "max", p
            yield 0, "parts", None
            yield 0, "rows", None
            for g in range(HKV):
                for s in range(STEPS):
                    if g + 1 < HKV:
                        for p in pieces[PPS * s:PPS * (s + 1)]:
                            yield g + 1, "max", p
                        if s == STEPS - 1:
                            yield g + 1, "parts", None
                            yield g + 1, "rows", None
                    if s == 0 and g >= 1:
                        yield g - 1, "out", 1
                    if s == 1 and g >= 1:
                        yield g - 1, "ctx", 1
                    if s == CH:
                        yield g, "out", 0
                    if s == CH + 1:
                        yield g, "ctx", 0
            yield HKV - 1, "out", 1
            yield HKV - 1, "ctx", 1

        block = ctx.enter_context(nc.Block())

        def end_phase(eng, k):
            eng.sem_inc(sg["phase"].sem, 1)
            eng.wait_ge(sg["phase"].sem, 4 * k)

        def end_batch(eng, own):
            eng.sem_inc(arrive, 1)
            eng.wait_ge(go[own], 1)
            eng.sem_clear(go[own])

        @block.sync
        def _(sp):
            w = setup["wload"]
            for i, n in enumerate(("Wq", "Wk", "Wv", "W1", "W2")):
                w.by(sp.dma_start(w_raw[:, i], a["L0_attn_" + n].rearrange("(c p) n -> p c n", p=P)), 16)
            for i, (n, c0, c1) in enumerate((("Wq", 0, D), ("Wk", D, D + KV), ("Wv", D + KV, NQKV))):
                w.by(sp.dma_start(wqkv2[:, :, c0:c1], a["L0_ffn_" + n].rearrange("(c p) n -> p c n", p=P)), 16)
            w.by(sp.dma_start(wo[:, :, :], a["L0_ffn_Wo"].rearrange("(c p) n -> p c n", p=P)), 16)
            w.by(sp.dma_start(wr[:, :, :], a["L0_ffn_Wr"].rearrange("(c p) n -> p c n", p=P)), 16)
            w.by(sp.dma_start(g1c[:, :], a["L0_attn_g1"].rearrange("(c p) -> p c", p=P), allow_slow_non_contiguous=True), 16)
            w.by(sp.dma_start(ln1c[:, :], a["L0_ffn_ln1_w"].rearrange("(c p) -> p c", p=P), allow_slow_non_contiguous=True), 16)
            w.by(sp.dma_start(g2row[:, 0:HD], a["L0_attn_g2"].partition_broadcast(P)), 16)
            w.by(sp.dma_start(g3row[:, :], a["L0_attn_g3"].partition_broadcast(P)), 16)
            w.by(sp.dma_start(ln2row[:, :], a["L0_ffn_ln2_w"].partition_broadcast(P)), 16)
            w.by(sp.dma_start(lam[:, 0:4], a["L0_attn_lambda_params"].partition_broadcast(P)), 16)
            w.by(sp.dma_start(rope[:, :, :], a["rope"].rearrange("(t p) n -> p t n", p=P)), 16)
            assert w.n == 16 * NWLOAD

            with sp.Fori(0, B) as b:
                sg["x_loaded"].by(sp.dma_start(X[:, :, :], xb[bass.ds(b, 1)].squeeze(0)), 16)
                sp.wait_ge(sg["kts"].sem, NT)
                sg["bouncek"].by(sp.dma_start(kd.rearrange("j r s -> r j s"), KTS[:, :, :]), 16)
                sp.wait_ge(sg["qts"].sem, NT)
                sg["bounced"].by(sp.dma_start(qd.rearrange("j (c r) s -> r j c s", c=FC), QTS), 16)
                sp.wait_ge(sg["bouncek"].sem, 16)
                for i in range(NSLOT):
                    sg["kst"].by(sp.dma_start(KST[HD * i:HD * (i + 1), :, :],
                                              kd[K_PART[i]].rearrange("(h e) s -> e h s", e=HD)), 16)
                sp.wait_ge(sg["bounced"].sem, 16)
                for i in range(NSLOT):
                    sg["qst"].by(sp.dma_start(QST[HD * i:HD * (i + 1), :, :],
                                              qd[Q_PART[i]].rearrange("(h e) s -> e h s", e=HD)), 16)
                for g in range(HKV):
                    sp.wait_ge(sg["mt"].sem, g + 1)
                    for j in range(3):
                        sg["mrow"].by(sp.dma_start(QST[MROW + j:MROW + j + 1, G * g:G * (g + 1), :],
                                                   MR[G * j:G * (j + 1), :]), 16)
                st_ = sg["stored"]
                sp.wait_ge(sg["x1"].sem, NT)
                st_.by(sp.dma_start(x1d[bass.ds(b, 1)].squeeze(0), X[:, :, :]), 16)
                sp.wait_ge(sg["h2"].sem, NT)
                st_.by(sp.dma_start(h2d[bass.ds(b, 1)].squeeze(0), H2[:, :, :]), 16)
                sp.wait_ge(sg["fl"].sem, NT)
                st_.by(sp.dma_start(fld[bass.ds(b, 1)].squeeze(0), FL[:, :, :]), 16)
                sp.wait_ge(sg["topk"].sem, 1)
                st_.by(sp.dma_start(routed[bass.ds(b, 1)].squeeze(0), ROUTE[:, :, :]), 16)
                st_.settle(sp)
                sp.wait_ge(arrive, len(go))
                for s in (arrive, *(x.sem for x in sg.all)):
                    sp.sem_clear(s)
                for s in go.values():
                    sp.sem_inc(s, 1)

        @block.gpsimd
        def _(pool):
            ps_ = setup["pool"]
            ps_.by(pool.memset(ident[:, :], 0.0))
            ps_.by(pool.memset(identb[:, :], 0.0))
            ps_.by(pool.memset(mask_qk[:, :], 0.0))
            ps_.by(pool.memset(mask_kq[:, :], 0.0))
            ps_.by(pool.memset(nhalf[:, :], -0.5))
            ps_.by(pool.memset(V1[:, :, :, HD:32], 0.0))
            ps_.settle(pool)
            ps_.by(pool.memset(KST[MROW:P, :, :], 1.0))
            ps_.settle(pool)
            ps_.settle(pool)
            for m in (ident, identb):
                ps_.by(pool.affine_select(out=m[:, :], in_=m[:, :], compare_op=ALU.not_equal, fill=1.0, base=0,
                                          pattern=[[-1, P]], channel_multiplier=1))
            ps_.by(pool.affine_select(out=mask_qk[:, :], in_=mask_qk[:, :], compare_op=ALU.is_ge, fill=MASKED,
                                      base=0, pattern=[[-1, P]], channel_multiplier=1))
            ps_.by(pool.affine_select(out=mask_kq[:, :], in_=mask_kq[:, :], compare_op=ALU.is_ge, fill=MASKED,
                                      base=0, pattern=[[1, P]], channel_multiplier=-1))
            ps_.by(pool.memset(V1[:, :, :, HD:HD + 1], 1.0))
            ps_.settle(pool)
            pool.wait_ge(setup["done"].sem, 1)

            ps1 = sg["pool_step"]

            def rsqrt(dst, src, scale, eps):
                ps1.by(pool.tensor_scalar(dst, src, scale, eps, ALU.mult, ALU.add))
                ps1.settle(pool)
                ps1.by(pool.tensor_tensor(dst, dst, nhalf[:, 0:dst.shape[-1]], ALU.pow))
                ps1.settle(pool)

            def mul(dst, x, y):
                ps1.by(pool.tensor_tensor(dst, x, y, ALU.mult))
                ps1.settle(pool)

            def norm_coefficients(eps2, done, with_second):
                rsqrt(st[:, 0, :], mv[:, :, 1], 1.0, LN_EPS)
                mul(st[:, 1, :], mv[:, :, 1], st[:, 0, :])
                mul(st[:, 1, :], st[:, 1, :], st[:, 0, :])
                rsqrt(st[:, 2, :], st[:, 1, :], 1.0, eps2)
                if with_second:
                    mul(st[:, 3, :], st[:, 0, :], st[:, 2, :])
                else:
                    ps1.by(pool.tensor_copy(st[:, 3, :], st[:, 0, :]))
                    ps1.settle(pool)
                mul(st[:, 4, :], mv[:, :, 0], st[:, 3, :])
                done.by(pool.tensor_scalar(st[:, 4, :], st[:, 4, :], -1.0, 0.0, ALU.mult, ALU.add))

            with pool.Fori(0, B) as b:
                pool.wait_ge(sg["stats"].sem, 2 * NT)
                norm_coefficients(EPS1, sg["coef"], True)
                for t in range(NT):
                    pool.wait_ge(sg["qk"].sem, t + 1)
                    sg["kprime"].by(pool.tensor_tensor(KP[:, t % 2], QK[:, t % 2, D:2 * D], crow[:, :], ALU.mult))
                    sg["kprime"].settle(pool)
                    pool.wait_ge(sg["vcopy"].sem, t + 1)
                    if t >= 2:
                        pool.wait_ge(sg["kv"].sem, t - 1)
                    sg["prod1"].by(pool.tensor_tensor(
                        P1[t % 2].rearrange("p (e d h) -> p e d h", e=HD, d=HD),
                        KP[:, t % 2].rearrange("p (h e) -> p e h", e=HD).unsqueeze(2).broadcast_to([P, HD, HD, H]),
                        VS[:, t % 2].rearrange("p (h d) -> p d h", d=HD).unsqueeze(1).broadcast_to([P, HD, HD, H]),
                        ALU.mult))
                pool.wait_ge(sg["ms"].sem, NT)
                R = R16[:, :, :].rearrange("p t h -> p (t h)")
                rsqrt(R, MS[:, :, :].rearrange("p t h -> p (t h)"), 1.0 / HD, EPS1)
                pool.sem_inc(sg["r16"].sem, 1)
                pool.wait_ge(sg["ssq"].sem, NT)
                rsqrt(st[:, 6, :], st[:, 5, :], 1.0 / D, EPS1)
                pool.sem_inc(sg["r16"].sem, 1)
                sg["prod1"].settle(pool)
                end_phase(pool, 1)
                pool.wait_ge(sg["stats2"].sem, 2 * NT)
                norm_coefficients(1.0, sg["coef2"], False)
                for t in range(NT):
                    pool.wait_ge(sg["y1"].sem, t + 1)
                    sg["x1"].by(pool.tensor_tensor(X[:, t], X[:, t], O1[:, t], ALU.add))
                sg["x1"].settle(pool)
                end_phase(pool, 2)
                pool.wait_ge(sg["stats2"].sem, 4 * NT)
                norm_coefficients(LN_EPS, sg["coef2"], False)
                for t in range(NT):
                    pool.wait_ge(sg["q2"].sem, t + 1)
                    q = Q2[:, t % 2].rearrange("p (h a e) -> p h a e", a=2, e=HD // 2)
                    ra = RA[:, :].rearrange("p (h a e) -> p h a e", a=2, e=HD // 2)
                    rb = RB[:, :].rearrange("p (h a e) -> p h a e", a=2, e=HD // 2)
                    nh = (D + KV) // HD
                    sh = [P, nh, HD // 2]

                    def table(c0):
                        return rope[:, t, c0:c0 + HD // 2].unsqueeze(1).broadcast_to(sh)
                    if t >= 1:
                        pool.wait_ge(sg["part1"].sem, 2 * t)
                    for half in range(2):
                        ps1.by(pool.tensor_tensor(ra[:, :, half], q[:, :, half], table(0), ALU.mult))
                        ps1.by(pool.tensor_tensor(rb[:, :, half], q[:, :, 1 - half], table(HD + 8 * half), ALU.mult))
                    ps1.settle(pool)
                    sg["rope"].by(pool.tensor_tensor(RA[:, :], RA[:, :], RB[:, :], ALU.add))
                    sg["rope"].settle(pool)
                end_phase(pool, 3)
                end_phase(pool, 4)
                pool.wait_ge(sg["ss2"].sem, NT)
                rsqrt(st[:, 8, :], st[:, 7, :], 1.0 / D, LN_EPS)
                pool.sem_inc(sg["coef3"].sem, 1)
                end_batch(pool, "pool")

        @block.scalar
        def _(act):
            act.wait_ge(setup["wload"].sem, 16 * NWLOAD)
            act.wait_ge(setup["dve"].sem, 2)
            setup["act"].by(act.activation(lam[:, 6:8], lam[:, 4:6], ACT.Exp))

            with act.Fori(0, B) as b:
                act.wait_ge(sg["coef"].sem, 1)
                for t in range(NT + 1):
                    if t < NT:
                        if t >= 2:
                            act.wait_ge(sg["tp"].sem, t - 1)
                        sg["xn"].by(act.activation(XN[:, t % 2], X[:, t], ACT.Identity, bias=st[:, 4, t:t + 1],
                                                   scale=st[:, 3, t:t + 1]))
                    if t >= 1:
                        u = t - 1
                        act.wait_ge(sg["qkv"].sem, u + 1)
                        if u >= 2:
                            act.wait_ge(sg["qk"].sem, u - 1)
                            act.wait_ge(sg["prod1"].sem, u - 1)
                        sg["expo"].by(act.activation(EX[:, u % 2], MX[:, u % 2, 0, :], ACT.Exp))
                        sg["vcopy"].by(act.activation(VS[:, u % 2], MX[:, u % 2, 1, 0:D], ACT.Copy))
                    if t >= 2:
                        u = t - 2
                        act.wait_ge(sg["attn"].sem, u + 1)
                        if u >= 2:
                            act.wait_ge(sg["ms"].sem, u - 1)
                        sg["sq"].by(act.activation(SQ[:, u % 2], AT[:, u], ACT.Square))
                u = NT - 1
                act.wait_ge(sg["attn"].sem, u + 1)
                act.wait_ge(sg["ms"].sem, u - 1)
                sg["sq"].by(act.activation(SQ[:, u % 2], AT[:, u], ACT.Square))
                act.wait_ge(sg["ms"].sem, NT)
                act.wait_ge(sg["an"].sem, 2)
                for t in range(NT):
                    if t >= 2:
                        act.wait_ge(sg["ssq"].sem, t - 1)
                    sg["ssq"].by(act.activation(SQ[:, t % 2], AT[:, t], ACT.Square, accum_out=st[:, 5, t:t + 1]))
                sg["ssq"].settle(act)
                end_phase(act, 1)
                for c in range(NT // CH):
                    for t in range(CH * c, CH * (c + 1)):
                        act.wait_ge(sg["tpb"].sem, t + 1)
                        if t == CH * c and c >= 1:
                            act.wait_ge(sg["hid"].sem, c)
                        sg["a2T"].by(act.activation(A2T[:, :, (t % CH) * P:(t % CH + 1) * P],
                                                    SP_[:, t % 2, 0:D].rearrange("p (c s) -> p c s", c=FC), ACT.Copy))
                    act.wait_ge(sg["hid"].sem, c + 1)
                    for fo in range(FC):
                        sg["hidT"].by(act.activation(HT[:, c, fo, :], MX[:, 0, fo, :], ACT.Gelu))
                act.wait_ge(sg["coef2"].sem, 1)
                for t in range(NT):
                    sg["y1"].by(act.activation(O1[:, t], O1[:, t], ACT.Identity, bias=st[:, 4, t:t + 1],
                                               scale=st[:, 3, t:t + 1]))
                sg["y1"].settle(act)
                end_phase(act, 2)
                act.wait_ge(sg["coef2"].sem, 2)
                for t in range(NT):
                    sg["hs"].by(act.activation(HS[:, t], X[:, t], ACT.Identity, bias=st[:, 4, t:t + 1],
                                               scale=st[:, 3, t:t + 1]))
                for t in range(NT):
                    act.wait_ge(sg["tph"].sem, t + 1)
                    if t >= 2:
                        act.wait_ge(sg["qkv2"].sem, t - 1)
                    sg["hT"].by(act.activation(XT[:, t % 2].rearrange("p c s -> p (c s)"), SP_[:, t % 2, 0:D], ACT.Copy))
                    act.wait_ge(sg["qkv2"].sem, t + 1)
                    if t >= 2:
                        act.wait_ge(sg["part2"].sem, t - 1)
                    sg["q2"].by(act.activation(Q2[:, t % 2], MX[:, 0, t % 2, 0:D + KV], ACT.Copy,
                                               scale=st[:, 2, t:t + 1]))
                    sg["v2"].by(act.activation(V1[:, t, :, 0:HD],
                                               MX[:, 0, t % 2, D + KV:NQKV].rearrange("p (g e) -> p g e", g=HKV),
                                               ACT.Copy, scale=st[:, 2, t:t + 1]))
                    if t >= 1:
                        u = t - 1
                        act.wait_ge(sg["tpq"].sem, 2 * u + 2)
                        sg["qts"].by(act.activation(
                            QTS[:, :, :, u * P:(u + 1) * P],
                            MX[:, 1, u % 2, :].bitcast(BF16)[:, 0:3 * FC * P].rearrange("p (j c s) -> p j c s", j=3, c=FC),
                            ACT.Copy))
                u = NT - 1
                act.wait_ge(sg["tpq"].sem, 2 * u + 2)
                sg["qts"].by(act.activation(
                    QTS[:, :, :, u * P:(u + 1) * P],
                    MX[:, 1, u % 2, :].bitcast(BF16)[:, 0:3 * FC * P].rearrange("p (j c s) -> p j c s", j=3, c=FC),
                    ACT.Copy))
                sg["qts"].settle(act)
                sg["v2"].settle(act)
                end_phase(act, 3)
                n = 0
                for g, c, kt in steps():
                    q0 = max(0, kt - CH * c) * P
                    for h in range(G):
                        act.wait_ge(sg["s"].sem, n + 1)
                        if n >= 8:
                            act.wait_ge(sg["pv"].sem, (n - 8) // G + 1)
                        sg["exp"].by(act.activation(PR[:, n % 8, q0:512], SP_[:, n % 2, q0:512], ACT.Exp))
                        n += 1
                sg["exp"].settle(act)
                end_phase(act, 4)
                for t in range(NT):
                    act.wait_ge(sg["tpc"].sem, t + 1)
                    if t >= 2:
                        act.wait_ge(sg["wo"].sem, t - 1)
                    sg["cT"].by(act.activation(XT[:, t % 2].rearrange("p c s -> p (c s)"), SP_[:, t % 2, 0:D], ACT.Copy))
                    if t >= 1:
                        u = t - 1
                        act.wait_ge(sg["h2"].sem, u + 1)
                        if u >= 2:
                            act.wait_ge(sg["ss2"].sem, u - 1)
                        sg["ss2"].by(act.activation(SQ[:, u % 2], H2[:, u], ACT.Square, accum_out=st[:, 7, u:u + 1]))
                u = NT - 1
                act.wait_ge(sg["h2"].sem, u + 1)
                act.wait_ge(sg["ss2"].sem, u - 1)
                sg["ss2"].by(act.activation(SQ[:, u % 2], H2[:, u], ACT.Square, accum_out=st[:, 7, u:u + 1]))
                for t in range(NT):
                    act.wait_ge(sg["tpf"].sem, t + 1)
                    if t >= 2:
                        act.wait_ge(sg["lg"].sem, t - 1)
                    sg["fT"].by(act.activation(XN[:, t % 2], SP_[:, t % 2, 0:D], ACT.Copy))
                act.wait_ge(sg["lgs"].sem, 1)
                sg["act_step"].by(act.activation(tw[:, 1, :], tw[:, 0, :], ACT.Exp))
                sg["act_step"].settle(act)
                end_batch(act, "act")

        @block.vector
        def _(dve):
            dve.wait_ge(setup["wload"].sem, 16 * NWLOAD)
            sd = setup["dve"]
            sd.by(dve.tensor_tensor(lam[:, 4:5], lam[:, 0:1], lam[:, 1:2], ALU.mult))
            sd.by(dve.tensor_tensor(lam[:, 5:6], lam[:, 2:3], lam[:, 3:4], ALU.mult))
            for n in (HD, 2 * HD, 4 * HD, 8 * HD):
                sd.settle(dve)
                sd.by(dve.tensor_copy(g2row[:, n:2 * n], g2row[:, 0:n]))
            sd.settle(dve)
            sd.by(dve.tensor_scalar(g2row[:, :], g2row[:, :], 1.0 - LAMBDA_INIT, None, ALU.mult))
            dve.wait_ge(setup["act"].sem, 1)
            sd.by(dve.memset(crow[:, :], SCALE1))
            sd.settle(dve)
            c3 = crow[:, :].rearrange("p (h e) -> p h e", e=HD)[:, :, HD // 2:HD]
            sd.by(dve.tensor_tensor(lam[:, 0:1], lam[:, 6:7], lam[:, 7:8], ALU.subtract))
            sd.settle(dve)
            sd.by(dve.tensor_scalar(lam[:, 0:1], lam[:, 0:1], LAMBDA_INIT, -1.0, ALU.add, ALU.mult))
            sd.settle(dve)
            assert sd.n == 10 - 0, sd.n
            sd.by(dve.tensor_scalar(c3, c3, lam[:, 0:1], None, ALU.mult))
            for c in range(FC):
                sd.by(dve.tensor_scalar(wqkv2[:, c, 0:D], wqkv2[:, c, 0:D], ln1c[:, c:c + 1], SCALE2, ALU.mult, ALU.mult))
                sd.by(dve.tensor_scalar(wqkv2[:, c, D:NQKV], wqkv2[:, c, D:NQKV], ln1c[:, c:c + 1], None, ALU.mult))
            for i in range(5):
                dve.wait_ge(setup["tpw"].sem, i + 1)
                src = SP_[:, i % 2, :].rearrange("p (c n) -> p c n", c=FC)
                if i < 3:
                    for c in range(FC):
                        setup["wT"].by(dve.tensor_scalar(wqkvT[:, c, i * D:(i + 1) * D], src[:, c], g1c[:, c:c + 1],
                                                         None, ALU.mult))
                else:
                    dst = (w1T, w2T)[i - 3]
                    for c in range(FC):
                        setup["wT"].by(dve.tensor_copy(dst[:, c], src[:, c]))
            setup["wT"].settle(dve)
            sd.settle(dve)
            dve.sem_inc(setup["done"].sem, 1)
            dve.wait_ge(setup["pool"].sem, 12)

            ds = sg["dve_step"]

            def stats(t, src, done):
                done.by(dve.bn_stats(bst[:, t], src))

            def aggregate(done):
                done.settle(dve)
                for t in range(NT):
                    done.by(dve.bn_aggr(mv[:, t], bst[:, t]))

            with dve.Fori(0, B) as b:
                dve.wait_ge(sg["x_loaded"].sem, 16)
                for t in range(NT):
                    stats(t, X[:, t], sg["stats"])
                aggregate(sg["stats"])
                for t in range(NT + 1):
                    if t < NT:
                        dve.wait_ge(sg["tp"].sem, t + 1)
                        if t >= 2:
                            dve.wait_ge(sg["qkv"].sem, t - 1)
                        sg["xT"].by(dve.tensor_copy(XT[:, t % 2].rearrange("p c s -> p (c s)"), SP_[:, t % 2, 0:D]))
                    if t >= 1:
                        u = t - 1
                        dve.wait_ge(sg["expo"].sem, u + 1)
                        sg["e1"].by(dve.tensor_scalar(EX[:, u % 2], EX[:, u % 2], 1.0, -1.0, ALU.min, ALU.add))
                        sg["e1"].settle(dve)
                        if u >= 2:
                            dve.wait_ge(sg["kprime"].sem, u - 1)
                        sg["qk"].by(dve.scalar_tensor_tensor(out=QK[:, u % 2], in0=MX[:, u % 2, 0, :], scalar=0.0,
                                                             in1=EX[:, u % 2], op0=ALU.max, op1=ALU.add))
                        sg["qk"].settle(dve)
                        dve.wait_ge(sg["prod1"].sem, u + 1)
                        sg["kv"].by(dve.tensor_reduce(KVS[:, :], P1[u % 2].rearrange("p (x h) -> p x h", h=H), AX.X, ALU.add))
                        sg["kv"].settle(dve)
                        sg["prod2"].by(dve.tensor_tensor(
                            P2.rearrange("p (h d e) -> p h d e", d=HD, e=HD),
                            QK[:, u % 2, 0:D].rearrange("p (h e) -> p h e", e=HD).unsqueeze(2).broadcast_to([P, H, HD, HD]),
                            KVS[:, :].rearrange("p (e d) -> p d e", d=HD).unsqueeze(1).broadcast_to([P, H, HD, HD]),
                            ALU.mult))
                        sg["prod2"].settle(dve)
                        sg["attn"].by(dve.tensor_reduce(AT[:, u], P2.rearrange("p (x e) -> p x e", e=HD), AX.X, ALU.add))
                    if t >= 2:
                        u = t - 2
                        dve.wait_ge(sg["sq"].sem, u + 1)
                        sg["ms"].by(dve.tensor_reduce(MS[:, u], SQ[:, u % 2].rearrange("p (h d) -> p h d", d=HD), AX.X, ALU.add))
                u = NT - 1
                dve.wait_ge(sg["sq"].sem, u + 1)
                sg["ms"].by(dve.tensor_reduce(MS[:, u], SQ[:, u % 2].rearrange("p (h d) -> p h d", d=HD), AX.X, ALU.add))
                dve.wait_ge(sg["r16"].sem, 1)
                at4 = AT[:, :, :].rearrange("p t (h d) -> p (t h) d", d=HD)
                sg["attn"].settle(dve)
                sg["an"].by(dve.tensor_tensor(at4, at4, R16[:, :, :].rearrange("p t h -> p (t h)").unsqueeze(2)
                                              .broadcast_to([P, NT * H, HD]), ALU.mult))
                sg["an"].settle(dve)
                sg["an"].by(dve.tensor_tensor(AT[:, :, :], AT[:, :, :], g2row[:, :].unsqueeze(1).broadcast_to([P, NT, D]),
                                              ALU.mult))
                sg["an"].settle(dve)
                dve.wait_ge(sg["r16"].sem, 2)
                for t in range(NT):
                    ds.by(dve.tensor_scalar(A2[:, t], g3row[:, :], st[:, 6, t:t + 1], 1.0, ALU.mult, ALU.add))
                ds.settle(dve)
                for t in range(NT):
                    sg["a2"].by(dve.tensor_tensor(A2[:, t], A2[:, t], AT[:, t], ALU.mult))
                sg["a2"].settle(dve)
                end_phase(dve, 1)
                for t in range(NT):
                    dve.wait_ge(sg["out1"].sem, t + 1)
                    sg["o1"].by(dve.tensor_tensor(O1[:, t], OAB(t)[:, 0:D], A2[:, t], ALU.add))
                    sg["o1"].settle(dve)
                    stats(t, O1[:, t], sg["stats2"])
                aggregate(sg["stats2"])
                sg["stats2"].settle(dve)
                end_phase(dve, 2)
                for t in range(NT):
                    stats(t, X[:, t], sg["stats2"])
                aggregate(sg["stats2"])
                for t in range(NT):
                    dve.wait_ge(sg["rope"].sem, t + 1)
                    if t >= 2:
                        dve.wait_ge(sg["tpq"].sem, 2 * (t - 1))
                    pt = PT[:, t % 2]
                    ds.by(dve.tensor_copy(pt[:, 0], RA[:, :]))
                    ds.settle(dve)
                    sg["part1"].by(dve.tensor_tensor(Q2[:, t % 2], RA[:, :], pt[:, 0], ALU.subtract))
                    sg["part1"].settle(dve)
                    sg["part1"].by(dve.tensor_copy(pt[:, 1], Q2[:, t % 2]))
                    sg["part1"].settle(dve)
                    sg["part2"].by(dve.tensor_tensor(pt[:, 2], Q2[:, t % 2], pt[:, 1], ALU.subtract))
                    if t >= 1:
                        u = t - 1
                        dve.wait_ge(sg["tpq"].sem, 2 * u + 2)
                        sg["kts"].by(dve.tensor_copy(
                            KTS[:, :, u * P:(u + 1) * P],
                            OAB(u).bitcast(BF16)[0:KV, 0:3 * P].rearrange("p (j s) -> p j s", j=3)))
                u = NT - 1
                dve.wait_ge(sg["tpq"].sem, 2 * u + 2)
                sg["kts"].by(dve.tensor_copy(
                    KTS[:, :, u * P:(u + 1) * P],
                    OAB(u).bitcast(BF16)[0:KV, 0:3 * P].rearrange("p (j s) -> p j s", j=3)))
                sg["kts"].settle(dve)
                end_phase(dve, 3)
                piece = 0
                for g, kind, arg in dve_plan():
                    if kind == "max":
                        h, qt = arg
                        dve.wait_ge(sg["nm"].sem, piece + 1)
                        n = (qt + 1) * P
                        src = MX[:, piece % 2].rearrange("p a n -> p (a n)")[:, 0:n]
                        sg["mx"].by(dve.tensor_reduce(NM[:, qt, h:h + 1], src, AX.X, ALU.max, negate=True))
                        piece += 1
                    elif kind == "parts":
                        sg["mx"].settle(dve)
                        mt = MT[:, :, :, :]
                        ds.by(dve.tensor_copy(mt[:, :, 0], NM[:, :, :]))
                        ds.settle(dve)
                        ds.by(dve.tensor_tensor(NMR[:, :, :], NM[:, :, :], mt[:, :, 0], ALU.subtract))
                        ds.settle(dve)
                        ds.by(dve.tensor_copy(mt[:, :, 1], NMR[:, :, :]))
                        ds.settle(dve)
                        sg["part0"].by(dve.tensor_tensor(mt[:, :, 2], NMR[:, :, :], mt[:, :, 1], ALU.subtract))
                    elif kind == "rows":
                        dve.wait_ge(sg["nm"].sem, piece + 1)
                        if g >= 1:
                            dve.wait_ge(sg["mrow"].sem, 48 * g)
                        src = MX[0:3 * G, piece % 2, 0, :].bitcast(BF16)
                        dve_mt = dve.tensor_copy(MR[:, :], src)
                        sg["mt"].by(dve_mt)
                        sg["mt"].settle(dve)
                        dve.sem_inc(sg["mx"].sem, 1)
                        sg["mx"].n += 1
                        piece += 1
                    elif kind == "out":
                        c = arg
                        k = (g * 2 + c)
                        dve.wait_ge(sg["pv"].sem, pv_steps(g, c))
                        if k >= 1:
                            dve.wait_ge(sg["otp"].sem, k)
                        sg["ot"].by(dve.tensor_copy(OT[:, :], OA[:, :]))
                    else:
                        c = arg
                        k = (g * 2 + c)
                        dve.wait_ge(sg["otp"].sem, k + 1)
                        o = OB[:, :].rearrange("p (q h d) -> p q h d", q=CH, h=G)
                        ds.by(dve.reciprocal(RC[:, :, :], o[:, :, :, HD]))
                        ds.settle(dve)
                        sg["ctx"].by(dve.tensor_tensor(
                            CTX[:, CH * c:CH * (c + 1), g * G * HD:(g + 1) * G * HD].rearrange("p q (h d) -> p q h d", d=HD),
                            o[:, :, :, 0:HD], RC[:, :, :].unsqueeze(3).broadcast_to([P, CH, G, HD]), ALU.mult))
                        sg["ctx"].settle(dve)
                end_phase(dve, 4)
                for t in range(NT):
                    dve.wait_ge(sg["wo"].sem, t + 1)
                    ds.by(dve.tensor_tensor(H2[:, t], OAB(t)[:, 0:D], HS[:, t], ALU.add))
                    ds.settle(dve)
                    sg["h2"].by(dve.tensor_scalar(H2[:, t], H2[:, t], 100.0, -100.0, ALU.min, ALU.max))
                sg["h2"].settle(dve)
                dve.wait_ge(sg["coef3"].sem, 1)
                for t in range(NT):
                    sg["fl"].by(dve.scalar_tensor_tensor(out=FL[:, t], in0=H2[:, t], scalar=st[:, 8, t:t + 1],
                                                         in1=ln2row[:, :], op0=ALU.mult, op1=ALU.mult))
                dve.wait_ge(sg["lg"].sem, NT)
                ds.by(dve.tensor_copy(LG[:, :, :], MX[:, 0, 0, 0:NT * E].rearrange("p (t e) -> p t e", e=E)))
                ds.settle(dve)
                for t in range(NT):
                    ds.by(dve.max(top[:, t], LG[:, t]))
                ds.settle(dve)
                for t in range(NT):
                    ds.by(dve.max_index(topi[:, t], top[:, t], LG[:, t]))
                sg["lgs"].by(dve.tensor_tensor(tw[:, 0, :], top[:, :, 1], top[:, :, 0], ALU.subtract))
                ds.settle(dve)
                ds.by(dve.tensor_copy(ROUTE[:, :, 0:2], topi[:, :, 0:2]))
                dve.wait_ge(sg["act_step"].sem, 1)
                ds.by(dve.tensor_scalar(tw[:, 2, :], tw[:, 1, :], 1.0, None, ALU.add))
                ds.settle(dve)
                ds.by(dve.reciprocal(tw[:, 3, :], tw[:, 2, :]))
                ds.settle(dve)
                ds.by(dve.tensor_copy(ROUTE[:, :, 2], tw[:, 3, :]))
                sg["topk"].by(dve.tensor_tensor(ROUTE[:, :, 3], tw[:, 1, :], tw[:, 3, :], ALU.mult))
                sg["topk"].settle(dve)
                end_batch(dve, "dve")

        @block.tensor
        def _(pe):
            pe.wait_ge(setup["pool"].sem, 12)
            pe.wait_ge(setup["wload"].sem, 16 * NWLOAD)
            for i in range(5):
                if i >= 2:
                    pe.wait_ge(setup["wT"].sem, 2 * (i - 1))
                for fc in range(FC):
                    for ec in range(FC):
                        m = pe.transpose(SP_[:, i % 2, fc * D + ec * P:fc * D + (ec + 1) * P],
                                         w_raw[:, i, ec, fc * P:(fc + 1) * P], ident[:, :])
                setup["tpw"].by(m)
            pe.wait_ge(setup["done"].sem, 1)

            def transpose_tile(dst, src):
                for c in range(FC):
                    m = pe.transpose(dst[:, c * P:(c + 1) * P], src[:, c * P:(c + 1) * P], ident[:, :])
                return m

            with pe.Fori(0, B) as b:
                for t in range(NT + 1):
                    if t < NT:
                        pe.wait_ge(sg["xn"].sem, t + 1)
                        if t >= 2:
                            pe.wait_ge(sg["xT"].sem, t - 1)
                        sg["tp"].by(transpose_tile(SP_[:, t % 2], XN[:, t % 2]))
                    if t >= 1:
                        u = t - 1
                        pe.wait_ge(sg["xT"].sem, u + 1)
                        if u >= 2:
                            pe.wait_ge(sg["qk"].sem, u - 1)
                            pe.wait_ge(sg["vcopy"].sem, u - 1)
                        for c in range(FC):
                            pe.matmul(MX[:, u % 2, 0, :], XT[:, u % 2, c], wqkvT[:, c, 0:2 * D], start=c == 0, stop=c == FC - 1)
                        for c in range(FC):
                            m = pe.matmul(MX[:, u % 2, 1, 0:D], XT[:, u % 2, c], wqkvT[:, c, 2 * D:3 * D], start=c == 0,
                                          stop=c == FC - 1)
                        sg["qkv"].by(m)
                sg["qkv"].settle(pe)
                end_phase(pe, 1)
                for c in range(NT // CH):
                    for t in range(CH * c, CH * (c + 1)):
                        if t >= 2:
                            pe.wait_ge(sg["a2T"].sem, t - 1)
                        sg["tpb"].by(transpose_tile(SP_[:, t % 2], A2[:, t]))
                    pe.wait_ge(sg["a2T"].sem, CH * (c + 1))
                    if c >= 1:
                        pe.wait_ge(sg["hidT"].sem, FC * c)
                    for fo in range(FC):
                        for k in range(FC):
                            m = pe.matmul(MX[:, 0, fo, :], w1T[:, k, fo * P:(fo + 1) * P], A2T[:, k, :], start=k == 0,
                                          stop=k == FC - 1)
                    sg["hid"].by(m)
                    pe.wait_ge(sg["hidT"].sem, FC * (c + 1))
                    for t in range(CH * c, CH * (c + 1)):
                        if t >= 2:
                            pe.wait_ge(sg["o1"].sem, t - 1)
                        for k in range(FC):
                            m = pe.matmul(OAB(t)[:, 0:D], HT[:, c, k, (t % CH) * P:(t % CH + 1) * P], w2T[:, k, :],
                                          start=k == 0, stop=k == FC - 1)
                        sg["out1"].by(m)
                sg["out1"].settle(pe)
                end_phase(pe, 2)
                for t in range(NT + 1):
                    if t < NT:
                        pe.wait_ge(sg["hs"].sem, t + 1)
                        if t >= 2:
                            pe.wait_ge(sg["hT"].sem, t - 1)
                        sg["tph"].by(transpose_tile(SP_[:, t % 2], HS[:, t]))
                        pe.wait_ge(sg["hT"].sem, t + 1)
                        if t >= 2:
                            pe.wait_ge(sg["v2"].sem, t - 1)
                        for k in range(FC):
                            m = pe.matmul(MX[:, 0, t % 2, 0:NQKV], XT[:, t % 2, k], wqkv2[:, k, :], start=k == 0, stop=k == FC - 1)
                        sg["qkv2"].by(m)
                    if t >= 1:
                        u = t - 1
                        pe.wait_ge(sg["part2"].sem, u + 1)
                        if u >= 2:
                            pe.wait_ge(sg["qts"].sem, u - 1)
                            pe.wait_ge(sg["kts"].sem, u - 1)
                        for j in range(3):
                            for k in range(FC):
                                m = pe.transpose(MX[:, 1, u % 2, :].bitcast(BF16)[:, (FC * j + k) * P:(FC * j + k + 1) * P],
                                                 PT[:, u % 2, j, k * P:(k + 1) * P], identb[:, :])
                        sg["tpq"].by(m)
                        for j in range(3):
                            m = pe.transpose(OAB(u).bitcast(BF16)[0:KV, j * P:(j + 1) * P], PT[:, u % 2, j, D:D + KV], identb[:, :])
                        sg["tpq"].by(m)
                sg["tpq"].settle(pe)
                end_phase(pe, 3)
                state = {"piece": 0, "n": 0}

                def max_piece(g, h, qt):
                    i = state["piece"]
                    if i >= 2:
                        pe.wait_ge(sg["mx"].sem, i - 1)
                    n = (qt + 1) * P
                    lhsT = QST[0:MROW, g * G + h, qt * P:(qt + 1) * P]
                    for k0 in range(0, n, 512):
                        k1 = min(n, k0 + 512)
                        out = MX[:, i % 2, k0 // 512, 0:k1 - k0]
                        last = k1 == n
                        m = pe.matmul(out, lhsT, KST[0:MROW, g, k0:k1], start=True, stop=not last)
                        if last:
                            m = pe.matmul(out[:, k1 - k0 - P:k1 - k0], identb[:, :], mask_qk[:, :], start=False, stop=True)
                    sg["nm"].by(m)
                    state["piece"] += 1

                def max_rows(g):
                    i = state["piece"]
                    pe.wait_ge(sg["part0"].sem, g + 1)
                    pe.wait_ge(sg["mx"].sem, i - 1)
                    for qt in range(NT):
                        m = pe.transpose(MX[0:3 * G, i % 2, 0, :].bitcast(BF16)[:, qt * P:(qt + 1) * P],
                                         MT[:, qt].rearrange("p j h -> p (j h)"), identb[:, :])
                    sg["nm"].by(m)
                    state["piece"] += 1

                def scores(g, c, kt, h):
                    n = state["n"]
                    q0 = max(0, kt - CH * c) * P
                    diag = kt >= CH * c
                    if n >= 2:
                        pe.wait_ge(sg["exp"].sem, n - 1)
                    m = pe.matmul(SP_[:, n % 2, q0:512], KST[0:KROWS, g, kt * P:(kt + 1) * P],
                                  QST[0:KROWS, g * G + h, c * 512 + q0:(c + 1) * 512], start=True, stop=not diag)
                    if diag:
                        m = pe.matmul(SP_[:, n % 2, q0:q0 + P], identb[:, :], mask_kq[:, :], start=False, stop=True)
                    sg["s"].by(m)
                    state["n"] += 1

                def weighted_values(k, g, c, kt):
                    q0 = max(0, kt - CH * c) * P
                    pe.wait_ge(sg["exp"].sem, G * (k + 1))
                    if kt == 0 and k > 0:
                        pe.wait_ge(sg["ot"].sem, 2 * g + c)
                    last = kt == CH * (c + 1) - 1
                    for h in range(G):
                        m = pe.matmul(OA[32 * h:32 * (h + 1), q0:512], V1[:, kt, g, :], PR[:, (G * k + h) % 8, q0:512],
                                      start=kt == 0, stop=last, tile_position=(0, 32 * h))
                    sg["pv"].by(m)

                def turn_out(i):
                    pe.wait_ge(sg["ot"].sem, i + 1)
                    if i >= 1:
                        pe.wait_ge(sg["ctx"].sem, i)
                    for q in range(CH):
                        m = pe.transpose(OB[:, q * P:(q + 1) * P], OT[:, q * P:(q + 1) * P], ident[:, :])
                    sg["otp"].by(m)

                pe.wait_ge(sg["qst"].sem, 16 * NSLOT)
                pe.wait_ge(sg["kst"].sem, 16 * NSLOT)
                pieces = [(h, qt) for h in range(G) for qt in range(NT)]
                for h, qt in pieces:
                    max_piece(0, h, qt)
                max_rows(0)
                order = list(steps())
                for k, (g, c, kt) in enumerate(order):
                    s = k % STEPS
                    if s == 0:
                        pe.wait_ge(sg["mrow"].sem, 48 * (g + 1))
                    scores(g, c, kt, 0)
                    scores(g, c, kt, 1)
                    if k >= 1:
                        weighted_values(k - 1, *order[k - 1])
                    scores(g, c, kt, 2)
                    scores(g, c, kt, 3)
                    if g + 1 < HKV:
                        for h, qt in pieces[PPS * s:PPS * (s + 1)]:
                            max_piece(g + 1, h, qt)
                        if s == STEPS - 1:
                            max_rows(g + 1)
                    if s == 1 and g >= 1:
                        turn_out(2 * g - 1)
                    if s == CH + 1:
                        turn_out(2 * g)
                weighted_values(len(order) - 1, *order[-1])
                turn_out(2 * HKV - 1)
                sg["otp"].settle(pe)
                end_phase(pe, 4)
                for t in range(NT + 1):
                    if t < NT:
                        if t >= 2:
                            pe.wait_ge(sg["cT"].sem, t - 1)
                        sg["tpc"].by(transpose_tile(SP_[:, t % 2], CTX[:, t]))
                    if t >= 1:
                        u = t - 1
                        pe.wait_ge(sg["cT"].sem, u + 1)
                        if u >= 2:
                            pe.wait_ge(sg["h2"].sem, u - 1)
                        for k in range(FC):
                            m = pe.matmul(OAB(u)[:, 0:D], XT[:, u % 2, k], wo[:, k, :], start=k == 0, stop=k == FC - 1)
                        sg["wo"].by(m)
                for t in range(NT + 1):
                    if t < NT:
                        pe.wait_ge(sg["fl"].sem, t + 1)
                        if t >= 2:
                            pe.wait_ge(sg["fT"].sem, t - 1)
                        else:
                            pe.wait_ge(sg["cT"].sem, NT)
                        sg["tpf"].by(transpose_tile(SP_[:, t % 2], FL[:, t]))
                    if t >= 1:
                        u = t - 1
                        pe.wait_ge(sg["fT"].sem, u + 1)
                        for k in range(FC):
                            m = pe.matmul(MX[:, 0, 0, u * E:(u + 1) * E], XN[:, u % 2, k * P:(k + 1) * P], wr[:, k, :],
                                          start=k == 0, stop=k == FC - 1)
                        sg["lg"].by(m)
                sg["lg"].settle(pe)
                end_batch(pe, "pe")


def experts_kernel(nc, a, dram, out):
    ctx = ExitStack()
    with ctx:
        def sb(name, shape, dt=F32):
            return ctx.enter_context(nc.sbuf_tensor(name, shape, dt))

        wg = sb("wg", [P, E, FC, F])
        wu = sb("wu", [P, E, FC, F])
        wd = sb("wd", [P, E, FK, D])
        identm = sb("identm", [P, P])
        RT = sb("RT", [P, TT, 4])
        slot = sb("slot", [P, 2, TT], U32)
        source = sb("source", [P, NSLOT_TILES], U32)
        texp = sb("texp", [P, NSLOT_TILES], I32)
        wsem = ctx.enter_context(nc.semaphore("r_wload"))
        route_tokens(nc, dram, RT, slot, source, texp, identm, (wg, wu, wd), a, wsem)
        run_experts(nc, dram, source, texp, identm, (wg, wu, wd), wsem)
        combine(nc, dram, RT, slot, out)


def route_tokens(nc, dram, RT, slot, source, texp, identm, weights, a, wsem):
    ctx = ExitStack()
    with ctx:
        def sb(name, shape, dt=F32):
            return ctx.enter_context(nc.sbuf_tensor(name, shape, dt))

        def ps(name, shape, dt=F32):
            return ctx.enter_context(nc.psum_tensor(name, shape, dt))

        NS = NSLOT_TILES
        below = sb("below", [P, P])
        ones = sb("ones", [P, P])
        io = sb("io", [P, max(NS, P)])
        io128 = sb("io128", [P, TT])
        token_lo = sb("token_lo", [P, 1])
        M = sb("M", [P, 2, TT, E])
        BR = sb("BR", [P, TT, E])
        tot = sb("tot", [P, E, TT])
        cum = sb("cum", [P, E, TT])
        base = sb("base", [P, E, TT])
        fill = sb("fill", [P, 4, E])
        cmp = sb("cmp", [P, NS, E])
        slotf = sb("slotf", [P, 2, TT])
        part = sb("part", [P, 2, 2, TT], U32)
        partf = sb("partf", [P, 2, 2, TT])
        lane1 = sb("lane1", [P, 2, P], BF16)
        tile1 = sb("tile1", [P, 2, 2, NS], BF16)
        src = sb("src", [P, 2, NS])
        pr = ps("pr", [P, 512])
        pt = ps("pt", [P, 512])
        pk = ps("pk", [P, 512])
        sg = Signals(nc, ctx, "loaded const step sums place onehot lists texp", "r_")
        block = ctx.enter_context(nc.Block())

        @block.sync
        def _(sp):
            sg["loaded"].by(sp.dma_start(RT[:, :, :], dram["route"].rearrange("(t p) f -> p t f", p=P)), 16)
            for w, n in zip(weights, ("Wg", "Wu", "Wd")):
                sp.dma_start(w[:, :], a["L0_ffn_" + n].rearrange("e (c p) f -> p e c f", p=P)).then_inc(wsem, 16)

        @block.gpsimd
        def _(pool):
            c = sg["const"]
            c.by(pool.memset(identm[:, :], 0.0))
            c.by(pool.memset(ones[:, :], 1.0))
            c.by(pool.memset(below[:, :], 0.0))
            c.by(pool.iota(io[:, :], [[1, max(NS, P)]], base=0, channel_multiplier=0, allow_small_or_imprecise_dtypes=True))
            c.by(pool.iota(io128[:, :], [[P, TT]], base=0, channel_multiplier=0, allow_small_or_imprecise_dtypes=True))
            c.by(pool.iota(token_lo[:, :], [[0, 1]], base=0, channel_multiplier=1, allow_small_or_imprecise_dtypes=True))
            c.settle(pool)
            c.by(pool.affine_select(out=identm[:, :], in_=identm[:, :], compare_op=ALU.not_equal, fill=1.0, base=0,
                                    pattern=[[-1, P]], channel_multiplier=1))
            c.by(pool.affine_select(out=below[:, :], in_=below[:, :], compare_op=ALU.is_ge, fill=1.0, base=0,
                                    pattern=[[-1, P]], channel_multiplier=1))

        @block.vector
        def _(dve):
            s = sg["step"]

            def do(instruction):
                s.by(instruction)
                s.settle(dve)

            dve.wait_ge(sg["const"].sem, 8)
            dve.wait_ge(sg["loaded"].sem, 16)
            sh = [P, TT, E]
            for j in range(2):
                do(dve.tensor_tensor(M[:, j], io[:, 0:E].unsqueeze(1).broadcast_to(sh),
                                     RT[:, :, j].unsqueeze(2).broadcast_to(sh), ALU.is_equal))
            do(dve.tensor_tensor(BR[:, :, :], M[:, 0], M[:, 1], ALU.add))
            dve.sem_inc(sg["onehot"].sem, 1)
            dve.wait_ge(sg["sums"].sem, 1)
            do(dve.tensor_copy(tot[:, :, :], pt[:, 0:TT * E].rearrange("p (t e) -> p e t", e=E)))
            for e in range(E):
                s.by(dve.tensor_tensor_scan(cum[:, e], ones[:, 0:TT], tot[:, e], 0.0, ALU.mult, ALU.add))
            s.settle(dve)
            do(dve.tensor_tensor(base[:, :, :], cum[:, :, :], tot[:, :, :], ALU.subtract))
            sh = [P, E, TT]
            do(dve.tensor_tensor(tot[:, :, :], cum[:, :, TT - 1:TT].broadcast_to(sh),
                                 io128[:, :].unsqueeze(1).broadcast_to(sh), ALU.is_gt))
            do(dve.tensor_reduce(fill[:, 0], tot[:, :, :], AX.X, ALU.add))
            do(dve.tensor_tensor_scan(fill[:, 1], ones[:, 0:E], fill[:, 0], 0.0, ALU.mult, ALU.add))
            do(dve.tensor_tensor(fill[:, 2], fill[:, 1], fill[:, 0], ALU.subtract))
            do(dve.tensor_scalar(fill[:, 3], fill[:, 2], float(P), None, ALU.mult))
            do(dve.tensor_tensor(base[:, :, :], base[:, :, :], fill[:, 3].unsqueeze(2).broadcast_to(sh), ALU.add))
            do(dve.tensor_tensor(BR[:, :, :], pr[:, 0:TT * E].rearrange("p (t e) -> p t e", e=E),
                                 base[:, :, :].rearrange("p e t -> p t e"), ALU.add))
            for j in range(2):
                do(dve.tensor_tensor(M[:, j], M[:, j], BR[:, :, :], ALU.mult))
                do(dve.tensor_reduce(slotf[:, j], M[:, j], AX.X, ALU.add))
            do(dve.tensor_copy(slot[:, :, :], slotf[:, :, :]))
            do(dve.tensor_scalar(part[:, 0], slot[:, :, :], 7, None, ALU.logical_shift_right))
            do(dve.tensor_scalar(part[:, 1], slot[:, :, :], P - 1, None, ALU.bitwise_and))
            do(dve.tensor_copy(partf[:, :, :, :], part[:, :, :, :]))
            sh = [P, NS, E]
            do(dve.tensor_tensor(cmp[:, :, :], io[:, 0:NS].unsqueeze(2).broadcast_to(sh),
                                 fill[:, 1].unsqueeze(1).broadcast_to(sh), ALU.is_ge))
            do(dve.tensor_reduce(src[:, 0], cmp[:, :, :], AX.X, ALU.add))
            do(dve.tensor_scalar(src[:, 0], src[:, 0], float(E - 1), None, ALU.min))
            do(dve.tensor_copy(texp[:, :], src[:, 0]))

            def one_hots(t, first=False):
                for j in range(2):
                    if not first:
                        dve.wait_ge(sg["lists"].sem, 2 * t + j - 1)
                    col = t if isinstance(t, int) else bass.ds(t, 1)
                    at = slice(t, t + 1) if isinstance(t, int) else col
                    lane = partf[:, 1, j, at]
                    til = partf[:, 0, j, at]
                    dve.tensor_scalar(lane1[:, j], io[:, 0:P], lane, None, ALU.is_equal)
                    dve.tensor_scalar(tile1[:, j, 0], io[:, 0:NS], til, token_lo[:, :], ALU.is_equal, ALU.mult)
                    dve.tensor_scalar(tile1[:, j, 1], io[:, 0:NS], til, io[:, at], ALU.is_equal, ALU.mult)\
                        .then_inc(sg["place"].sem, 1)

            one_hots(0, True)
            with dve.Fori(1, TT - 1) as t:
                one_hots(t)
            one_hots(TT - 1)
            dve.wait_ge(sg["lists"].sem, 2 * TT)
            do(dve.tensor_copy(src[:, :, :], pk[:, 0:2 * NS].rearrange("p (x n) -> p x n", x=2)))
            do(dve.scalar_tensor_tensor(out=src[:, 0], in0=src[:, 1], scalar=float(P), in1=src[:, 0], op0=ALU.mult, op1=ALU.add))
            do(dve.tensor_copy(source[:, :], src[:, 0]))

        @block.tensor
        def _(pe):
            pe.wait_ge(sg["onehot"].sem, 1)
            choices = BR[:, :, :].rearrange("p t e -> p (t e)")
            pe.matmul(pr[:, 0:TT * E], below[:, :], choices, start=True, stop=True)
            sg["sums"].by(pe.matmul(pt[:, 0:TT * E], ones[:, :], choices, start=True, stop=True))

            def lists(t, first=False, last=False):
                for j in range(2):
                    pe.wait_ge(sg["place"].sem, 2 * t + j + 1)
                    pe.matmul(pk[:, 0:2 * NS], lane1[:, j], tile1[:, j].rearrange("p x n -> p (x n)"),
                              start=first and j == 0, stop=last and j == 1).then_inc(sg["lists"].sem, 1)

            lists(0, first=True)
            with pe.Fori(1, TT - 1) as t:
                lists(t)
            lists(TT - 1, last=True)


def run_experts(nc, dram, source, texp, identm, weights, wsem):
    wg, wu, wd = weights
    ctx = ExitStack()
    with ctx:
        def sb(name, shape, dt=F32):
            return ctx.enter_context(nc.sbuf_tensor(name, shape, dt))

        def ps(name, shape, dt=F32):
            return ctx.enter_context(nc.psum_tensor(name, shape, dt))

        index = sb("index", [P, 2, 4], U32)
        XG = sb("XG", [P, 4, D])
        XT = sb("XTm", [P, 2, D])
        SL = sb("SL", [P, 2, F])
        AG = sb("AG", [P, 2, F])
        AGT = sb("AGT", [P, 2, F])
        Y = sb("Y", [P, 2, D])
        GB = ps("GB", [P, 2, F])
        UB = ps("UB", [P, 2, F])
        TX = ps("TX", [P, 2, 512])
        TA = ps("TA", [P, 512])
        DN = ps("DN", [P, 512])
        sg = Signals(nc, ctx, "index gathered0 gathered1 gathered2 gathered3 tx xT g gu silu ag tpa agT down y stored0 stored1 moved", "m_")
        N = NSLOT_TILES
        U = UNROLL
        yd = dram["y"]
        block = ctx.enter_context(nc.Block())

        def rolled(eng, body):
            with eng.Fori(0, N // U - 1) as i:
                body(i * U, i, False)
            body(N - U, N // U - 1, True)

        CREDIT = 2

        @block.sync
        def _(sp):
            def body(n0, i, last):
                for s in range(U):
                    sp.wait_ge(sg["y"].sem, n0 + s + 1 + CREDIT)
                    rows = yd[(n0 + s) * P:(n0 + s + 1) * P, :] if last else yd[bass.ds((n0 + s) * P, P), :]
                    sp.dma_start(rows, Y[:, s % 2]).then_inc(sg[f"stored{s % 2}"].sem, 16)
            for j in range(2):
                sp.sem_inc(sg[f"stored{j}"].sem, 16)
            rolled(sp, body)
            for j in range(2):
                sp.wait_ge(sg[f"stored{j}"].sem, 16 * (N // 2 + 1))

        @block.gpsimd
        def _(pool):
            def gather(s, ind):
                pool.indirect_dma_start(out=XG[:, s % 4], out_offset=None, in_=dram["flat"],
                                        in_offset=bass.IndirectOffsetOnAxis(ap=ind, axis=0))\
                    .then_inc(sg[f"gathered{s % 4}"].sem, 16)

            pool.tensor_copy(index[:, 1, :], source[:, 0:4]).then_inc(sg["index"].sem, 1)
            pool.wait_ge(sg["index"].sem, 1)
            for s in range(4):
                gather(s, index[:, 1, s:s + 1])

            def body(n0, i, last):
                for s in range(4 if last else U):
                    pool.wait_ge(sg["tx"].sem, n0 + s + 1)
                    pool.sem_inc(sg["moved"].sem, 1)
                    if s % 4 == 0:
                        first = n0 + s + 4
                        ind = source[:, first:first + 4] if last else source[:, bass.ds(first, 4)]
                        pool.tensor_copy(index[:, s // 4, 0:4], ind).then_inc(sg["index"].sem, 1)
                        pool.wait_ge(sg["index"].sem, 2 * i + s // 4 + 2)
                        pool.sem_inc(sg["moved"].sem, 1)
                    gather(s, index[:, s // 4, s % 4:s % 4 + 1])
            rolled(pool, body)

        @block.scalar
        def _(act):
            def x_evac(s, n):
                act.wait_ge(sg["tx"].sem, n + 1)
                act.activation(XT[:, s % 2], TX[:, s % 2, 0:D], ACT.Copy).then_inc(sg["xT"].sem, 1)

            def silu(s, n):
                act.wait_ge(sg["g"].sem, n + 1)
                act.wait_ge(sg["ag"].sem, n - 1 + CREDIT)
                act.activation(SL[:, s % 2], GB[:, s % 2], ACT.Silu).then_inc(sg["silu"].sem, 1)

            x_evac(0, 0)
            x_evac(1, 1)
            silu(0, 0)

            def body(n0, i, last):
                for s in range(U):
                    if not (last and s + 1 >= U):
                        silu(s + 1, n0 + s + 1)
                    act.wait_ge(sg["tpa"].sem, n0 + s + 1 + CREDIT)
                    act.activation(AGT[:, s % 2], TA[:, :], ACT.Copy).then_inc(sg["agT"].sem, 1)
                    if not (last and s + 2 >= U):
                        x_evac(s, n0 + s + 2)
            act.sem_inc(sg["agT"].sem, CREDIT)
            rolled(act, body)

        @block.vector
        def _(dve):
            def gate(s, n):
                dve.wait_ge(sg["gu"].sem, n + 1)
                dve.wait_ge(sg["silu"].sem, n + 1)
                dve.wait_ge(sg["tpa"].sem, n - 1 + CREDIT)
                dve.tensor_tensor(AG[:, s % 2], UB[:, s % 2], SL[:, s % 2], ALU.mult).then_inc(sg["ag"].sem, 1)

            dve.sem_inc(sg["ag"].sem, CREDIT)
            dve.sem_inc(sg["y"].sem, CREDIT)
            gate(0, 0)

            def body(n0, i, last):
                for s in range(U):
                    if not (last and s + 1 >= U):
                        gate(s + 1, n0 + s + 1)
                    dve.wait_ge(sg["down"].sem, n0 + s + 1)
                    dve.wait_ge(sg[f"stored{s % 2}"].sem, (i * (U // 2) + s // 2 + 1) * 16)
                    dve.tensor_copy(Y[:, s % 2], DN[:, 0:D]).then_inc(sg["y"].sem, 1)
            rolled(dve, body)

        @block.tensor
        def _(pe):
            def turn_x(s, i):
                pe.wait_ge(sg[f"gathered{s % 4}"].sem, (i * (U // 4) + s // 4 + 1) * 16)
                for c in range(FC):
                    m = pe.transpose(TX[:, s % 2, c * P:(c + 1) * P], XG[:, s % 4, c * P:(c + 1) * P], identm[:, :])
                m.then_inc(sg["tx"].sem, 1)

            def expert(n):
                at = texp[0:1, n:n + 1] if isinstance(n, int) else texp[0:1, bass.ds(n, 1)]
                return pe.value_load(at, min_val=0, max_val=E - 1)

            def project(s, n, e, w, out, done):
                for c in range(FC):
                    m = pe.matmul(out[:, s % 2], XT[:, s % 2, c * P:(c + 1) * P], w[:, bass.ds(e, 1), c, :].squeeze(1),
                                  start=c == 0, stop=c == FC - 1)
                m.then_inc(sg[done].sem, 1)

            pe.wait_ge(wsem, 48)
            pe.sem_inc(sg["tpa"].sem, CREDIT)
            turn_x(0, 0)
            turn_x(1, 0)
            e0 = expert(0)
            pe.wait_ge(sg["xT"].sem, 1)
            project(0, 0, e0, wg, GB, "g")
            project(0, 0, e0, wu, UB, "gu")

            def body(n0, i, last):
                for s in range(U):
                    n = n0 + s
                    more = not (last and s + 1 >= U)
                    if more:
                        e1 = expert(n + 1)
                        pe.wait_ge(sg["xT"].sem, n + 2)
                        pe.wait_ge(sg["ag"].sem, n + CREDIT)
                        project(s + 1, n + 1, e1, wg, GB, "g")
                    e = expert(n)
                    pe.wait_ge(sg["ag"].sem, n + 1 + CREDIT)
                    pe.wait_ge(sg["agT"].sem, n + CREDIT)
                    for c in range(FK):
                        m = pe.transpose(TA[:, c * P:(c + 1) * P], AG[:, s % 2, c * P:(c + 1) * P], identm[:, :])
                    m.then_inc(sg["tpa"].sem, 1)
                    if more:
                        project(s + 1, n + 1, e1, wu, UB, "gu")
                    pe.wait_ge(sg["agT"].sem, n + 1 + CREDIT)
                    pe.wait_ge(sg["y"].sem, n + CREDIT)
                    for c in range(FK):
                        m = pe.matmul(DN[:, 0:D], AGT[:, s % 2, c * P:(c + 1) * P], wd[:, bass.ds(e, 1), c, :].squeeze(1),
                                      start=c == 0, stop=c == FK - 1)
                    m.then_inc(sg["down"].sem, 1)
                    if not (last and s + 2 >= U):
                        turn_x(s + 2, i)
            rolled(pe, body)


def combine(nc, dram, RT, slot, out):
    ctx = ExitStack()
    with ctx:
        def sb(name, shape, dt=F32):
            return ctx.enter_context(nc.sbuf_tensor(name, shape, dt))

        U = 4
        NB = TT // U
        index = sb("indexc", [P, 2, 2, U], U32)
        share = sb("share", [P, 2, 2, U])
        Y2 = sb("Y2", [P, 2, 2, U, D])
        XH = sb("XH", [P, 2, 2, U, D])
        st = sb("stc", [P, U, 6])
        mv = sb("mvc", [P, U, 2])
        cf = sb("cfc", [P, 4, U])
        eps = sb("epsc", [P, 1])
        sg = Signals(nc, ctx, "index loaded0 loaded1 gathered0 gathered1 share sum clip stat var std coef norm out stored0 stored1 moved eps", "c_")
        rows = {n: dram[n].rearrange("(i t p) f -> i p t f", t=U, p=P) for n in ("x1", "h2")}
        od = out.rearrange("b (i t p) f -> (b i) p t f", t=U, p=P)
        block = ctx.enter_context(nc.Block())
        NP = NB // 2

        @block.sync
        def _(sp):
            def load(i, k, first=False):
                if not first:
                    sp.wait_ge(sg[f"stored{k}"].sem, i * 16)
                for x, n in enumerate(("x1", "h2")):
                    src = rows[n][2 * i + k] if isinstance(i, int) else rows[n][bass.ds(2 * i + k, 1)].squeeze(0)
                    sp.dma_start(XH[:, k, x], src).then_inc(sg[f"loaded{k}"].sem, 16)

            def store(i, k):
                sp.wait_ge(sg["out"].sem, (2 * i + k + 1) * U)
                dst = od[2 * i + k] if isinstance(i, int) else od[bass.ds(2 * i + k, 1)].squeeze(0)
                sp.dma_start(dst, XH[:, k, 0]).then_inc(sg[f"stored{k}"].sem, 16)

            load(0, 0, True)
            load(0, 1, True)
            with sp.Fori(0, NP - 1) as i:
                for k in range(2):
                    store(i, k)
                    load(i + 1, k)
            for k in range(2):
                store(NP - 1, k)
            for k in range(2):
                sp.wait_ge(sg[f"stored{k}"].sem, 16 * NP)

        @block.gpsimd
        def _(pool):
            def gather(i, k, first=False):
                b0 = (2 * i + k) * U
                if not first:
                    pool.wait_ge(sg["out"].sem, (2 * i + k - 1) * U)
                    pool.sem_inc(sg["moved"].sem, 1)
                for j in range(2):
                    src = slot[:, j, b0:b0 + U] if first else slot[:, j, bass.ds(b0, U)]
                    pool.tensor_copy(index[:, k, j, :], src).then_inc(sg["index"].sem, 1)
                pool.wait_ge(sg["index"].sem, 2 * (2 * i + k) + 2)
                pool.sem_inc(sg["moved"].sem, 1)
                for u in range(U):
                    for j in range(2):
                        pool.indirect_dma_start(out=Y2[:, k, j, u], out_offset=None, in_=dram["y"],
                                                in_offset=bass.IndirectOffsetOnAxis(ap=index[:, k, j, u:u + 1], axis=0))\
                            .then_inc(sg[f"gathered{k}"].sem, 16)
            gather(0, 0, True)
            gather(0, 1, True)
            with pool.Fori(1, NP) as i:
                for k in range(2):
                    gather(i, k)

        @block.scalar
        def _(act):
            act.wait_ge(sg["eps"].sem, 1)
            with act.Fori(0, NP) as i:
                for k in range(2):
                    n = 2 * i + k
                    act.wait_ge(sg["var"].sem, (n + 1) * U)
                    act.activation(cf[:, 0], mv[:, :, 1], ACT.Sqrt, bias=eps[:, :]).then_inc(sg["std"].sem, 1)
                    act.wait_ge(sg["coef"].sem, 2 * n + 2)
                    for u in range(U):
                        act.activation(XH[:, k, 1, u], XH[:, k, 1, u], ACT.Identity, bias=cf[:, 2, u:u + 1],
                                       scale=cf[:, 1, u:u + 1]).then_inc(sg["norm"].sem, 1)

        @block.vector
        def _(dve):
            dve.memset(eps[:, :], LN_EPS).then_inc(sg["eps"].sem, 1)
            with dve.Fori(0, NP) as i:
                for k in range(2):
                    n = 2 * i + k
                    h = XH[:, k, 1]
                    for j in range(2):
                        dve.tensor_copy(share[:, k, j, :], RT[:, bass.ds(n * U, U), 2 + j]).then_inc(sg["share"].sem, 1)
                    dve.wait_ge(sg["share"].sem, 2 * n + 2)
                    dve.wait_ge(sg[f"loaded{k}"].sem, (i + 1) * 32)
                    dve.wait_ge(sg[f"gathered{k}"].sem, (i + 1) * 32 * U)
                    for j in range(2):
                        for u in range(U):
                            if j:
                                dve.wait_ge(sg["sum"].sem, n * 2 * U + u + 1)
                            dve.scalar_tensor_tensor(out=h[:, u], in0=Y2[:, k, j, u], scalar=share[:, k, j, u:u + 1],
                                                     in1=h[:, u], op0=ALU.mult, op1=ALU.add).then_inc(sg["sum"].sem, 1)
                    dve.wait_ge(sg["sum"].sem, (n + 1) * 2 * U)
                    dve.tensor_scalar(h, h, 100.0, -100.0, ALU.min, ALU.max).then_inc(sg["clip"].sem, 1)
                    dve.wait_ge(sg["clip"].sem, n + 1)
                    for u in range(U):
                        dve.bn_stats(st[:, u], h[:, u]).then_inc(sg["stat"].sem, 1)
                    dve.wait_ge(sg["stat"].sem, (n + 1) * U)
                    dve.sem_inc(sg["moved"].sem, 1)
                    for u in range(U):
                        dve.bn_aggr(mv[:, u], st[:, u]).then_inc(sg["var"].sem, 1)
                    dve.wait_ge(sg["std"].sem, n + 1)
                    dve.reciprocal(cf[:, 1], cf[:, 0]).then_inc(sg["coef"].sem, 1)
                    dve.wait_ge(sg["coef"].sem, 2 * n + 1)
                    dve.scalar_tensor_tensor(out=cf[:, 2], in0=mv[:, :, 0], scalar=-1.0, in1=cf[:, 1], op0=ALU.mult,
                                             op1=ALU.mult).then_inc(sg["coef"].sem, 1)
                    for u in range(U):
                        dve.wait_ge(sg["norm"].sem, n * U + u + 1)
                        dve.tensor_tensor(XH[:, k, 0, u], XH[:, k, 0, u], h[:, u], ALU.add).then_inc(sg["out"].sem, 1)


_INS = ["L0_attn_x", "L0_attn_Wq", "L0_attn_Wk", "L0_attn_Wv", "L0_attn_lambda_params", "L0_attn_g1", "L0_attn_g2",
        "L0_attn_g3", "L0_attn_W1", "L0_attn_W2", "L0_ffn_ln1_w", "L0_ffn_ln2_w", "L0_ffn_Wq", "L0_ffn_Wk", "L0_ffn_Wv",
        "L0_ffn_Wo", "L0_ffn_Wr", "L0_ffn_Wg", "L0_ffn_Wu", "L0_ffn_Wd"]


def rope_table():
    inv = (1.0 / np.float32(THETA) ** (np.arange(0, HD, 2, dtype=np.float32) / np.float32(HD))).astype(np.float32)
    ang = (np.arange(S, dtype=np.float32)[:, None] * inv).astype(np.float32)
    c, s = np.cos(ang).astype(np.float32), np.sin(ang).astype(np.float32)
    return np.concatenate([c, c, -s, s], axis=1)


def build(nc, a, out):
    dram = {}
    for name, shape, dt in (("x1", [B * S, D], F32), ("h2", [B * S, D], F32), ("flat", [B * S, D], F32),
                            ("route", [B * S, 4], F32), ("y", [NSLOT_TILES * P, D], F32), ("qd", [3, D, S], BF16), ("kd", [3, KV, S], BF16)):
        dram[name] = nc.dram_tensor("scratch_" + name, shape, dt, kind="Internal").ap()
    attention_kernel(nc, a, dram)
    experts_kernel(nc, a, dram, out)


def kernel(**inputs):
    import concourse.bacc as bacc
    from concourse.bass_utils import run_bass_kernel_spmd

    nc = bacc.Bacc("TRN2", target_bir_lowering=False, num_devices=1)
    arrays = {"in_" + n: np.ascontiguousarray(inputs[n]) for n in _INS}
    arrays["in_rope"] = rope_table()
    a = {n[3:]: nc.dram_tensor(n, v.shape, mybir.dt.from_np(v.dtype), kind="ExternalInput").ap() for n, v in arrays.items()}
    out = nc.dram_tensor("out", (B, S, D), F32, kind="ExternalOutput").ap()
    build(nc, a, out)
    r = run_bass_kernel_spmd(nc, [arrays], core_ids=[0])
    return r.results[0]["out"]
```

```python
from contextlib import ExitStack

import numpy as np

import concourse.bass as bass
from concourse import mybir

F32 = mybir.dt.float32
BF16 = mybir.dt.bfloat16
U32 = mybir.dt.uint32
I32 = mybir.dt.int32
ALU = mybir.AluOpType
ACT = mybir.ActivationFunctionType
AX = mybir.AxisListType

P = 128
B, S, D = 8, 1024, 256
NT = S // P
FC = D // P
H, HD = 16, 16
HKV = 4
G = H // HKV
KV = HKV * HD
NQKV = D + 2 * KV
E, F = 8, 512
FK = F // P
TT = B * NT
UNROLL = 8
NSLOT_TILES = -(-(2 * TT + E - 1) // UNROLL) * UNROLL
CH = 4
POOL_HEADS = 3
LAST_HEADS = 12
LN_EPS = 1e-5
EPS1 = float(np.finfo(np.float32).eps)
LAMBDA_INIT = 0.8 - 0.6 * float(np.exp(-0.3 * 0))
SCALE1 = 1.0 / float(np.sqrt(D // 2))
SCALE2 = 0.25
THETA = 10000.0
MASKED = -1e30
Q_PART = [0, 0, 0, 1, 1, 2]
K_PART = [0, 1, 2, 0, 1, 0]
NSLOT = len(Q_PART)
MROW = NSLOT * HD
KROWS = MROW + 3


class Signal:

    def __init__(self, sem):
        self.sem = sem
        self.n = 0

    def by(self, instruction, k=1):
        instruction.then_inc(self.sem, k)
        self.n += k

    def settle(self, eng):
        eng.wait_ge(self.sem, self.n)


class Signals:
    def __init__(self, nc, ctx, names, prefix):
        self.all = []
        self.table = {}
        for name in names.split():
            s = Signal(ctx.enter_context(nc.semaphore(prefix + name)))
            self.table[name] = s
            self.all.append(s)

    def __getitem__(self, name):
        return self.table[name]


def attention_kernel(nc, a, dram):
    ctx = ExitStack()
    with ctx:
        def sb(name, shape, dt=F32):
            return ctx.enter_context(nc.sbuf_tensor(name, shape, dt))

        def ps(name, shape, dt=F32):
            return ctx.enter_context(nc.psum_tensor(name, shape, dt))

        w_raw = sb("w_raw", [P, 5, FC, D])
        wqkvT = sb("wqkvT", [P, FC, 3 * D])
        w1T = sb("w1T", [P, FC, D])
        w2T = sb("w2T", [P, FC, D])
        wqkv2 = sb("wqkv2", [P, FC, NQKV])
        wo = sb("wo", [P, FC, D])
        wr = sb("wr", [P, FC, E])
        g1c = sb("g1c", [P, FC])
        ln1c = sb("ln1c", [P, FC])
        g2row = sb("g2row", [P, D])
        g3row = sb("g3row", [P, D])
        ln2row = sb("ln2row", [P, D])
        lam = sb("lam", [P, 8])
        rope = sb("rope", [P, NT, 2 * HD])
        ident = sb("ident", [P, P])
        identb = sb("identb", [P, P], BF16)
        mask_qk = sb("mask_qk", [P, P], BF16)
        mask_kq = sb("mask_kq", [P, P], BF16)
        X = sb("X", [P, NT, D])
        AT = sb("AT", [P, NT, D])
        A2 = sb("A2", [P, NT, D])
        O1 = sb("O1", [P, NT, D])
        HS = sb("HS", [P, NT, D])
        XN = sb("XN", [P, 2, D])
        XT = sb("XT", [P, 2, FC, P])
        EX = sb("EX", [P, 2, 2 * D])
        QK = sb("QK", [P, 3, 2 * D])
        VS = sb("VS", [P, 2, D])
        KVS = sb("KVS", [P, 2, D])
        PP = sb("PP", [P, 2, POOL_HEADS * D])
        SQ = sb("SQ", [P, 2, D])
        work = sb("work", [P, 3 * H * D])
        P1 = [work[:, i * H * D:(i + 1) * H * D] for i in range(2)]
        P2 = work[:, 2 * H * D:3 * H * D]
        workb = work[:, :].bitcast(BF16)
        QST = workb[:, 0:H * S].rearrange("p (h s) -> p h s", h=H)
        QTS = workb[:, H * S:H * S + 3 * FC * S].rearrange("p (j c s) -> p j c s", j=3, c=FC)
        KST = sb("KST", [P, HKV, S], BF16)
        KTS = sb("KTS", [KV, 3, S], BF16)
        A2T = sb("A2T", [P, FC, CH * P])
        HT = sb("HT", [P, 2, FC, CH * P])
        Q2 = sb("Q2", [P, 2, D + KV])
        PT = sb("PT", [P, 2, 3, D + KV], BF16)
        V1 = sb("V1", [P, NT, HKV, 32])
        PR = sb("PR", [P, 8, 512])
        OT = sb("OT", [P, 512])
        RC = sb("RC", [P, 4, G])
        NM = sb("NM", [P, NT, G])
        NMR = sb("NMR", [P, NT, G])
        MT = sb("MT", [P, NT, 3, G], BF16)
        MR = sb("MR", [3 * G, S], BF16)
        RA = EX[:, :, 0:D + KV]
        RB = PP[:, :, 0:D + KV]
        CTX = O1
        H2 = A2
        FL = AT
        bst = sb("bst", [P, NT, 6])
        mv = sb("mv", [P, NT, 2])
        st = sb("st", [P, 12, NT])
        MS = sb("MS", [P, NT, H])
        R16 = sb("R16", [P, NT, H])
        LG = sb("LG", [P, NT, E])
        top = sb("top", [P, NT, 8])
        topi = sb("topi", [P, NT, 8], U32)
        ROUTE = sb("ROUTE", [P, NT, 4])
        tw = sb("tw", [P, 4, NT])

        MX = ps("MX", [P, 2, 2, 512])
        SP_ = ps("SP_", [P, 2, 512])
        MXB = MX[:, :, :, :].rearrange("p a b n -> p (a b n)")
        OA = ps("OA", [P, 512])
        OB = ps("OB", [P, 512])

        names = (
            "stats coef u1 u3 xn tp xT qkv expo vcopy e1 qk prod1 kv kvs prod2 share2 attn last_products "
            "last_sum last_attn ag sq ms m16 rt16 r16 an ssq m1 rtrow rrow gain a2 "
            "tpb a2T hid hidT out1 o1 y1 x1 stats2 uB uC coefB coefC rt2 "
            "hs tph hT qkv2 q2 v2 rope part0 part1 part2 tpq qts kts half0 half1 stack0 stack1 "
            "mx nm mt mrow0 mrow1 s exp pv ot otp ctx "
            "tpc cT wo h2 ss2 fl tpf fT lg lgs topk stored dve_step act_step phase "
        )
        sg = Signals(nc, ctx, names, "s_")
        setup = Signals(nc, ctx, "wload tpw wT pool dve act lam done stats u root coef", "i_")
        x_loaded = ctx.enter_context(nc.semaphore("x_loaded"))
        arrive = ctx.enter_context(nc.semaphore("batch_arrive"))
        go = {n: ctx.enter_context(nc.semaphore("batch_go_" + n)) for n in ("act", "dve", "pe", "pool")}

        xb = a["L0_attn_x"].rearrange("b (t p) f -> b p t f", p=P)
        qd, kd = dram["qd"], dram["kd"]
        x1d, h2d, fld, routed = (dram[n].rearrange("(b t p) f -> b p t f", b=B, p=P) for n in ("x1", "h2", "flat", "route"))
        NWLOAD = 5 + 3 + 1 + 1 + 2 + 3 + 1 + 1

        NCH = S // 512
        UNITS = [(g, c) for g in range(HKV) for c in range(NCH)]
        FIRST_STEP = [sum(CH * (c + 1) for _, c in UNITS[:u]) for u in range(len(UNITS) + 1)]
        ROWS_LATER = 0.4

        def OAB(t):
            return (OA, OB)[t % 2][:, :]

        def q_product(eng, dst, u, h0, h1):
            shape = [P, h1 - h0, HD, HD]
            return eng.tensor_tensor(
                dst.rearrange("p (h e d) -> p h e d", e=HD, d=HD),
                QK[:, u % 3, h0 * HD:h1 * HD].rearrange("p (h e) -> p h e", e=HD).unsqueeze(3).broadcast_to(shape),
                KVS[:, u % 2].rearrange("p (e d) -> p e d", d=HD).unsqueeze(1).broadcast_to(shape), ALU.mult)

        def chunk(c):
            return range(CH * c, CH * (c + 1))

        def chunk_slice(c):
            return slice(CH * c, CH * (c + 1))

        def steps():
            for u, (g, c) in enumerate(UNITS):
                for kt in range(CH * (c + 1)):
                    yield u, kt

        def max_plan():
            def pieces(u):
                c = UNITS[u][1]
                return [("piece", u, h, qt) for h in range(G) for qt in range(CH * c, CH * (c + 1))]

            timed = []
            for u, (g, c) in enumerate(UNITS):
                if u == 0:
                    continue
                if u == 1:
                    s0, s1 = -0.5, 2
                else:
                    s1 = FIRST_STEP[u] - (3.5, 3)[c]
                    s0 = max(2, s1 - 12)
                actions = pieces(u)
                timed.extend((s0 + i * (s1 - s0) / len(actions), action) for i, action in enumerate(actions))
                timed.append((s1 - 0.01, ("parts", u)))
                timed.append((s1 + ROWS_LATER, ("rows", u)))
            timed.sort(key=lambda x: x[0])
            plan = [pieces(0) + [("parts", 0), ("rows", 0)]] + [[] for _ in range(FIRST_STEP[-1])]
            for time, action in timed:
                plan[max(0, 1 + int(time // 1))].append(action)
            bank, users, index = 0, {}, 0
            placed = []
            for actions in plan:
                placed.append([])
                for kind, *args in actions:
                    if kind == "parts":
                        placed[-1].append((kind, *args, None))
                        continue
                    width = 2 if kind == "piece" and args[-1] >= CH else 1
                    if bank + width > 4:
                        bank = 0
                    taken = range(bank, bank + width)
                    before = max(users.get(x, 0) for x in taken)
                    for x in taken:
                        users[x] = index + 1
                    placed[-1].append((kind, *args, (bank, before)))
                    bank = (bank + width) % 4
                    index += 1
            return placed

        def dve_plan():
            plan = max_plan()
            yield from plan[0]
            for k, (u, kt) in enumerate(steps()):
                actions = plan[k + 1]
                first = len(actions) // G
                yield from actions[:first]
                if kt == 0 and u >= 1:
                    yield "out", u - 1
                yield from actions[first:]
                if kt == 1 and u >= 1:
                    yield "ctx", u - 1
            yield "out", len(UNITS) - 1
            yield "ctx", len(UNITS) - 1

        block = ctx.enter_context(nc.Block())

        def end_phase(eng, k):
            eng.sem_inc(sg["phase"].sem, 1)
            eng.wait_ge(sg["phase"].sem, 4 * k)

        def end_batch(eng, own):
            eng.sem_inc(arrive, 1)
            eng.wait_ge(go[own], 1)
            eng.sem_clear(go[own])

        @block.sync
        def _(sp):
            w = setup["wload"]
            for i, n in enumerate(("Wq", "Wk", "Wv", "W1", "W2")):
                w.by(sp.dma_start(w_raw[:, i], a["L0_attn_" + n].rearrange("(c p) n -> p c n", p=P)), 16)
            for i, (n, c0, c1) in enumerate((("Wq", 0, D), ("Wk", D, D + KV), ("Wv", D + KV, NQKV))):
                w.by(sp.dma_start(wqkv2[:, :, c0:c1], a["L0_ffn_" + n].rearrange("(c p) n -> p c n", p=P)), 16)
            w.by(sp.dma_start(wo[:, :, :], a["L0_ffn_Wo"].rearrange("(c p) n -> p c n", p=P)), 16)
            w.by(sp.dma_start(wr[:, :, :], a["L0_ffn_Wr"].rearrange("(c p) n -> p c n", p=P)), 16)
            w.by(sp.dma_start(g1c[:, :], a["L0_attn_g1"].rearrange("(c p) -> p c", p=P), allow_slow_non_contiguous=True), 16)
            w.by(sp.dma_start(ln1c[:, :], a["L0_ffn_ln1_w"].rearrange("(c p) -> p c", p=P), allow_slow_non_contiguous=True), 16)
            w.by(sp.dma_start(g2row[:, 0:HD], a["L0_attn_g2"].partition_broadcast(P)), 16)
            w.by(sp.dma_start(g3row[:, :], a["L0_attn_g3"].partition_broadcast(P)), 16)
            w.by(sp.dma_start(ln2row[:, :], a["L0_ffn_ln2_w"].partition_broadcast(P)), 16)
            w.by(sp.dma_start(lam[:, 0:4], a["L0_attn_lambda_params"].partition_broadcast(P)), 16)
            w.by(sp.dma_start(rope[:, :, :], a["rope"].rearrange("(t p) n -> p t n", p=P)), 16)
            assert w.n == 16 * NWLOAD

            sp.dma_start(X[:, :, :], xb[0]).then_inc(x_loaded, 16)

            def batch(b, prefetch):
                for c in range(NCH):
                    half, stack = sg["half%d" % c], sg["stack%d" % c]
                    cols = slice(512 * c, 512 * (c + 1))
                    sp.wait_ge(sg["kts"].sem, CH * (c + 1))
                    half.by(sp.dma_start(kd.rearrange("j r s -> r j s")[:, :, cols], KTS[:, :, cols]), 16)
                    sp.wait_ge(sg["qts"].sem, CH * (c + 1))
                    for j in range(3):
                        half.by(sp.dma_start(qd[j].rearrange("(c r) s -> r c s", c=FC)[:, :, cols], QTS[:, j, :, cols]), 16)
                    half.settle(sp)
                    for i in range(NSLOT):
                        stack.by(sp.dma_start(KST[HD * i:HD * (i + 1), :, cols],
                                              kd[K_PART[i]].rearrange("(h e) s -> e h s", e=HD)[:, :, cols]), 16)
                        stack.by(sp.dma_start(QST[HD * i:HD * (i + 1), :, cols],
                                              qd[Q_PART[i]].rearrange("(h e) s -> e h s", e=HD)[:, :, cols]), 16)
                st_ = sg["stored"]
                sp.wait_ge(sg["x1"].sem, NT)
                st_.by(sp.dma_start(x1d[bass.ds(b, 1)].squeeze(0), X[:, :, :]), 16)
                if prefetch:
                    sp.wait_ge(sg["hs"].sem, NT)
                    st_.settle(sp)
                    sp.dma_start(X[:, :, :], xb[bass.ds(b + 1, 1)].squeeze(0)).then_inc(x_loaded, 16)
                else:
                    sp.sem_inc(x_loaded, 16)
                for u, (g, c) in enumerate(UNITS):
                    sp.wait_ge(sg["mt"].sem, u + 1)
                    for j in range(3):
                        sg["mrow%d" % (u % 2)].by(sp.dma_start(QST[MROW + j:MROW + j + 1, G * g:G * (g + 1), 512 * c:512 * (c + 1)],
                                                   MR[G * j:G * (j + 1), 512 * (u % 2):512 * (u % 2 + 1)]), 16)
                sp.wait_ge(sg["h2"].sem, NT)
                st_.by(sp.dma_start(h2d[bass.ds(b, 1)].squeeze(0), H2[:, :, :]), 16)
                sp.wait_ge(sg["fl"].sem, NT)
                st_.by(sp.dma_start(fld[bass.ds(b, 1)].squeeze(0), FL[:, :, :]), 16)
                sp.wait_ge(sg["topk"].sem, 1)
                st_.by(sp.dma_start(routed[bass.ds(b, 1)].squeeze(0), ROUTE[:, :, :]), 16)
                st_.settle(sp)
                sp.wait_ge(arrive, len(go))
                for s in (arrive, *(x.sem for x in sg.all)):
                    sp.sem_clear(s)
                for s in go.values():
                    sp.sem_inc(s, 1)

            with sp.Fori(0, B - 1) as b:
                batch(b, True)
            for signal in sg.all:
                signal.n = 0
            batch(B - 1, False)

        @block.gpsimd
        def _(pool):
            ps_ = setup["pool"]
            ps_.by(pool.memset(ident[:, :], 0.0))
            ps_.by(pool.memset(identb[:, :], 0.0))
            ps_.by(pool.memset(mask_qk[:, :], 0.0))
            ps_.by(pool.memset(mask_kq[:, :], 0.0))
            ps_.by(pool.memset(V1[:, :, :, HD:32], 0.0))
            ps_.settle(pool)
            ps_.by(pool.memset(KST[MROW:P, :, :], 1.0))
            ps_.settle(pool)
            for m in (ident, identb):
                ps_.by(pool.affine_select(out=m[:, :], in_=m[:, :], compare_op=ALU.not_equal, fill=1.0, base=0,
                                          pattern=[[-1, P]], channel_multiplier=1))
            ps_.by(pool.affine_select(out=mask_qk[:, :], in_=mask_qk[:, :], compare_op=ALU.is_ge, fill=MASKED,
                                      base=0, pattern=[[-1, P]], channel_multiplier=1))
            ps_.by(pool.affine_select(out=mask_kq[:, :], in_=mask_kq[:, :], compare_op=ALU.is_ge, fill=MASKED,
                                      base=0, pattern=[[1, P]], channel_multiplier=-1))
            ps_.by(pool.memset(V1[:, :, :, HD:HD + 1], 1.0))
            ps_.settle(pool)
            pool.wait_ge(setup["done"].sem, 1)

            with pool.Fori(0, B) as b:
                def q_share(u):
                    pool.wait_ge(sg["kvs"].sem, 2 * u + 2)
                    if u >= 2:
                        pool.wait_ge(sg["attn"].sem, 2 * (u - 1))
                    sg["share2"].by(q_product(pool, PP[:, u % 2], u, H - POOL_HEADS, H))

                def last_products():
                    u = NT - 1
                    pool.wait_ge(sg["kvs"].sem, 2 * u + 2)
                    pool.wait_ge(sg["kv"].sem, NT - 1)
                    for e in (slice(0, HD // 2), slice(HD // 2, HD)):
                        shape = [P, LAST_HEADS, HD // 2, HD]
                        sg["last_products"].by(pool.tensor_tensor(
                            P1[NT % 2][:, 0:LAST_HEADS * D].rearrange("p (h e d) -> p h e d", e=HD, d=HD)[:, :, e],
                            QK[:, u % 3, (H - LAST_HEADS) * HD:D].rearrange("p (h e) -> p h e", e=HD)[:, :, e].unsqueeze(3)
                            .broadcast_to(shape),
                            KVS[:, u % 2].rearrange("p (e d) -> p e d", d=HD)[:, e].unsqueeze(1).broadcast_to(shape),
                            ALU.mult))

                def gain2(u):
                    if u < NT - 1:
                        pool.wait_ge(sg["attn"].sem, 2 * u + 2)
                    else:
                        pool.wait_ge(sg["attn"].sem, 2 * u + 1)
                        pool.wait_ge(sg["last_attn"].sem, 1)
                    sg["ag"].by(pool.tensor_tensor(A2[:, u], AT[:, u], g2row[:, :], ALU.mult))

                for t in range(NT + 3):
                    if t < NT:
                        pool.wait_ge(sg["qk"].sem, t + 1)
                        pool.wait_ge(sg["vcopy"].sem, t + 1)
                        if t >= 2:
                            pool.wait_ge(sg["kv"].sem, t - 1)
                        hh = H // 2
                        for i in range(2):
                            r = slice(i * hh * HD, (i + 1) * hh * HD)
                            sg["prod1"].by(pool.tensor_tensor(
                                P1[t % 2][:, i * hh * D:(i + 1) * hh * D].rearrange("p (h e d) -> p h e d", h=hh, e=HD),
                                QK[:, t % 3, D:2 * D][:, r].rearrange("p (h e) -> p h e", e=HD).unsqueeze(3)
                                .broadcast_to([P, hh, HD, HD]),
                                VS[:, t % 2, r].rearrange("p (h d) -> p h d", d=HD).unsqueeze(2)
                                .broadcast_to([P, hh, HD, HD]), ALU.mult))
                    if 1 <= t < NT:
                        q_share(t - 1)
                    if t == NT:
                        last_products()
                    if t >= 3:
                        gain2(t - 3)
                sg["ag"].settle(pool)
                for t in range(NT):
                    pool.wait_ge(sg["q2"].sem, t + 1)
                    q = Q2[:, t % 2].rearrange("p (h a e) -> p h a e", a=2, e=HD // 2)
                    ra = RA[:, t % 2].rearrange("p (h a e) -> p h a e", a=2, e=HD // 2)
                    rb = RB[:, t % 2].rearrange("p (h a e) -> p h a e", a=2, e=HD // 2)
                    nh = (D + KV) // HD
                    sh = [P, nh, HD // 2]

                    def table(c0):
                        return rope[:, t, c0:c0 + HD // 2].unsqueeze(1).broadcast_to(sh)
                    if t >= 2:
                        pool.wait_ge(sg["part1"].sem, 2 * (t - 1))
                    for half in range(2):
                        sg["rope"].by(pool.tensor_tensor(ra[:, :, half], q[:, :, half], table(0), ALU.mult))
                        sg["rope"].by(pool.tensor_tensor(rb[:, :, half], q[:, :, 1 - half], table(HD + 8 * half), ALU.mult))
                sg["rope"].settle(pool)
                end_phase(pool, 1)
                end_phase(pool, 2)
                end_batch(pool, "pool")

        @block.scalar
        def _(act):
            act.wait_ge(setup["wload"].sem, 16 * NWLOAD)
            act.wait_ge(setup["dve"].sem, 2)
            setup["act"].by(act.activation(lam[:, 6:8], lam[:, 4:6], ACT.Exp))

            act.wait_ge(setup["u"].sem, 2)
            setup["root"].by(act.activation(st[:, 9, :], st[:, 9, :], ACT.Sqrt))
            act.wait_ge(setup["coef"].sem, 2)

            with act.Fori(0, B) as b:
                def normalized(t):
                    if t >= 2:
                        act.wait_ge(sg["tp"].sem, t - 1)
                    sg["xn"].by(act.activation(XN[:, t % 2], X[:, t], ACT.Identity, bias=st[:, 11, t:t + 1],
                                               scale=st[:, 10, t:t + 1]))

                def transposed(t):
                    act.wait_ge(sg["tp"].sem, t + 1)
                    if t >= 2:
                        act.wait_ge(sg["qkv"].sem, t - 1)
                    sg["xT"].by(act.activation(XT[:, t % 2].rearrange("p c s -> p (c s)"), SP_[:, t % 2, 0:D], ACT.Copy))

                def kv_sums(u):
                    act.wait_ge(sg["kv"].sem, u + 1)
                    if u >= 2:
                        act.wait_ge(sg["prod2"].sem, u - 1)
                        act.wait_ge(sg["share2"].sem, u - 1)
                    sg["kvs"].by(act.activation(KVS[:, u % 2, 0:D // 2], OAB(u)[:, 0:D // 2], ACT.Copy, scale=SCALE1))
                    sg["kvs"].by(act.activation(KVS[:, u % 2, D // 2:D], OAB(u)[:, D // 2:D], ACT.Copy,
                                                scale=lam[:, 0:1]))

                def squares(u):
                    if u < NT - 1:
                        act.wait_ge(sg["attn"].sem, 2 * u + 2)
                    else:
                        act.wait_ge(sg["last_sum"].sem, 1)
                        sg["last_attn"].by(act.activation(AT[:, u, D - LAST_HEADS * HD:D], OA[:, 0:LAST_HEADS * HD], ACT.Copy))
                        act.wait_ge(sg["attn"].sem, 2 * u + 1)
                        sg["last_attn"].settle(act)
                    if u >= 2:
                        act.wait_ge(sg["ms"].sem, u - 1)
                    sg["sq"].by(act.activation(SQ[:, u % 2], AT[:, u], ACT.Square))

                def root(done, x, ready, k):
                    act.wait_ge(ready.sem, k)
                    done.by(act.activation(x, x, ACT.Sqrt))

                def squared_rows(c):
                    for t in chunk(c):
                        act.wait_ge(sg["an"].sem, t + 1)
                        if t >= 2:
                            sg["ssq"].settle(act)
                        sg["ssq"].by(act.activation(EX[:, t % 2, 0:D], AT[:, t], ACT.Square, accum_out=st[:, 5, t:t + 1]))

                def gains(c):
                    act.wait_ge(sg["rrow"].sem, c + 1)
                    for t in chunk(c):
                        sg["gain"].by(act.activation(A2[:, t], g3row[:, :], ACT.Copy, bias=1.0, scale=st[:, 6, t:t + 1]))

                def attention_turned(c):
                    for t in chunk(c):
                        act.wait_ge(sg["tpb"].sem, t + 1)
                        if t == CH * c and c >= 1:
                            act.wait_ge(sg["hid"].sem, c)
                        sg["a2T"].by(act.activation(A2T[:, :, (t % CH) * P:(t % CH + 1) * P],
                                                    SP_[:, t % 2, 0:D].rearrange("p (c s) -> p c s", c=FC), ACT.Copy))

                def hidden(c):
                    act.wait_ge(sg["hid"].sem, c + 1)
                    for fo in range(FC):
                        sg["hidT"].by(act.activation(HT[:, c, fo, :], MX[:, 0, fo, :], ACT.Gelu))

                def layer_normed(c):
                    act.wait_ge(sg["coefB"].sem, c + 1)
                    for t in chunk(c):
                        sg["y1"].by(act.activation(O1[:, t], O1[:, t], ACT.Identity, bias=st[:, 4, t:t + 1],
                                                   scale=st[:, 3, t:t + 1]))

                normalized(0)
                normalized(1)
                transposed(0)
                for t in range(NT + 3):
                    if t < NT:
                        act.wait_ge(sg["qkv"].sem, t + 1)
                        if t >= 2:
                            act.wait_ge(sg["qk"].sem, t - 1)
                            act.wait_ge(sg["prod1"].sem, 2 * (t - 1))
                        sg["expo"].by(act.activation(EX[:, t % 2], MX[:, t % 2, 0, :], ACT.Exp))
                        sg["vcopy"].by(act.activation(VS[:, t % 2], MX[:, t % 2, 1, 0:D], ACT.Copy))
                        sg["expo"].settle(act)
                        sg["e1"].by(act.activation(EX[:, t % 2], EX[:, t % 2], ACT.Relu, scale=-1.0, bias=1.0))
                    if t + 1 < NT:
                        transposed(t + 1)
                    if t + 2 < NT:
                        normalized(t + 2)
                    if 1 <= t <= NT:
                        kv_sums(t - 1)
                    if t == NT:
                        root(sg["rt16"], R16[:, chunk_slice(0)], sg["m16"], 1)
                    if t == NT + 1:
                        squared_rows(0)
                    if t >= 3:
                        squares(t - 3)
                    if t == NT + 1:
                        root(sg["rtrow"], st[:, 5, chunk_slice(0)], sg["m1"], 1)
                        gains(0)
                root(sg["rt16"], R16[:, chunk_slice(1)], sg["m16"], 2)
                attention_turned(0)
                squared_rows(1)
                root(sg["rtrow"], st[:, 5, chunk_slice(1)], sg["m1"], 2)
                gains(1)
                hidden(0)
                attention_turned(1)
                root(sg["rt2"], st[:, 0, chunk_slice(0)], sg["uB"], 1)
                layer_normed(0)
                hidden(1)
                root(sg["rt2"], st[:, 0:2, chunk_slice(0)], sg["uC"], 1)
                def normed(t):
                    act.wait_ge(sg["coefC"].sem, t // CH + 1)
                    sg["hs"].by(act.activation(HS[:, t], X[:, t], ACT.Identity, bias=st[:, 4, t:t + 1],
                                               scale=st[:, 3, t:t + 1]))

                def turned(t):
                    act.wait_ge(sg["tph"].sem, t + 1)
                    if t >= 2:
                        act.wait_ge(sg["qkv2"].sem, t - 1)
                    sg["hT"].by(act.activation(XT[:, t % 2].rearrange("p c s -> p (c s)"), SP_[:, t % 2, 0:D], ACT.Copy))

                normed(0)
                normed(1)
                normed(2)
                turned(0)
                root(sg["rt2"], st[:, 0, chunk_slice(1)], sg["uB"], 2)
                layer_normed(1)
                for t in range(NT + 2):
                    if t + 1 < NT:
                        turned(t + 1)
                    if t == 0:
                        root(sg["rt2"], st[:, 0:2, chunk_slice(1)], sg["uC"], 2)
                    if t < NT:
                        act.wait_ge(sg["qkv2"].sem, t + 1)
                        if t >= 2:
                            act.wait_ge(sg["part2"].sem, t - 1)
                        sg["q2"].by(act.activation(Q2[:, t % 2], MX[:, 0, t % 2, 0:D + KV], ACT.Copy,
                                                   scale=st[:, 2, t:t + 1]))
                        sg["v2"].by(act.activation(V1[:, t, :, 0:HD],
                                                   MX[:, 0, t % 2, D + KV:NQKV].rearrange("p (g e) -> p g e", g=HKV),
                                                   ACT.Copy, scale=st[:, 2, t:t + 1]))
                    if t + 3 < NT:
                        normed(t + 3)
                    if t >= 2:
                        u = t - 2
                        act.wait_ge(sg["tpq"].sem, 2 * u + 2)
                        sg["kts"].by(act.activation(
                            KTS[:, :, u * P:(u + 1) * P],
                            OAB(u).bitcast(BF16)[0:KV, 0:3 * P].rearrange("p (j s) -> p j s", j=3), ACT.Copy))
                        sg["qts"].by(act.activation(
                            QTS[:, :, :, u * P:(u + 1) * P],
                            MX[:, 1, u % 2, :].bitcast(BF16)[:, 0:3 * FC * P].rearrange("p (j c s) -> p j c s", j=3, c=FC),
                            ACT.Copy))
                sg["qts"].settle(act)
                sg["v2"].settle(act)
                end_phase(act, 1)
                n = 0
                for u, kt in steps():
                    c = UNITS[u][1]
                    q0 = max(0, kt - CH * c) * P
                    for h in range(G):
                        act.wait_ge(sg["s"].sem, n + 1)
                        if n >= 8:
                            act.wait_ge(sg["pv"].sem, (n - 8) // G + 1)
                        sg["exp"].by(act.activation(PR[:, n % 8, q0:512], SP_[:, n % 2, q0:512], ACT.Exp))
                        n += 1
                sg["exp"].settle(act)
                end_phase(act, 2)
                def squares2(u):
                    act.wait_ge(sg["h2"].sem, u + 1)
                    if u >= 2:
                        sg["ss2"].settle(act)
                    sg["ss2"].by(act.activation(SQ[:, u % 2], H2[:, u], ACT.Square, accum_out=st[:, 7, u:u + 1]))

                for t in range(NT):
                    act.wait_ge(sg["tpc"].sem, t + 1)
                    if t >= 2:
                        act.wait_ge(sg["wo"].sem, t - 1)
                    sg["cT"].by(act.activation(XT[:, t % 2].rearrange("p c s -> p (c s)"), SP_[:, t % 2, 0:D], ACT.Copy))
                    if t >= 2:
                        squares2(t - 2)
                    if t == CH + 2:
                        root(sg["rt2"], st[:, 8, chunk_slice(0)], sg["u3"], 1)
                squares2(NT - 2)
                squares2(NT - 1)
                root(sg["rt2"], st[:, 8, chunk_slice(1)], sg["u3"], 2)
                for t in range(NT):
                    act.wait_ge(sg["tpf"].sem, t + 1)
                    if t >= 2:
                        act.wait_ge(sg["lg"].sem, t - 1)
                    sg["fT"].by(act.activation(XN[:, t % 2], SP_[:, t % 2, 0:D], ACT.Copy))
                root(sg["rt2"], st[:, 9, :], sg["u1"], 2)
                act.wait_ge(sg["lgs"].sem, 1)
                sg["act_step"].by(act.activation(tw[:, 1, :], tw[:, 0, :], ACT.Exp))
                sg["act_step"].settle(act)
                end_batch(act, "act")

        @block.vector
        def _(dve):
            dve.wait_ge(setup["wload"].sem, 16 * NWLOAD)
            sd = setup["dve"]
            sd.by(dve.tensor_tensor(lam[:, 4:5], lam[:, 0:1], lam[:, 1:2], ALU.mult))
            sd.by(dve.tensor_tensor(lam[:, 5:6], lam[:, 2:3], lam[:, 3:4], ALU.mult))
            for n in (HD, 2 * HD, 4 * HD, 8 * HD):
                sd.settle(dve)
                sd.by(dve.tensor_copy(g2row[:, n:2 * n], g2row[:, 0:n]))
            sd.settle(dve)
            sd.by(dve.tensor_scalar(g2row[:, :], g2row[:, :], 1.0 - LAMBDA_INIT, None, ALU.mult))
            dve.wait_ge(setup["act"].sem, 1)
            sd.by(dve.tensor_tensor(lam[:, 0:1], lam[:, 6:7], lam[:, 7:8], ALU.subtract))
            sd.settle(dve)
            sd.by(dve.tensor_scalar(lam[:, 0:1], lam[:, 0:1], LAMBDA_INIT, -SCALE1, ALU.add, ALU.mult))
            sd.settle(dve)
            for c in range(FC):
                sd.by(dve.tensor_scalar(wqkv2[:, c, 0:D], wqkv2[:, c, 0:D], ln1c[:, c:c + 1], SCALE2, ALU.mult, ALU.mult))
                sd.by(dve.tensor_scalar(wqkv2[:, c, D:NQKV], wqkv2[:, c, D:NQKV], ln1c[:, c:c + 1], None, ALU.mult))
            for i in range(5):
                dve.wait_ge(setup["tpw"].sem, i + 1)
                src = SP_[:, i % 2, :].rearrange("p (c n) -> p c n", c=FC)
                if i < 3:
                    for c in range(FC):
                        setup["wT"].by(dve.tensor_scalar(wqkvT[:, c, i * D:(i + 1) * D], src[:, c], g1c[:, c:c + 1],
                                                         None, ALU.mult))
                else:
                    dst = (w1T, w2T)[i - 3]
                    for c in range(FC):
                        setup["wT"].by(dve.tensor_copy(dst[:, c], src[:, c]))
            setup["wT"].settle(dve)
            sd.settle(dve)
            dve.sem_inc(setup["done"].sem, 1)
            dve.wait_ge(setup["pool"].sem, 11)

            ds = sg["dve_step"]

            def stats(t, src, done):
                done.by(dve.bn_stats(bst[:, t], src))

            def aggregate(done, tiles=range(NT)):
                done.settle(dve)
                for t in tiles:
                    done.by(dve.bn_aggr(mv[:, t], bst[:, t]))

            def x_coefficients(stat, u, rooted, k, done):
                dve.wait_ge(x_loaded, 16)
                dve.sem_clear(x_loaded)
                for t in range(NT):
                    stats(t, X[:, t], stat)
                aggregate(stat)
                stat.settle(dve)
                u.by(dve.tensor_scalar(st[:, 9, :], mv[:, :, 1], LN_EPS, EPS1, ALU.add, ALU.mult))
                u.settle(dve)
                u.by(dve.tensor_tensor(st[:, 9, :], st[:, 9, :], mv[:, :, 1], ALU.add))
                dve.wait_ge(rooted.sem, k)
                done.by(dve.reciprocal(st[:, 10, :], st[:, 9, :]))
                done.settle(dve)
                done.by(dve.scalar_tensor_tensor(out=st[:, 11, :], in0=mv[:, :, 0], scalar=-1.0, in1=st[:, 10, :],
                                                 op0=ALU.mult, op1=ALU.mult))
                done.settle(dve)

            x_coefficients(setup["stats"], setup["u"], setup["root"], 1, setup["coef"])

            with dve.Fori(0, B) as b:
                def elu(u):
                    dve.wait_ge(sg["e1"].sem, u + 1)
                    if u >= 3:
                        dve.wait_ge(sg["prod1"].sem, 2 * (u - 2))
                        dve.wait_ge(sg["share2"].sem, u - 2)
                    sg["qk"].by(dve.scalar_tensor_tensor(out=QK[:, u % 3], in0=MX[:, u % 2, 0, :], scalar=0.0,
                                                         in1=EX[:, u % 2], op0=ALU.max, op1=ALU.subtract))

                def scale_head_squares(c):
                    sg["ms"].settle(dve)
                    sg["m16"].by(dve.tensor_scalar(R16[:, chunk_slice(c)], MS[:, chunk_slice(c)], 1.0 / HD, EPS1, ALU.mult,
                                                   ALU.add))

                def norm_heads(c):
                    dve.wait_ge(sg["rt16"].sem, c + 1)
                    sg["r16"].by(dve.reciprocal(R16[:, chunk_slice(c)], R16[:, chunk_slice(c)]))
                    sg["r16"].settle(dve)
                    dve.wait_ge(sg["ag"].sem, CH * (c + 1))
                    for t in chunk(c):
                        sg["an"].by(dve.tensor_tensor(AT[:, t].rearrange("p (h d) -> p h d", d=HD),
                                                      A2[:, t].rearrange("p (h d) -> p h d", d=HD),
                                                      R16[:, t, :].unsqueeze(2).broadcast_to([P, H, HD]), ALU.mult))

                def scale_row_squares(c):
                    dve.wait_ge(sg["ssq"].sem, CH * (c + 1))
                    x = st[:, 5, chunk_slice(c)]
                    sg["m1"].by(dve.tensor_scalar(x, x, 1.0 / D, EPS1, ALU.mult, ALU.add))

                def invert_rows(c):
                    dve.wait_ge(sg["rtrow"].sem, c + 1)
                    sg["rrow"].by(dve.reciprocal(st[:, 6, chunk_slice(c)], st[:, 5, chunk_slice(c)]))

                def add_gains(c):
                    for t in chunk(c):
                        dve.wait_ge(sg["gain"].sem, t + 1)
                        sg["a2"].by(dve.tensor_tensor(A2[:, t], A2[:, t], AT[:, t], ALU.mult))

                def attended_last():
                    u, n = NT - 1, H - LAST_HEADS
                    dve.wait_ge(sg["kvs"].sem, 2 * u + 2)
                    sg["attn"].settle(dve)
                    sg["prod2"].by(q_product(dve, P2[:, 0:n * D], u, 0, n))
                    sg["prod2"].settle(dve)
                    sg["attn"].by(dve.tensor_reduce(AT[:, u, 0:n * HD].rearrange("p (h d) -> p h d", d=HD),
                                                    P2[:, 0:n * D].rearrange("p (h e d) -> p h d e", e=HD, d=HD),
                                                    AX.X, ALU.add))

                def attended(u):
                    dve.wait_ge(sg["kvs"].sem, 2 * u + 2)
                    if u >= 1:
                        sg["attn"].settle(dve)
                    sg["prod2"].by(q_product(dve, P2[:, 0:(H - POOL_HEADS) * D], u, 0, H - POOL_HEADS))
                    dve.wait_ge(sg["share2"].sem, u + 1)
                    c0 = (H - POOL_HEADS) * HD
                    sg["attn"].by(dve.tensor_reduce(AT[:, u, c0:D].rearrange("p (h d) -> p h d", d=HD),
                                                    PP[:, u % 2].rearrange("p (h e d) -> p h d e", e=HD, d=HD), AX.X, ALU.add))
                    sg["prod2"].settle(dve)
                    sg["attn"].by(dve.tensor_reduce(AT[:, u, 0:c0].rearrange("p (h d) -> p h d", d=HD),
                                                    P2[:, 0:(H - POOL_HEADS) * D].rearrange("p (h e d) -> p h d e", e=HD, d=HD),
                                                    AX.X, ALU.add))

                for t in range(NT + 3):
                    if t < NT:
                        elu(t)
                    if t == NT + 1:
                        attended_last()
                    if 2 <= t <= NT:
                        attended(t - 2)
                    if t >= 3:
                        u = t - 3
                        dve.wait_ge(sg["sq"].sem, u + 1)
                        sg["ms"].by(dve.tensor_reduce(MS[:, u], SQ[:, u % 2].rearrange("p (h d) -> p h d", d=HD), AX.X, ALU.add))
                    if t == NT - 1:
                        scale_head_squares(0)
                    if t == NT:
                        norm_heads(0)
                    if t == NT + 1:
                        scale_row_squares(0)
                        invert_rows(0)
                        add_gains(0)
                scale_head_squares(1)
                norm_heads(1)
                scale_row_squares(1)
                invert_rows(1)
                add_gains(1)

                def add_attention(c):
                    for t in chunk(c):
                        dve.wait_ge(sg["out1"].sem, t + 1)
                        sg["o1"].by(dve.tensor_tensor(O1[:, t], OAB(t)[:, 0:D], A2[:, t], ALU.add))
                        sg["o1"].settle(dve)
                        stats(t, O1[:, t], sg["stats2"])
                    aggregate(sg["stats2"], chunk(c))
                    sg["stats2"].settle(dve)
                    sg["uB"].by(dve.tensor_scalar(st[:, 0, chunk_slice(c)], mv[:, chunk_slice(c), 1], LN_EPS, None, ALU.add))

                def layer_norm_coefficients(c, root_of, done, second):
                    x = chunk_slice(c)
                    dve.wait_ge(sg["rt2"].sem, root_of)
                    ds.by(dve.reciprocal(st[:, 3, x], st[:, 0, x]))
                    if second:
                        ds.by(dve.reciprocal(st[:, 2, x], st[:, 1, x]))
                    ds.settle(dve)
                    if second:
                        ds.by(dve.tensor_tensor(st[:, 2, x], st[:, 2, x], st[:, 0, x], ALU.mult))
                        ds.settle(dve)
                    done.by(dve.scalar_tensor_tensor(out=st[:, 4, x], in0=mv[:, x, 0], scalar=-1.0, in1=st[:, 3, x],
                                                     op0=ALU.mult, op1=ALU.mult))

                def add_residual(c):
                    x = chunk_slice(c)
                    for t in chunk(c):
                        dve.wait_ge(sg["y1"].sem, t + 1)
                        sg["x1"].by(dve.tensor_tensor(X[:, t], X[:, t], O1[:, t], ALU.add))
                        sg["x1"].settle(dve)
                        stats(t, X[:, t], sg["stats2"])
                    aggregate(sg["stats2"], chunk(c))
                    sg["stats2"].settle(dve)
                    ds.by(dve.tensor_scalar(st[:, 0, x], mv[:, x, 1], LN_EPS, None, ALU.add))
                    ds.settle(dve)
                    sg["uC"].by(dve.scalar_tensor_tensor(out=st[:, 1, x], in0=st[:, 0, x], scalar=LN_EPS, in1=mv[:, x, 1],
                                                         op0=ALU.mult, op1=ALU.add))

                add_attention(0)
                layer_norm_coefficients(0, 1, sg["coefB"], False)
                add_residual(0)
                layer_norm_coefficients(0, 2, sg["coefC"], True)
                add_attention(1)
                layer_norm_coefficients(1, 3, sg["coefB"], False)
                add_residual(1)
                layer_norm_coefficients(1, 4, sg["coefC"], True)
                for t in range(NT):
                    dve.wait_ge(sg["rope"].sem, 4 * (t + 1))
                    ra = RA[:, t % 2]
                    ds.by(dve.tensor_tensor(ra, ra, RB[:, t % 2], ALU.add))
                    ds.settle(dve)
                    if t >= 2:
                        dve.wait_ge(sg["tpq"].sem, 2 * (t - 1))
                    pt = PT[:, t % 2]
                    ds.by(dve.tensor_copy(pt[:, 0], ra))
                    ds.settle(dve)
                    sg["part1"].by(dve.tensor_tensor(Q2[:, t % 2], ra, pt[:, 0], ALU.subtract))
                    sg["part1"].settle(dve)
                    sg["part1"].by(dve.tensor_copy(pt[:, 1], Q2[:, t % 2]))
                    sg["part1"].settle(dve)
                    sg["part2"].by(dve.tensor_tensor(pt[:, 2], Q2[:, t % 2], pt[:, 1], ALU.subtract))
                end_phase(dve, 1)
                piece = 0
                for kind, u, *rest in dve_plan():
                    g, c = UNITS[u]
                    if kind == "piece":
                        h, qt, (bank, _) = rest
                        dve.wait_ge(sg["nm"].sem, piece + 1)
                        n = (qt + 1) * P
                        src = MXB[:, 512 * bank:512 * bank + n]
                        sg["mx"].by(dve.tensor_reduce(NM[:, qt, h:h + 1], src, AX.X, ALU.max, negate=True))
                        piece += 1
                    elif kind == "parts":
                        tiles = chunk_slice(c)
                        sg["mx"].settle(dve)
                        mt, nm, nmr = MT[:, tiles], NM[:, tiles], NMR[:, tiles]
                        ds.by(dve.tensor_copy(mt[:, :, 0], nm))
                        ds.settle(dve)
                        ds.by(dve.tensor_tensor(nmr, nm, mt[:, :, 0], ALU.subtract))
                        ds.settle(dve)
                        ds.by(dve.tensor_copy(mt[:, :, 1], nmr))
                        ds.settle(dve)
                        sg["part0"].by(dve.tensor_tensor(mt[:, :, 2], nmr, mt[:, :, 1], ALU.subtract))
                    elif kind == "rows":
                        bank, _ = rest[0]
                        dve.wait_ge(sg["nm"].sem, piece + 1)
                        if u >= 2:
                            dve.wait_ge(sg["mrow%d" % (u % 2)].sem, 48 * (u // 2))
                        sg["mt"].by(dve.tensor_copy(MR[:, 512 * (u % 2):512 * (u % 2 + 1)],
                                                    MXB[0:3 * G, 512 * bank:512 * (bank + 1)].bitcast(BF16)[:, 0:512]))
                        sg["mt"].settle(dve)
                        dve.sem_inc(sg["mx"].sem, 1)
                        sg["mx"].n += 1
                        piece += 1
                    elif kind == "out":
                        dve.wait_ge(sg["pv"].sem, FIRST_STEP[u + 1])
                        if u >= 1:
                            dve.wait_ge(sg["otp"].sem, u)
                        sg["ot"].by(dve.tensor_copy(OT[:, :], OA[:, :]))
                    else:
                        dve.wait_ge(sg["otp"].sem, u + 1)
                        o = OB[:, :].rearrange("p (q h d) -> p q h d", q=CH, h=G)
                        ds.by(dve.reciprocal(RC[:, :, :], o[:, :, :, HD]))
                        ds.settle(dve)
                        sg["ctx"].by(dve.tensor_tensor(
                            CTX[:, CH * c:CH * (c + 1), g * G * HD:(g + 1) * G * HD].rearrange("p q (h d) -> p q h d", d=HD),
                            o[:, :, :, 0:HD], RC[:, :, :].unsqueeze(3).broadcast_to([P, CH, G, HD]), ALU.mult))
                        sg["ctx"].settle(dve)
                end_phase(dve, 2)
                def add_context(tiles):
                    for t in tiles:
                        dve.wait_ge(sg["wo"].sem, t + 1)
                        ds.by(dve.tensor_tensor(H2[:, t], OAB(t)[:, 0:D], HS[:, t], ALU.add))
                        ds.settle(dve)
                        sg["h2"].by(dve.tensor_scalar(H2[:, t], H2[:, t], 100.0, -100.0, ALU.min, ALU.max))

                def scale_squares(c):
                    dve.wait_ge(sg["ss2"].sem, CH * (c + 1))
                    x = chunk_slice(c)
                    sg["u3"].by(dve.tensor_scalar(st[:, 8, x], st[:, 7, x], 1.0 / D, LN_EPS, ALU.mult, ALU.add))

                def flatten(c):
                    x = chunk_slice(c)
                    dve.wait_ge(sg["rt2"].sem, 5 + c)
                    ds.by(dve.reciprocal(st[:, 8, x], st[:, 8, x]))
                    ds.settle(dve)
                    sg["h2"].settle(dve)
                    for t in chunk(c):
                        sg["fl"].by(dve.scalar_tensor_tensor(out=FL[:, t], in0=H2[:, t], scalar=st[:, 8, t:t + 1],
                                                             in1=ln2row[:, :], op0=ALU.mult, op1=ALU.mult))

                add_context(chunk(0))
                scale_squares(0)
                for t in chunk(1):
                    if t == NT - 1:
                        flatten(0)
                    add_context([t])
                scale_squares(1)
                flatten(1)
                x_coefficients(sg["stats"], sg["u1"], sg["rt2"], 7, sg["coef"])
                dve.wait_ge(sg["lg"].sem, NT)
                ds.by(dve.tensor_copy(LG[:, :, :], MX[:, 0, 0, 0:NT * E].rearrange("p (t e) -> p t e", e=E)))
                ds.settle(dve)
                for t in range(NT):
                    ds.by(dve.max(top[:, t], LG[:, t]))
                ds.settle(dve)
                for t in range(NT):
                    ds.by(dve.max_index(topi[:, t], top[:, t], LG[:, t]))
                sg["lgs"].by(dve.tensor_tensor(tw[:, 0, :], top[:, :, 1], top[:, :, 0], ALU.subtract))
                ds.settle(dve)
                ds.by(dve.tensor_copy(ROUTE[:, :, 0:2], topi[:, :, 0:2]))
                dve.wait_ge(sg["act_step"].sem, 1)
                ds.by(dve.tensor_scalar(tw[:, 2, :], tw[:, 1, :], 1.0, None, ALU.add))
                ds.settle(dve)
                ds.by(dve.reciprocal(tw[:, 3, :], tw[:, 2, :]))
                ds.settle(dve)
                ds.by(dve.tensor_copy(ROUTE[:, :, 2], tw[:, 3, :]))
                sg["topk"].by(dve.tensor_tensor(ROUTE[:, :, 3], tw[:, 1, :], tw[:, 3, :], ALU.mult))
                sg["topk"].settle(dve)
                end_batch(dve, "dve")

        @block.tensor
        def _(pe):
            pe.wait_ge(setup["pool"].sem, 11)
            pe.wait_ge(setup["wload"].sem, 16 * NWLOAD)
            for i in range(5):
                if i >= 2:
                    pe.wait_ge(setup["wT"].sem, 2 * (i - 1))
                for fc in range(FC):
                    for ec in range(FC):
                        m = pe.transpose(SP_[:, i % 2, fc * D + ec * P:fc * D + (ec + 1) * P],
                                         w_raw[:, i, ec, fc * P:(fc + 1) * P], ident[:, :])
                setup["tpw"].by(m)
            pe.wait_ge(setup["done"].sem, 1)

            def transpose_tile(dst, src):
                for c in range(FC):
                    m = pe.transpose(dst[:, c * P:(c + 1) * P], src[:, c * P:(c + 1) * P], ident[:, :])
                return m

            with pe.Fori(0, B) as b:
                def transpose_x(t):
                    pe.wait_ge(sg["xn"].sem, t + 1)
                    if t >= 2:
                        pe.wait_ge(sg["xT"].sem, t - 1)
                    sg["tp"].by(transpose_tile(SP_[:, t % 2], XN[:, t % 2]))

                transpose_x(0)
                for t in range(NT + 1):
                    if t < NT:
                        if t + 1 < NT:
                            transpose_x(t + 1)
                        pe.wait_ge(sg["xT"].sem, t + 1)
                        if t >= 2:
                            pe.wait_ge(sg["qk"].sem, t - 1)
                            pe.wait_ge(sg["vcopy"].sem, t - 1)
                        for c in range(FC):
                            pe.matmul(MX[:, t % 2, 0, :], XT[:, t % 2, c], wqkvT[:, c, 0:2 * D], start=c == 0, stop=c == FC - 1)
                        for c in range(FC):
                            m = pe.matmul(MX[:, t % 2, 1, 0:D], XT[:, t % 2, c], wqkvT[:, c, 2 * D:3 * D], start=c == 0,
                                          stop=c == FC - 1)
                        sg["qkv"].by(m)
                    if t >= 1:
                        u = t - 1
                        if u >= 2:
                            pe.wait_ge(sg["kvs"].sem, 2 * (u - 1))
                        for h in range(H):
                            if h % (H // 2) == 0:
                                pe.wait_ge(sg["prod1"].sem, 2 * u + 1 + h // (H // 2))
                            m = pe.matmul(OAB(u)[:, 0:D], ident[:, :], P1[u % 2][:, h * D:(h + 1) * D], start=h == 0,
                                          stop=h == H - 1)
                        sg["kv"].by(m)
                pe.wait_ge(sg["kvs"].sem, 2 * (NT - 1))
                products = P1[NT % 2][:, 0:LAST_HEADS * D].rearrange("p (h e d) -> p h e d", e=HD, d=HD)
                for e in range(HD):
                    if e % (HD // 2) == 0:
                        pe.wait_ge(sg["last_products"].sem, 1 + e // (HD // 2))
                    m = pe.matmul(OA[:, 0:LAST_HEADS * HD].rearrange("p (h d) -> p h d", d=HD), ident[:, :], products[:, :, e],
                                  start=e == 0, stop=e == HD - 1)
                sg["last_sum"].by(m)
                sg["kv"].settle(pe)
                sg["qkv"].settle(pe)
                for c in range(NT // CH):
                    for t in range(CH * c, CH * (c + 1)):
                        pe.wait_ge(sg["a2"].sem, t + 1)
                        if t >= 2:
                            pe.wait_ge(sg["a2T"].sem, t - 1)
                        sg["tpb"].by(transpose_tile(SP_[:, t % 2], A2[:, t]))
                    pe.wait_ge(sg["a2T"].sem, CH * (c + 1))
                    if c >= 1:
                        pe.wait_ge(sg["hidT"].sem, FC * c)
                    for fo in range(FC):
                        for k in range(FC):
                            m = pe.matmul(MX[:, 0, fo, :], w1T[:, k, fo * P:(fo + 1) * P], A2T[:, k, :], start=k == 0,
                                          stop=k == FC - 1)
                    sg["hid"].by(m)
                    pe.wait_ge(sg["hidT"].sem, FC * (c + 1))
                    for t in range(CH * c, CH * (c + 1)):
                        if t >= 2:
                            pe.wait_ge(sg["o1"].sem, t - 1)
                        else:
                            pe.wait_ge(sg["last_attn"].sem, 1)
                        for k in range(FC):
                            m = pe.matmul(OAB(t)[:, 0:D], HT[:, c, k, (t % CH) * P:(t % CH + 1) * P], w2T[:, k, :],
                                          start=k == 0, stop=k == FC - 1)
                        sg["out1"].by(m)
                sg["out1"].settle(pe)
                pe.wait_ge(sg["hidT"].sem, FC * NT // CH)
                def transpose_h(t):
                    pe.wait_ge(sg["hs"].sem, t + 1)
                    if t >= 2:
                        pe.wait_ge(sg["hT"].sem, t - 1)
                    sg["tph"].by(transpose_tile(SP_[:, t % 2], HS[:, t]))

                transpose_h(0)
                for t in range(NT + 2):
                    if t + 1 < NT:
                        transpose_h(t + 1)
                    if t < NT:
                        pe.wait_ge(sg["hT"].sem, t + 1)
                        if t >= 2:
                            pe.wait_ge(sg["v2"].sem, t - 1)
                        for k in range(FC):
                            m = pe.matmul(MX[:, 0, t % 2, 0:NQKV], XT[:, t % 2, k], wqkv2[:, k, :], start=k == 0, stop=k == FC - 1)
                        sg["qkv2"].by(m)
                    if t >= 2:
                        u = t - 2
                        pe.wait_ge(sg["part2"].sem, u + 1)
                        if u >= 2:
                            pe.wait_ge(sg["qts"].sem, u - 1)
                            pe.wait_ge(sg["kts"].sem, u - 1)
                        for j in range(3):
                            for k in range(FC):
                                m = pe.transpose(MX[:, 1, u % 2, :].bitcast(BF16)[:, (FC * j + k) * P:(FC * j + k + 1) * P],
                                                 PT[:, u % 2, j, k * P:(k + 1) * P], identb[:, :])
                        sg["tpq"].by(m)
                        for j in range(3):
                            m = pe.transpose(OAB(u).bitcast(BF16)[0:KV, j * P:(j + 1) * P], PT[:, u % 2, j, D:D + KV], identb[:, :])
                        sg["tpq"].by(m)
                sg["tpq"].settle(pe)
                end_phase(pe, 1)
                state = {"n": 0, "second half": False}

                def max_piece(u, h, qt, place):
                    g = UNITS[u][0]
                    bank, before = place
                    if before:
                        pe.wait_ge(sg["mx"].sem, before)
                    n = (qt + 1) * P
                    lhsT = QST[0:MROW, g * G + h, qt * P:(qt + 1) * P]
                    for k0 in range(0, n, 512):
                        k1 = min(n, k0 + 512)
                        out = MXB[:, 512 * bank + k0:512 * bank + k1]
                        last = k1 == n
                        m = pe.matmul(out, lhsT, KST[0:MROW, g, k0:k1], start=True, stop=not last)
                        if last:
                            m = pe.matmul(out[:, k1 - k0 - P:k1 - k0], identb[:, :], mask_qk[:, :], start=False, stop=True)
                    sg["nm"].by(m)

                def max_rows(u, place):
                    bank, before = place
                    c = UNITS[u][1]
                    pe.wait_ge(sg["part0"].sem, u + 1)
                    pe.wait_ge(sg["mx"].sem, before)
                    for q in range(CH):
                        m = pe.transpose(MXB[0:3 * G, 512 * bank:512 * (bank + 1)].bitcast(BF16)[:, q * P:(q + 1) * P],
                                         MT[:, CH * c + q].rearrange("p j h -> p (j h)"), identb[:, :])
                    sg["nm"].by(m)

                def maxima(actions):
                    for kind, *args in actions:
                        if kind == "piece":
                            if args[2] >= CH and not state["second half"]:
                                pe.wait_ge(sg["stack1"].sem, 2 * 16 * NSLOT)
                                state["second half"] = True
                            max_piece(*args)
                        elif kind == "rows":
                            max_rows(*args)

                def scores(u, kt, h):
                    g, c = UNITS[u]
                    n = state["n"]
                    q0 = max(0, kt - CH * c) * P
                    diag = kt >= CH * c
                    if n >= 2:
                        pe.wait_ge(sg["exp"].sem, n - 1)
                    m = pe.matmul(SP_[:, n % 2, q0:512], KST[0:KROWS, g, kt * P:(kt + 1) * P],
                                  QST[0:KROWS, g * G + h, c * 512 + q0:(c + 1) * 512], start=True, stop=not diag)
                    if diag:
                        m = pe.matmul(SP_[:, n % 2, q0:q0 + P], identb[:, :], mask_kq[:, :], start=False, stop=True)
                    sg["s"].by(m)
                    state["n"] += 1

                def weighted_values(k, u, kt):
                    g, c = UNITS[u]
                    q0 = max(0, kt - CH * c) * P
                    pe.wait_ge(sg["exp"].sem, G * (k + 1))
                    if kt == 0 and u > 0:
                        pe.wait_ge(sg["ot"].sem, u)
                    last = kt == CH * (c + 1) - 1
                    for h in range(G):
                        m = pe.matmul(OA[32 * h:32 * (h + 1), q0:512], V1[:, kt, g, :], PR[:, (G * k + h) % 8, q0:512],
                                      start=kt == 0, stop=last, tile_position=(0, 32 * h))
                    sg["pv"].by(m)

                def turn_out(i):
                    pe.wait_ge(sg["ot"].sem, i + 1)
                    if i >= 1:
                        pe.wait_ge(sg["ctx"].sem, i)
                    for q in range(CH):
                        m = pe.transpose(OB[:, q * P:(q + 1) * P], OT[:, q * P:(q + 1) * P], ident[:, :])
                    sg["otp"].by(m)

                plan = max_plan()
                pe.wait_ge(sg["stack0"].sem, 2 * 16 * NSLOT)
                maxima(plan[0])
                order = list(steps())
                for k, (u, kt) in enumerate(order):
                    if kt == 0:
                        pe.wait_ge(sg["mrow%d" % (u % 2)].sem, 48 * (u // 2 + 1))
                    actions = plan[k + 1]
                    n = len(actions)
                    for h in range(G):
                        scores(u, kt, h)
                        if h == 1 and k >= 1:
                            weighted_values(k - 1, *order[k - 1])
                        maxima(actions[n * h // G:n * (h + 1) // G])
                    if kt == 1 and u >= 1:
                        turn_out(u - 1)
                weighted_values(len(order) - 1, *order[-1])
                turn_out(len(UNITS) - 1)
                sg["otp"].settle(pe)
                end_phase(pe, 2)
                for t in range(NT + 1):
                    if t < NT:
                        if t >= 2:
                            pe.wait_ge(sg["cT"].sem, t - 1)
                        sg["tpc"].by(transpose_tile(SP_[:, t % 2], CTX[:, t]))
                    if t >= 1:
                        u = t - 1
                        pe.wait_ge(sg["cT"].sem, u + 1)
                        if u >= 2:
                            pe.wait_ge(sg["h2"].sem, u - 1)
                        for k in range(FC):
                            m = pe.matmul(OAB(u)[:, 0:D], XT[:, u % 2, k], wo[:, k, :], start=k == 0, stop=k == FC - 1)
                        sg["wo"].by(m)
                for t in range(NT + 1):
                    if t < NT:
                        pe.wait_ge(sg["fl"].sem, t + 1)
                        if t >= 2:
                            pe.wait_ge(sg["fT"].sem, t - 1)
                        else:
                            pe.wait_ge(sg["cT"].sem, NT)
                        sg["tpf"].by(transpose_tile(SP_[:, t % 2], FL[:, t]))
                    if t >= 1:
                        u = t - 1
                        pe.wait_ge(sg["fT"].sem, u + 1)
                        for k in range(FC):
                            m = pe.matmul(MX[:, 0, 0, u * E:(u + 1) * E], XN[:, u % 2, k * P:(k + 1) * P], wr[:, k, :],
                                          start=k == 0, stop=k == FC - 1)
                        sg["lg"].by(m)
                sg["lg"].settle(pe)
                end_batch(pe, "pe")


def experts_kernel(nc, a, dram, out):
    ctx = ExitStack()
    with ctx:
        def sb(name, shape, dt=F32):
            return ctx.enter_context(nc.sbuf_tensor(name, shape, dt))

        wg = sb("wg", [P, E, FC, F])
        wu = sb("wu", [P, E, FC, F])
        wd = sb("wd", [P, E, FK, D])
        identm = sb("identm", [P, P])
        RT = sb("RT", [P, TT, 4])
        slot = sb("slot", [P, 2, TT], U32)
        source = sb("source", [P, NSLOT_TILES], U32)
        texp = sb("texp", [P, NSLOT_TILES], I32)
        wsem = ctx.enter_context(nc.semaphore("r_wload"))
        route_tokens(nc, dram, RT, slot, source, texp, identm, (wg, wu, wd), a, wsem)
        run_experts(nc, dram, source, texp, identm, (wg, wu, wd), wsem)
        combine(nc, dram, RT, slot, out)


def route_tokens(nc, dram, RT, slot, source, texp, identm, weights, a, wsem):
    ctx = ExitStack()
    with ctx:
        def sb(name, shape, dt=F32):
            return ctx.enter_context(nc.sbuf_tensor(name, shape, dt))

        def ps(name, shape, dt=F32):
            return ctx.enter_context(nc.psum_tensor(name, shape, dt))

        NS = NSLOT_TILES
        below = sb("below", [P, P])
        ones = sb("ones", [P, P])
        io = sb("io", [P, max(NS, P)])
        io128 = sb("io128", [P, TT])
        token_lo = sb("token_lo", [P, 1])
        M = sb("M", [P, 2, TT, E])
        BR = sb("BR", [P, TT, E])
        tot = sb("tot", [P, E, TT])
        cum = sb("cum", [P, E, TT])
        base = sb("base", [P, E, TT])
        fill = sb("fill", [P, 4, E])
        cmp = sb("cmp", [P, NS, E])
        slotf = sb("slotf", [P, 2, TT])
        part = sb("part", [P, 2, 2, TT], U32)
        partf = sb("partf", [P, 2, 2, TT])
        lane1 = sb("lane1", [P, 2, P], BF16)
        tile1 = sb("tile1", [P, 2, 2, NS], BF16)
        src = sb("src", [P, 2, NS])
        pr = ps("pr", [P, 512])
        pt = ps("pt", [P, 512])
        pk = ps("pk", [P, 512])
        sg = Signals(nc, ctx, "loaded const step sums place onehot lists texp", "r_")
        block = ctx.enter_context(nc.Block())

        @block.sync
        def _(sp):
            sg["loaded"].by(sp.dma_start(RT[:, :, :], dram["route"].rearrange("(t p) f -> p t f", p=P)), 16)
            for w, n in zip(weights, ("Wg", "Wu", "Wd")):
                sp.dma_start(w[:, :], a["L0_ffn_" + n].rearrange("e (c p) f -> p e c f", p=P)).then_inc(wsem, 16)

        @block.gpsimd
        def _(pool):
            c = sg["const"]
            c.by(pool.memset(identm[:, :], 0.0))
            c.by(pool.memset(ones[:, :], 1.0))
            c.by(pool.memset(below[:, :], 0.0))
            c.by(pool.iota(io[:, :], [[1, max(NS, P)]], base=0, channel_multiplier=0, allow_small_or_imprecise_dtypes=True))
            c.by(pool.iota(io128[:, :], [[P, TT]], base=0, channel_multiplier=0, allow_small_or_imprecise_dtypes=True))
            c.by(pool.iota(token_lo[:, :], [[0, 1]], base=0, channel_multiplier=1, allow_small_or_imprecise_dtypes=True))
            c.settle(pool)
            c.by(pool.affine_select(out=identm[:, :], in_=identm[:, :], compare_op=ALU.not_equal, fill=1.0, base=0,
                                    pattern=[[-1, P]], channel_multiplier=1))
            c.by(pool.affine_select(out=below[:, :], in_=below[:, :], compare_op=ALU.is_ge, fill=1.0, base=0,
                                    pattern=[[-1, P]], channel_multiplier=1))

        @block.vector
        def _(dve):
            s = sg["step"]

            def do(instruction):
                s.by(instruction)
                s.settle(dve)

            dve.wait_ge(sg["const"].sem, 8)
            dve.wait_ge(sg["loaded"].sem, 16)
            sh = [P, TT, E]
            for j in range(2):
                do(dve.tensor_tensor(M[:, j], io[:, 0:E].unsqueeze(1).broadcast_to(sh),
                                     RT[:, :, j].unsqueeze(2).broadcast_to(sh), ALU.is_equal))
            do(dve.tensor_tensor(BR[:, :, :], M[:, 0], M[:, 1], ALU.add))
            dve.sem_inc(sg["onehot"].sem, 1)
            dve.wait_ge(sg["sums"].sem, 1)
            do(dve.tensor_copy(tot[:, :, :], pt[:, 0:TT * E].rearrange("p (t e) -> p e t", e=E)))
            for e in range(E):
                s.by(dve.tensor_tensor_scan(cum[:, e], ones[:, 0:TT], tot[:, e], 0.0, ALU.mult, ALU.add))
            s.settle(dve)
            do(dve.tensor_tensor(base[:, :, :], cum[:, :, :], tot[:, :, :], ALU.subtract))
            sh = [P, E, TT]
            do(dve.tensor_tensor(tot[:, :, :], cum[:, :, TT - 1:TT].broadcast_to(sh),
                                 io128[:, :].unsqueeze(1).broadcast_to(sh), ALU.is_gt))
            do(dve.tensor_reduce(fill[:, 0], tot[:, :, :], AX.X, ALU.add))
            do(dve.tensor_tensor_scan(fill[:, 1], ones[:, 0:E], fill[:, 0], 0.0, ALU.mult, ALU.add))
            do(dve.tensor_tensor(fill[:, 2], fill[:, 1], fill[:, 0], ALU.subtract))
            do(dve.tensor_scalar(fill[:, 3], fill[:, 2], float(P), None, ALU.mult))
            do(dve.tensor_tensor(base[:, :, :], base[:, :, :], fill[:, 3].unsqueeze(2).broadcast_to(sh), ALU.add))
            do(dve.tensor_tensor(BR[:, :, :], pr[:, 0:TT * E].rearrange("p (t e) -> p t e", e=E),
                                 base[:, :, :].rearrange("p e t -> p t e"), ALU.add))
            for j in range(2):
                do(dve.tensor_tensor(M[:, j], M[:, j], BR[:, :, :], ALU.mult))
                do(dve.tensor_reduce(slotf[:, j], M[:, j], AX.X, ALU.add))
            do(dve.tensor_copy(slot[:, :, :], slotf[:, :, :]))
            do(dve.tensor_scalar(part[:, 0], slot[:, :, :], 7, None, ALU.logical_shift_right))
            do(dve.tensor_scalar(part[:, 1], slot[:, :, :], P - 1, None, ALU.bitwise_and))
            do(dve.tensor_copy(partf[:, :, :, :], part[:, :, :, :]))
            sh = [P, NS, E]
            do(dve.tensor_tensor(cmp[:, :, :], io[:, 0:NS].unsqueeze(2).broadcast_to(sh),
                                 fill[:, 1].unsqueeze(1).broadcast_to(sh), ALU.is_ge))
            do(dve.tensor_reduce(src[:, 0], cmp[:, :, :], AX.X, ALU.add))
            do(dve.tensor_scalar(src[:, 0], src[:, 0], float(E - 1), None, ALU.min))
            do(dve.tensor_copy(texp[:, :], src[:, 0]))

            def one_hots(t, first=False):
                for j in range(2):
                    if not first:
                        dve.wait_ge(sg["lists"].sem, 2 * t + j - 1)
                    col = t if isinstance(t, int) else bass.ds(t, 1)
                    at = slice(t, t + 1) if isinstance(t, int) else col
                    lane = partf[:, 1, j, at]
                    til = partf[:, 0, j, at]
                    dve.tensor_scalar(lane1[:, j], io[:, 0:P], lane, None, ALU.is_equal)
                    dve.tensor_scalar(tile1[:, j, 0], io[:, 0:NS], til, token_lo[:, :], ALU.is_equal, ALU.mult)
                    dve.tensor_scalar(tile1[:, j, 1], io[:, 0:NS], til, io[:, at], ALU.is_equal, ALU.mult)\
                        .then_inc(sg["place"].sem, 1)

            one_hots(0, True)
            with dve.Fori(1, TT - 1) as t:
                one_hots(t)
            one_hots(TT - 1)
            dve.wait_ge(sg["lists"].sem, 2 * TT)
            do(dve.tensor_copy(src[:, :, :], pk[:, 0:2 * NS].rearrange("p (x n) -> p x n", x=2)))
            do(dve.scalar_tensor_tensor(out=src[:, 0], in0=src[:, 1], scalar=float(P), in1=src[:, 0], op0=ALU.mult, op1=ALU.add))
            do(dve.tensor_copy(source[:, :], src[:, 0]))

        @block.tensor
        def _(pe):
            pe.wait_ge(sg["onehot"].sem, 1)
            choices = BR[:, :, :].rearrange("p t e -> p (t e)")
            pe.matmul(pr[:, 0:TT * E], below[:, :], choices, start=True, stop=True)
            sg["sums"].by(pe.matmul(pt[:, 0:TT * E], ones[:, :], choices, start=True, stop=True))

            def lists(t, first=False, last=False):
                for j in range(2):
                    pe.wait_ge(sg["place"].sem, 2 * t + j + 1)
                    pe.matmul(pk[:, 0:2 * NS], lane1[:, j], tile1[:, j].rearrange("p x n -> p (x n)"),
                              start=first and j == 0, stop=last and j == 1).then_inc(sg["lists"].sem, 1)

            lists(0, first=True)
            with pe.Fori(1, TT - 1) as t:
                lists(t)
            lists(TT - 1, last=True)


def run_experts(nc, dram, source, texp, identm, weights, wsem):
    wg, wu, wd = weights
    ctx = ExitStack()
    with ctx:
        def sb(name, shape, dt=F32):
            return ctx.enter_context(nc.sbuf_tensor(name, shape, dt))

        def ps(name, shape, dt=F32):
            return ctx.enter_context(nc.psum_tensor(name, shape, dt))

        index = sb("index", [P, 2, 4], U32)
        XG = sb("XG", [P, 4, D])
        XT = sb("XTm", [P, 2, D])
        SL = sb("SL", [P, 2, F])
        AG = sb("AG", [P, 2, F])
        AGT = sb("AGT", [P, 2, F])
        Y = sb("Y", [P, 2, D])
        GB = ps("GB", [P, 2, F])
        UB = ps("UB", [P, 2, F])
        TX = ps("TX", [P, 2, 512])
        TA = ps("TA", [P, 512])
        DN = ps("DN", [P, 512])
        sg = Signals(nc, ctx, "index gathered0 gathered1 gathered2 gathered3 tx xT g gu silu ag tpa agT down y stored0 stored1 moved", "m_")
        N = NSLOT_TILES
        U = UNROLL
        yd = dram["y"]
        block = ctx.enter_context(nc.Block())

        def rolled(eng, body):
            with eng.Fori(0, N // U - 1) as i:
                body(i * U, i, False)
            body(N - U, N // U - 1, True)

        CREDIT = 2

        @block.sync
        def _(sp):
            def body(n0, i, last):
                for s in range(U):
                    sp.wait_ge(sg["y"].sem, n0 + s + 1 + CREDIT)
                    rows = yd[(n0 + s) * P:(n0 + s + 1) * P, :] if last else yd[bass.ds((n0 + s) * P, P), :]
                    sp.dma_start(rows, Y[:, s % 2]).then_inc(sg[f"stored{s % 2}"].sem, 16)
            for j in range(2):
                sp.sem_inc(sg[f"stored{j}"].sem, 16)
            rolled(sp, body)
            for j in range(2):
                sp.wait_ge(sg[f"stored{j}"].sem, 16 * (N // 2 + 1))

        @block.gpsimd
        def _(pool):
            def gather(s, ind):
                pool.indirect_dma_start(out=XG[:, s % 4], out_offset=None, in_=dram["flat"],
                                        in_offset=bass.IndirectOffsetOnAxis(ap=ind, axis=0))\
                    .then_inc(sg[f"gathered{s % 4}"].sem, 16)

            pool.tensor_copy(index[:, 1, :], source[:, 0:4]).then_inc(sg["index"].sem, 1)
            pool.wait_ge(sg["index"].sem, 1)
            for s in range(4):
                gather(s, index[:, 1, s:s + 1])

            def body(n0, i, last):
                for s in range(4 if last else U):
                    pool.wait_ge(sg["tx"].sem, n0 + s + 1)
                    pool.sem_inc(sg["moved"].sem, 1)
                    if s % 4 == 0:
                        first = n0 + s + 4
                        ind = source[:, first:first + 4] if last else source[:, bass.ds(first, 4)]
                        pool.tensor_copy(index[:, s // 4, 0:4], ind).then_inc(sg["index"].sem, 1)
                        pool.wait_ge(sg["index"].sem, 2 * i + s // 4 + 2)
                        pool.sem_inc(sg["moved"].sem, 1)
                    gather(s, index[:, s // 4, s % 4:s % 4 + 1])
            rolled(pool, body)

        @block.scalar
        def _(act):
            def x_evac(s, n):
                act.wait_ge(sg["tx"].sem, n + 1)
                act.activation(XT[:, s % 2], TX[:, s % 2, 0:D], ACT.Copy).then_inc(sg["xT"].sem, 1)

            def silu(s, n):
                act.wait_ge(sg["g"].sem, n + 1)
                act.wait_ge(sg["ag"].sem, n - 1 + CREDIT)
                act.activation(SL[:, s % 2], GB[:, s % 2], ACT.Silu).then_inc(sg["silu"].sem, 1)

            x_evac(0, 0)
            x_evac(1, 1)
            silu(0, 0)

            def body(n0, i, last):
                for s in range(U):
                    if not (last and s + 1 >= U):
                        silu(s + 1, n0 + s + 1)
                    act.wait_ge(sg["tpa"].sem, n0 + s + 1 + CREDIT)
                    act.activation(AGT[:, s % 2], TA[:, :], ACT.Copy).then_inc(sg["agT"].sem, 1)
                    if not (last and s + 2 >= U):
                        x_evac(s, n0 + s + 2)
            act.sem_inc(sg["agT"].sem, CREDIT)
            rolled(act, body)

        @block.vector
        def _(dve):
            def gate(s, n):
                dve.wait_ge(sg["gu"].sem, n + 1)
                dve.wait_ge(sg["silu"].sem, n + 1)
                dve.wait_ge(sg["tpa"].sem, n - 1 + CREDIT)
                dve.tensor_tensor(AG[:, s % 2], UB[:, s % 2], SL[:, s % 2], ALU.mult).then_inc(sg["ag"].sem, 1)

            dve.sem_inc(sg["ag"].sem, CREDIT)
            dve.sem_inc(sg["y"].sem, CREDIT)
            gate(0, 0)

            def body(n0, i, last):
                for s in range(U):
                    if not (last and s + 1 >= U):
                        gate(s + 1, n0 + s + 1)
                    dve.wait_ge(sg["down"].sem, n0 + s + 1)
                    dve.wait_ge(sg[f"stored{s % 2}"].sem, (i * (U // 2) + s // 2 + 1) * 16)
                    dve.tensor_copy(Y[:, s % 2], DN[:, 0:D]).then_inc(sg["y"].sem, 1)
            rolled(dve, body)

        @block.tensor
        def _(pe):
            def turn_x(s, i):
                pe.wait_ge(sg[f"gathered{s % 4}"].sem, (i * (U // 4) + s // 4 + 1) * 16)
                for c in range(FC):
                    m = pe.transpose(TX[:, s % 2, c * P:(c + 1) * P], XG[:, s % 4, c * P:(c + 1) * P], identm[:, :])
                m.then_inc(sg["tx"].sem, 1)

            def expert(n):
                at = texp[0:1, n:n + 1] if isinstance(n, int) else texp[0:1, bass.ds(n, 1)]
                return pe.value_load(at, min_val=0, max_val=E - 1)

            def project(s, n, e, w, out, done):
                for c in range(FC):
                    m = pe.matmul(out[:, s % 2], XT[:, s % 2, c * P:(c + 1) * P], w[:, bass.ds(e, 1), c, :].squeeze(1),
                                  start=c == 0, stop=c == FC - 1)
                m.then_inc(sg[done].sem, 1)

            pe.wait_ge(wsem, 48)
            pe.sem_inc(sg["tpa"].sem, CREDIT)
            turn_x(0, 0)
            turn_x(1, 0)
            e0 = expert(0)
            pe.wait_ge(sg["xT"].sem, 1)
            project(0, 0, e0, wg, GB, "g")
            project(0, 0, e0, wu, UB, "gu")

            def body(n0, i, last):
                e1 = expert(n0)
                for s in range(U):
                    n = n0 + s
                    more = not (last and s + 1 >= U)
                    e = e1
                    if more:
                        e1 = expert(n + 1)
                        pe.wait_ge(sg["xT"].sem, n + 2)
                        pe.wait_ge(sg["ag"].sem, n + CREDIT)
                        project(s + 1, n + 1, e1, wg, GB, "g")
                    pe.wait_ge(sg["ag"].sem, n + 1 + CREDIT)
                    pe.wait_ge(sg["agT"].sem, n + CREDIT)
                    for c in range(FK):
                        m = pe.transpose(TA[:, c * P:(c + 1) * P], AG[:, s % 2, c * P:(c + 1) * P], identm[:, :])
                    m.then_inc(sg["tpa"].sem, 1)
                    if not (last and s + 2 >= U):
                        turn_x(s + 2, i)
                    if more:
                        project(s + 1, n + 1, e1, wu, UB, "gu")
                    pe.wait_ge(sg["agT"].sem, n + 1 + CREDIT)
                    pe.wait_ge(sg["y"].sem, n + CREDIT)
                    for c in range(FK):
                        m = pe.matmul(DN[:, 0:D], AGT[:, s % 2, c * P:(c + 1) * P], wd[:, bass.ds(e, 1), c, :].squeeze(1),
                                      start=c == 0, stop=c == FK - 1)
                    m.then_inc(sg["down"].sem, 1)
            rolled(pe, body)


def combine(nc, dram, RT, slot, out):
    ctx = ExitStack()
    with ctx:
        def sb(name, shape, dt=F32):
            return ctx.enter_context(nc.sbuf_tensor(name, shape, dt))

        U = 4
        NB = TT // U
        index = sb("indexc", [P, 2, 2, U], U32)
        share = sb("share", [P, 2, 2, U])
        Y2 = sb("Y2", [P, 2, 2, U, D])
        XH = sb("XH", [P, 2, 2, U, D])
        st = sb("stc", [P, U, 6])
        mv = sb("mvc", [P, U, 2])
        cf = sb("cfc", [P, 4, U])
        eps = sb("epsc", [P, 1])
        sg = Signals(nc, ctx, "index loaded0 loaded1 gathered0 gathered1 share sum clip stat var std coef norm out stored0 stored1 moved eps", "c_")
        rows = {n: dram[n].rearrange("(i t p) f -> i p t f", t=U, p=P) for n in ("x1", "h2")}
        od = out.rearrange("b (i t p) f -> (b i) p t f", t=U, p=P)
        block = ctx.enter_context(nc.Block())
        NP = NB // 2

        @block.sync
        def _(sp):
            def load(i, k, first=False):
                if not first:
                    sp.wait_ge(sg[f"stored{k}"].sem, i * 16)
                for x, n in enumerate(("x1", "h2")):
                    src = rows[n][2 * i + k] if isinstance(i, int) else rows[n][bass.ds(2 * i + k, 1)].squeeze(0)
                    sp.dma_start(XH[:, k, x], src).then_inc(sg[f"loaded{k}"].sem, 16)

            def store(i, k):
                sp.wait_ge(sg["out"].sem, (2 * i + k + 1) * U)
                dst = od[2 * i + k] if isinstance(i, int) else od[bass.ds(2 * i + k, 1)].squeeze(0)
                sp.dma_start(dst, XH[:, k, 0]).then_inc(sg[f"stored{k}"].sem, 16)

            load(0, 0, True)
            load(0, 1, True)
            with sp.Fori(0, NP - 1) as i:
                for k in range(2):
                    store(i, k)
                    load(i + 1, k)
            for k in range(2):
                store(NP - 1, k)
            for k in range(2):
                sp.wait_ge(sg[f"stored{k}"].sem, 16 * NP)

        @block.gpsimd
        def _(pool):
            def gather(i, k, first=False):
                b0 = (2 * i + k) * U
                if not first:
                    pool.wait_ge(sg["out"].sem, (2 * i + k - 1) * U)
                    pool.sem_inc(sg["moved"].sem, 1)
                for j in range(2):
                    src = slot[:, j, b0:b0 + U] if first else slot[:, j, bass.ds(b0, U)]
                    pool.tensor_copy(index[:, k, j, :], src).then_inc(sg["index"].sem, 1)
                pool.wait_ge(sg["index"].sem, 2 * (2 * i + k) + 2)
                pool.sem_inc(sg["moved"].sem, 1)
                for u in range(U):
                    for j in range(2):
                        pool.indirect_dma_start(out=Y2[:, k, j, u], out_offset=None, in_=dram["y"],
                                                in_offset=bass.IndirectOffsetOnAxis(ap=index[:, k, j, u:u + 1], axis=0))\
                            .then_inc(sg[f"gathered{k}"].sem, 16)
            gather(0, 0, True)
            gather(0, 1, True)
            with pool.Fori(1, NP) as i:
                for k in range(2):
                    gather(i, k)

        @block.scalar
        def _(act):
            act.wait_ge(sg["eps"].sem, 1)
            with act.Fori(0, NP) as i:
                for k in range(2):
                    n = 2 * i + k
                    act.wait_ge(sg["var"].sem, (n + 1) * U)
                    act.activation(cf[:, 0], mv[:, :, 1], ACT.Sqrt, bias=eps[:, :]).then_inc(sg["std"].sem, 1)
                    act.wait_ge(sg["coef"].sem, 2 * n + 2)
                    for u in range(U):
                        act.activation(XH[:, k, 1, u], XH[:, k, 1, u], ACT.Identity, bias=cf[:, 2, u:u + 1],
                                       scale=cf[:, 1, u:u + 1]).then_inc(sg["norm"].sem, 1)

        @block.vector
        def _(dve):
            dve.memset(eps[:, :], LN_EPS).then_inc(sg["eps"].sem, 1)
            with dve.Fori(0, NP) as i:
                for k in range(2):
                    n = 2 * i + k
                    h = XH[:, k, 1]
                    for j in range(2):
                        dve.tensor_copy(share[:, k, j, :], RT[:, bass.ds(n * U, U), 2 + j]).then_inc(sg["share"].sem, 1)
                    dve.wait_ge(sg["share"].sem, 2 * n + 2)
                    dve.wait_ge(sg[f"loaded{k}"].sem, (i + 1) * 32)
                    dve.wait_ge(sg[f"gathered{k}"].sem, (i + 1) * 32 * U)
                    for j in range(2):
                        for u in range(U):
                            if j:
                                dve.wait_ge(sg["sum"].sem, n * 2 * U + u + 1)
                            dve.scalar_tensor_tensor(out=h[:, u], in0=Y2[:, k, j, u], scalar=share[:, k, j, u:u + 1],
                                                     in1=h[:, u], op0=ALU.mult, op1=ALU.add).then_inc(sg["sum"].sem, 1)
                    dve.wait_ge(sg["sum"].sem, (n + 1) * 2 * U)
                    dve.tensor_scalar(h, h, 100.0, -100.0, ALU.min, ALU.max).then_inc(sg["clip"].sem, 1)
                    dve.wait_ge(sg["clip"].sem, n + 1)
                    for u in range(U):
                        dve.bn_stats(st[:, u], h[:, u]).then_inc(sg["stat"].sem, 1)
                    dve.wait_ge(sg["stat"].sem, (n + 1) * U)
                    dve.sem_inc(sg["moved"].sem, 1)
                    for u in range(U):
                        dve.bn_aggr(mv[:, u], st[:, u]).then_inc(sg["var"].sem, 1)
                    dve.wait_ge(sg["std"].sem, n + 1)
                    dve.reciprocal(cf[:, 1], cf[:, 0]).then_inc(sg["coef"].sem, 1)
                    dve.wait_ge(sg["coef"].sem, 2 * n + 1)
                    dve.scalar_tensor_tensor(out=cf[:, 2], in0=mv[:, :, 0], scalar=-1.0, in1=cf[:, 1], op0=ALU.mult,
                                             op1=ALU.mult).then_inc(sg["coef"].sem, 1)
                    for u in range(U):
                        dve.wait_ge(sg["norm"].sem, n * U + u + 1)
                        dve.tensor_tensor(XH[:, k, 0, u], XH[:, k, 0, u], h[:, u], ALU.add).then_inc(sg["out"].sem, 1)


_INS = ["L0_attn_x", "L0_attn_Wq", "L0_attn_Wk", "L0_attn_Wv", "L0_attn_lambda_params", "L0_attn_g1", "L0_attn_g2",
        "L0_attn_g3", "L0_attn_W1", "L0_attn_W2", "L0_ffn_ln1_w", "L0_ffn_ln2_w", "L0_ffn_Wq", "L0_ffn_Wk", "L0_ffn_Wv",
        "L0_ffn_Wo", "L0_ffn_Wr", "L0_ffn_Wg", "L0_ffn_Wu", "L0_ffn_Wd"]


def rope_table():
    inv = (1.0 / np.float32(THETA) ** (np.arange(0, HD, 2, dtype=np.float32) / np.float32(HD))).astype(np.float32)
    ang = (np.arange(S, dtype=np.float32)[:, None] * inv).astype(np.float32)
    c, s = np.cos(ang).astype(np.float32), np.sin(ang).astype(np.float32)
    return np.concatenate([c, c, -s, s], axis=1)


def build(nc, a, out):
    dram = {}
    for name, shape, dt in (("x1", [B * S, D], F32), ("h2", [B * S, D], F32), ("flat", [B * S, D], F32),
                            ("route", [B * S, 4], F32), ("y", [NSLOT_TILES * P, D], F32), ("qd", [3, D, S], BF16), ("kd", [3, KV, S], BF16)):
        dram[name] = nc.dram_tensor("scratch_" + name, shape, dt, kind="Internal").ap()
    attention_kernel(nc, a, dram)
    experts_kernel(nc, a, dram, out)


def kernel(**inputs):
    import concourse.bacc as bacc
    from concourse.bass_utils import run_bass_kernel_spmd

    nc = bacc.Bacc("TRN2", target_bir_lowering=False, num_devices=1)
    arrays = {"in_" + n: np.ascontiguousarray(inputs[n]) for n in _INS}
    arrays["in_rope"] = rope_table()
    a = {n[3:]: nc.dram_tensor(n, v.shape, mybir.dt.from_np(v.dtype), kind="ExternalInput").ap() for n, v in arrays.items()}
    out = nc.dram_tensor("out", (B, S, D), F32, kind="ExternalOutput").ap()
    build(nc, a, out)
    r = run_bass_kernel_spmd(nc, [arrays], core_ids=[0])
    return r.results[0]["out"]
```
